# Optimizing a Trainium2 kernel written in Bass

```python
import numpy as np
import jax
import jax.numpy as jnp

def _softmax(x, axis=-1):
    return jax.nn.softmax(x, axis=axis)

def _gelu(x):
    return jax.nn.gelu(x, approximate=True)

def _silu(x):
    return jax.nn.silu(x)

def _sigmoid(x):
    return jax.nn.sigmoid(x)

def _layernorm(x, axis=-1, eps=1e-05):
    m = jnp.mean(x, axis=axis, keepdims=True)
    v = jnp.var(x, axis=axis, keepdims=True)
    return (x - m) / jnp.sqrt(v + eps)

def _scatter_add(tgt, idx, src, axis=0):
    return tgt.at[idx].add(src)

def _segment_sum(src, seg, n):
    return jax.ops.segment_sum(src, seg, n)
kernel_name = 'mk_prb_d1_jaxref_r2_f980ef'

def setup_inputs(seed: int=0):
    np.random.seed(seed)
    _w = jnp.asarray

    def _L0_attn_setup():
        import jax, jax.numpy as jnp
        import numpy as np
        from jax import lax
        DIM = 512
        INNER = 1024
        STATE = 64
        B, T = (4, 1024)
        DECAY = 0.95
        INPUT_FACTOR = 0.05
        LN_EPS = 1e-05

        def _layernorm(x, g, b):
            mu = jnp.mean(x, axis=-1, keepdims=True)
            var = jnp.mean(jnp.square(x - mu), axis=-1, keepdims=True)
            return (x - mu) * lax.rsqrt(var + LN_EPS) * g + b
        key = jax.random.key(seed)
        ks = jax.random.split(key, 8)
        s = 0.02
        return {'x': jax.random.normal(ks[0], (B, T, DIM), jnp.float32), 'W_in': jax.random.normal(ks[1], (2 * INNER, DIM), jnp.float32) * s, 'conv_w': jax.random.normal(ks[2], (INNER, 1, 4), jnp.float32) * s, 'conv_b': jax.random.normal(ks[3], (INNER,), jnp.float32) * s, 'W_B': jax.random.normal(ks[4], (STATE, INNER), jnp.float32) * s, 'W_C': jax.random.normal(ks[5], (INNER, STATE), jnp.float32) * s, 'D_param': jax.random.normal(ks[6], (INNER,), jnp.float32) * s, 'W_out': jax.random.normal(ks[7], (DIM, INNER), jnp.float32) * s, 'ln_gamma': jnp.ones((DIM,), jnp.float32), 'ln_beta': jnp.zeros((DIM,), jnp.float32)}
    _L0_attn_in = _L0_attn_setup()

    def _L0_ffn_setup():
        import jax, jax.numpy as jnp
        import numpy as np
        EMBED_DIM = 512
        MLP_RATIO = 4
        NUM_EXPERTS = 8
        CAPACITY = 1.0
        LN_EPS = 1e-05

        def _layernorm(y, gamma, beta):
            mu = jnp.mean(y, axis=-1, keepdims=True)
            var = jnp.mean(jnp.square(y - mu), axis=-1, keepdims=True)
            return (y - mu) * jax.lax.rsqrt(var + LN_EPS) * gamma + beta
        key = jax.random.key(seed)
        k0, k1, k2, k3, k4, k5 = jax.random.split(key, 6)
        d = EMBED_DIM
        dd = EMBED_DIM * MLP_RATIO
        n = NUM_EXPERTS
        x = jax.random.normal(k0, (4, 1024, d), dtype=jnp.float32)
        gate_w = jax.random.normal(k1, (n, d), dtype=jnp.float32) * 0.02
        ln_gamma = jnp.ones((d,), dtype=jnp.float32)
        ln_beta = jnp.zeros((d,), dtype=jnp.float32)
        fc1s = jax.random.normal(k2, (n, dd, d), dtype=jnp.float32) * (1.0 / np.sqrt(d))
        b1s = jax.random.normal(k3, (n, dd), dtype=jnp.float32) * 0.02
        fc2s = jax.random.normal(k4, (n, d, dd), dtype=jnp.float32) * (1.0 / np.sqrt(dd))
        b2s = jax.random.normal(k5, (n, d), dtype=jnp.float32) * 0.02
        return {'x': x, 'gate_w': gate_w, 'ln_gamma': ln_gamma, 'ln_beta': ln_beta, 'fc1s': fc1s, 'b1s': b1s, 'fc2s': fc2s, 'b2s': b2s}
    _L0_ffn_in = _L0_ffn_setup()
    _d = {'L0_attn_x': _L0_attn_in['x'], 'L0_attn_W_in': _L0_attn_in['W_in'], 'L0_attn_conv_w': _L0_attn_in['conv_w'], 'L0_attn_conv_b': _L0_attn_in['conv_b'], 'L0_attn_W_B': _L0_attn_in['W_B'], 'L0_attn_W_C': _L0_attn_in['W_C'], 'L0_attn_D_param': _L0_attn_in['D_param'], 'L0_attn_W_out': _L0_attn_in['W_out'], 'L0_attn_ln_gamma': _L0_attn_in['ln_gamma'], 'L0_attn_ln_beta': _L0_attn_in['ln_beta'], 'L0_ffn_gate_w': _L0_ffn_in['gate_w'], 'L0_ffn_ln_gamma': _L0_ffn_in['ln_gamma'], 'L0_ffn_ln_beta': _L0_ffn_in['ln_beta'], 'L0_ffn_fc1s': _L0_ffn_in['fc1s'], 'L0_ffn_b1s': _L0_ffn_in['b1s'], 'L0_ffn_fc2s': _L0_ffn_in['fc2s'], 'L0_ffn_b2s': _L0_ffn_in['b2s']}
    _x0 = _d['L0_attn_x']
    _d['L0_attn_x'] = jax.random.normal(jax.random.fold_in(jax.random.key(seed), 1), (4, 2048, 512), dtype=_x0.dtype)
    del _x0
    return _d

def reference(L0_attn_x, L0_attn_W_in, L0_attn_conv_w, L0_attn_conv_b, L0_attn_W_B, L0_attn_W_C, L0_attn_D_param, L0_attn_W_out, L0_attn_ln_gamma, L0_attn_ln_beta, L0_ffn_gate_w, L0_ffn_ln_gamma, L0_ffn_ln_beta, L0_ffn_fc1s, L0_ffn_b1s, L0_ffn_fc2s, L0_ffn_b2s):

    def _L0_attn_ref(x, W_in, conv_w, conv_b, W_B, W_C, D_param, W_out, ln_gamma, ln_beta):
        import jax, jax.numpy as jnp
        import numpy as np
        from jax import lax
        DIM = 512
        INNER = 1024
        STATE = 64
        B, T = (4, 1024)
        DECAY = 0.95
        INPUT_FACTOR = 0.05
        LN_EPS = 1e-05

        def _layernorm(x, g, b):
            mu = jnp.mean(x, axis=-1, keepdims=True)
            var = jnp.mean(jnp.square(x - mu), axis=-1, keepdims=True)
            return (x - mu) * lax.rsqrt(var + LN_EPS) * g + b
        Bn, Tn, Dn = x.shape
        x_proj = jnp.einsum('btd,ed->bte', x, W_in)
        x_input, x_gate = jnp.split(x_proj, 2, axis=-1)
        xc = lax.conv_general_dilated(x_input.transpose(0, 2, 1), conv_w, window_strides=(1,), padding=[(3, 0)], feature_group_count=INNER) + conv_b[None, :, None]
        u = jax.nn.silu(xc).transpose(0, 2, 1)
        Bu = jnp.einsum('btc,sc->bts', u, W_B)

        def step(h, bu_t):
            h = DECAY * h + INPUT_FACTOR * bu_t
            return (h, h)
        h0 = jnp.zeros((Bn, STATE), x.dtype)
        _, hs = lax.scan(step, h0, Bu.transpose(1, 0, 2))
        hs = hs.transpose(1, 0, 2)
        y = jnp.einsum('bts,cs->btc', hs, W_C) + D_param * u
        y = y * jax.nn.silu(x_gate)
        y = jnp.einsum('btc,dc->btd', y, W_out)
        return _layernorm(y + x, ln_gamma, ln_beta)

    def _L0_ffn_ref(x, gate_w, ln_gamma, ln_beta, fc1s, b1s, fc2s, b2s):
        import jax, jax.numpy as jnp
        import numpy as np
        EMBED_DIM = 512
        MLP_RATIO = 4
        NUM_EXPERTS = 8
        CAPACITY = 1.0
        LN_EPS = 1e-05

        def _layernorm(y, gamma, beta):
            mu = jnp.mean(y, axis=-1, keepdims=True)
            var = jnp.mean(jnp.square(y - mu), axis=-1, keepdims=True)
            return (y - mu) * jax.lax.rsqrt(var + LN_EPS) * gamma + beta
        og_shape = x.shape
        d = og_shape[-1]
        xf = x.reshape(-1, d)
        bs = xf.shape[0]
        n = gate_w.shape[0]
        k = int(bs * CAPACITY) // n
        scores = xf @ gate_w.T
        scores = (jnp.tanh(scores) + 1.0) * 0.5
        vals, idx = jax.lax.top_k(scores.T, k)
        kept_w = vals.T
        flat_idx = idx.T.reshape(-1)
        y = xf[flat_idx].reshape(k, n, d)
        y = _layernorm(y, ln_gamma, ln_beta)
        h = jnp.einsum('knd,nfd->knf', y, fc1s) + b1s
        h = jax.nn.gelu(h, approximate=True)
        o = jnp.einsum('knf,ndf->knd', h, fc2s) + b2s
        o = o * kept_w[:, :, None]
        out = xf.at[flat_idx].add(o.reshape(k * n, d))
        return out.reshape(og_shape)
    x = L0_attn_x
    xn = _layernorm(x, axis=-1)
    x = x + _L0_attn_ref(xn, L0_attn_W_in, L0_attn_conv_w, L0_attn_conv_b, L0_attn_W_B, L0_attn_W_C, L0_attn_D_param, L0_attn_W_out, L0_attn_ln_gamma, L0_attn_ln_beta) + _L0_ffn_ref(xn, L0_ffn_gate_w, L0_ffn_ln_gamma, L0_ffn_ln_beta, L0_ffn_fc1s, L0_ffn_b1s, L0_ffn_fc2s, L0_ffn_b2s)
    return x

_drawn_inputs = setup_inputs


def setup_inputs(seed=0):
    import zlib

    import numpy as np

    out = dict(_drawn_inputs(seed))
    spreads = {'L0_attn_ln_gamma': (1.0, 0.2),
     'L0_attn_ln_beta': (0.0, 0.1),
     'L0_ffn_ln_gamma': (1.0, 0.2),
     'L0_ffn_ln_beta': (0.0, 0.44)}
    factors = {'L0_attn_W_in': 8.0,
     'L0_attn_conv_w': 8.0,
     'L0_attn_conv_b': 8.0,
     'L0_attn_W_B': 8.0,
     'L0_attn_W_C': 8.0,
     'L0_attn_D_param': 8.0,
     'L0_attn_W_out': 8.0,
     'L0_ffn_b1s': 8.0,
     'L0_ffn_b2s': 8.0}
    for name, (base, spread) in spreads.items():
        noise = np.random.default_rng([zlib.crc32(name.encode()), seed]).standard_normal(out[name].shape)
        drawn = base * np.exp(spread * noise) if base else spread * noise
        out[name] = jnp.asarray(drawn.astype(out[name].dtype))
    for name, factor in factors.items():
        out[name] = (out[name] * factor).astype(out[name].dtype)
    return out
```

```python
from contextlib import ExitStack

import concourse.bass as bass
from concourse import mybir
from concourse.alu_op_type import AluOpType as ALU

F32 = mybir.dt.float32
F32R = mybir.dt.float32r
BF16 = mybir.dt.bfloat16
U32 = mybir.dt.uint32
ACT = mybir.ActivationFunctionType
AX = mybir.AxisListType
RADD = bass.bass_isa.ReduceOp.add

P = 128
N, D, C, S, E, F = 8192, 512, 1024, 64, 8, 2048
SEQ = 2048
TB = 512
NB = N // TB
BPS = SEQ // TB
J = TB // P
NT = N // P
KD = D // P
NC_ = C // P
NW = 2 * NC_
FT = F // P
CAP = N // E
CH = CAP // P
XW = D + E
EPS = 1e-5
DECAY, INPUT_FACTOR = 0.95, 0.05
LO = 32
HI = CAP // LO


class Count:

    def __init__(self, sem):
        self.sem = sem

    def start(self, eng):
        eng.sem_inc(self.sem, 1)

    def wait(self, eng, pieces):
        eng.wait_ge(self.sem, pieces + 1)


class PoolCount(Count):

    def start(self, eng):
        pass

    def prime(self, pool, dst, src):
        pool.dma_start(dst, src).then_inc(self.sem, 16)

    def wait(self, eng, pieces):
        eng.wait_ge(self.sem, pieces + 16)


class Mem:

    def __init__(self, nc, stack):
        self.nc, self.stack, self.counts = nc, stack, []
        self.ticks = {}

    def sb(self, name, shape, dt=F32):
        return self.stack.enter_context(self.nc.sbuf_tensor(name, shape, dt))

    def ps(self, name, shape, dt=F32):
        return self.stack.enter_context(self.nc.psum_tensor(name, shape, dt))

    def count(self, name):
        c = Count(self.stack.enter_context(self.nc.semaphore(name)))
        self.counts.append(c)
        return c

    def pool_count(self, name):
        return PoolCount(self.stack.enter_context(self.nc.semaphore(name)))

    def start(self):
        with self.nc.Block() as block:
            @block.sync
            def _(sp):
                for c in self.counts:
                    c.start(sp)

    def tick(self, name):
        return self.stack.enter_context(self.nc.semaphore(name))


def f(ap):
    return ap.bitcast(F32)


class MixerWeights:

    def __init__(self, m):
        self.w_in = m.sb("w_in", [P, NW, KD * P])
        self.wout_h = m.sb("wout_h", [P, NC_, D], F32R)
        self.wout_l = m.sb("wout_l", [P, NC_, D], F32R)
        self.wb = m.sb("wb", [P, NC_, 2 * S], F32R)
        self.wc_h = m.sb("wc_h", [P, C], F32R)
        self.wc_l = m.sb("wc_l", [P, C], F32R)
        self.cw = m.sb("cw", [P, NC_, 4])
        self.cb = m.sb("cb", [P, NC_])
        self.dp = m.sb("dp", [P, NC_])
        self.gamma = m.sb("ln_g", [P, D])
        self.beta = m.sb("ln_b", [P, D])


def stage_gate(nc, t, gates, ident, w):
    with ExitStack() as stack:
        m = Mem(nc, stack)
        xt = [m.sb(f"g_x{i}", [P, J, D]) for i in range(2)]
        ext = [m.sb(f"g_ext{i}", [P, J, XW]) for i in range(2)]
        stats = m.sb("g_stats", [P, J, 6])
        mv = [m.sb(f"g_mv{i}", [P, J, 2]) for i in range(2)]
        std = m.sb("g_std", [P, J])
        rstd = [m.sb(f"g_rstd{i}", [P, J]) for i in range(2)]
        half = m.sb("g_half", [P, J])
        xnt = [m.sb(f"g_xnt{i}", [P, TB]) for i in range(2)]
        sc_t = m.sb("g_sc_t", [E, TB])
        staged = m.sb("g_staged", [P, NC_, TB])
        staged2 = m.sb("g_staged2", [P, 4, TB])
        tanh = m.sb("g_tanh", [P, J * E])
        gw = m.sb("g_gw", [P, KD, E])
        pt = [m.ps(f"g_pt{i}", [P, TB]) for i in range(2)]
        pst = m.ps("g_pst", [E, TB])
        psc = m.ps("g_psc", [P, J * E])

        c_id = m.count("g_id")
        c_gw = m.count("g_gw_in")
        c_x = [m.count(f"g_x_in{i}") for i in range(2)]
        c_st = [m.count(f"g_out{i}") for i in range(2)]
        c_bn = m.count("g_bn")
        c_mv = m.count("g_mv_set")
        c_eps = m.count("g_eps")
        c_rs = m.count("g_rs")
        c_xn = m.count("g_xn")
        c_t = m.count("g_t")
        c_tc = m.count("g_tc")
        c_st_ = m.count("g_sct")
        c_sr = m.count("g_sr")
        c_sc = m.count("g_sc")
        c_win = m.count("g_win")
        c_in = m.count("g_infac")
        c_sh = m.count("g_sh")
        c_sl = m.count("g_sl")
        c_th = m.count("g_th")
        c_v = m.count("g_v")
        d_tick = m.tick("g_dtick")
        p_tick = m.tick("g_ptick")
        t_tick = m.tick("g_ttick")

        x_v = t["x"].rearrange("(b j p) d -> b p j d", p=P, j=J)
        xn_v = t["xn"].rearrange("(b j p) d -> b p j d", p=P, j=J)

        m.start()
        with nc.Block() as block:
            @block.sync
            def _(sp):
                sp.dma_start(gw[:, :, :], t["gate_w"]).then_inc(c_gw.sem, 16)
                for i in range(2):
                    sp.dma_start(xt[i][:, :, :], x_v[i]).then_inc(c_x[i].sem, 16)
                sp.dma_start(staged[:, :, :], t["w_out"]).then_inc(c_win.sem, 16)
                sp.dma_start(staged2[0:S, 0:2, :], t["w_c"]).then_inc(c_win.sem, 16)
                sp.dma_start(staged2[S:P, 0:2, :], t["w_c"]).then_inc(c_win.sem, 16)
                sp.dma_start(staged2[:, 2, :], t["w_b"]).then_inc(c_win.sem, 16)
                with sp.Fori(0, NB // 2 - 1) as h:
                    for i in range(2):
                        c_xn.wait(sp, (h * 2 + i + 1) * J)
                        sp.dma_start(xt[i][:, :, :], x_v[h * 2 + i + 2]).then_inc(c_x[i].sem, 16)

                sp.dma_start(w.w_in[:, :, :], t["w_in"]).then_inc(c_win.sem, 16)
                sp.dma_start(w.cw[:, :, :], t["conv_w"]).then_inc(c_win.sem, 16)
                sp.dma_start(w.cb[:, :], t["conv_b"]).then_inc(c_win.sem, 16)
                sp.dma_start(w.dp[:, :], t["d_param"]).then_inc(c_win.sem, 16)
                sp.dma_start(w.gamma[:, :], t["ln_g"].to_broadcast([P, D])).then_inc(c_win.sem, 16)
                sp.dma_start(w.beta[:, :], t["ln_b"].to_broadcast([P, D])).then_inc(c_win.sem, 16)
                c_win.wait(sp, 16 * 10)

            @block.gpsimd
            def _(pool):
                c_id.wait(pool, 0)
                pool.memset(ident[:, :], 0.0).then_inc(c_id.sem, 1)
                pool.memset(half[:, :], -0.5).then_inc(c_id.sem, 1)
                c_id.wait(pool, 2)
                pool.affine_select(out=ident[:, :], in_=ident[:, :], compare_op=ALU.not_equal, fill=1.0,
                                   base=0, pattern=[[-1, P]], channel_multiplier=1).then_inc(c_id.sem, 1)
                with pool.Fori(0, NB // 2) as h:
                    for i in range(2):
                        b = h * 2 + i
                        c_mv.wait(pool, (b + 1) * J)
                        c_rs.wait(pool, b)
                        pool.sem_inc(p_tick, 1)
                        pool.tensor_scalar(std[:, :], mv[i][:, :, 1], EPS, None, ALU.add).then_inc(c_eps.sem, 1)
                        c_eps.wait(pool, b + 1)
                        pool.tensor_tensor(rstd[i][:, :], std[:, :], half[:, :], ALU.pow).then_inc(c_rs.sem, 1)

            @block.vector
            def _(dve):
                def statistics(b, h, i):
                    c_x[i].wait(dve, h * 16 + 16)
                    c_mv.wait(dve, b * J)
                    for j in range(J):
                        dve.bn_stats(stats[:, j, :], xt[i][:, j, :]).then_inc(c_bn.sem, 1)
                    c_bn.wait(dve, (b + 1) * J)
                    c_rs.wait(dve, b)
                    c_xn.wait(dve, b * J)
                    dve.sem_inc(d_tick, 1)
                    for j in range(J):
                        dve.bn_aggr(mv[i][:, j, :], stats[:, j, :]).then_inc(c_mv.sem, 1)

                def normalise(b, h, i):
                    c_rs.wait(dve, b + 1)
                    c_mv.wait(dve, (b + 1) * J)
                    c_st[i].wait(dve, h * 16)
                    for j in range(J):
                        dve.tensor_scalar(ext[i][:, j, 0:D], xt[i][:, j, :], mv[i][:, j, 0:1],
                                          rstd[i][:, j:j + 1], ALU.subtract, ALU.mult).then_inc(c_xn.sem, 1)

                def gate_values(b, i):
                    c_th.wait(dve, b + 1)
                    half_tanh = tanh[:, :].rearrange("p (j e) -> p j e", e=E)
                    dve.tensor_scalar(ext[i][:, :, D:XW], half_tanh, 1.0, 0.5,
                                      ALU.add, ALU.mult).then_inc(c_v.sem, 1)
                    dve.tensor_scalar(gates[:, :, bass.ds(b * J, J)], tanh[:, :].rearrange("p (j e) -> p e j", e=E),
                                      1.0, 0.5, ALU.add, ALU.mult).then_inc(c_v.sem, 1)

                def low_parts():
                    c_win.wait(dve, 64)
                    dve.tensor_scalar(staged2[:, 3, :], staged2[:, 2, :], INPUT_FACTOR, None,
                                      ALU.mult).then_inc(c_in.sem, 1)
                    c_sh.wait(dve, 1)
                    dve.tensor_tensor(w.wout_l[:, :, :], staged[:, :, :], f(w.wout_h[:, :, :]),
                                      ALU.subtract).then_inc(c_sl.sem, 1)
                    c_sh.wait(dve, 2)
                    dve.tensor_tensor(w.wc_l[:, :], staged2[:, 0:2, :].rearrange("p a b -> p (a b)"),
                                      f(w.wc_h[:, :]), ALU.subtract).then_inc(c_sl.sem, 1)
                    c_sh.wait(dve, 3)
                    dve.tensor_tensor(w.wb[:, :, S:2 * S], staged2[:, 3, :].rearrange("p (c s) -> p c s", s=S),
                                      f(w.wb[:, :, 0:S]), ALU.subtract).then_inc(c_sl.sem, 1)

                def turns(first, end):
                    with dve.Fori(first, end) as h:
                        normalise(h * 2, h, 0)
                        statistics(h * 2 + 1, h, 1)
                        gate_values(h * 2, 0)
                        normalise(h * 2 + 1, h, 1)
                        statistics(h * 2 + 2, h + 1, 0)
                        gate_values(h * 2 + 1, 1)

                statistics(0, 0, 0)
                turns(0, NB // 4)
                low_parts()
                turns(NB // 4, NB // 2 - 1)
                last = NB // 2 - 1
                normalise(NB - 2, last, 0)
                statistics(NB - 1, last, 1)
                gate_values(NB - 2, 0)
                normalise(NB - 1, last, 1)
                gate_values(NB - 1, 1)

            @block.tensor
            def _(pe):
                c_id.wait(pe, 3)
                c_gw.wait(pe, 16)
                with pe.Fori(0, NB // 2) as h:
                    for i in range(2):
                        b = h * 2 + i

                        def transposes(k):
                            for j in range(J):
                                if k == 0:
                                    c_xn.wait(pe, b * J + j + 1)
                                last = pe.transpose(pt[k % 2][:, j * P:(j + 1) * P],
                                                    ext[i][:, j, k * P:(k + 1) * P], ident[:, :])
                            last.then_inc(c_t.sem, 1)

                        def share(k):
                            c_tc.wait(pe, b * KD + k + 1)
                            pe.matmul(pst[:, :], gw[:, k, :], xnt[k % 2][:, :], start=(k == 0),
                                      stop=(k == KD - 1)).then_inc(c_st_.sem, 1)

                        c_tc.wait(pe, b * KD)
                        transposes(0)
                        transposes(1)
                        c_sr.wait(pe, b)
                        share(0)
                        transposes(2)
                        share(1)
                        transposes(3)
                        share(2)
                        share(3)
                        c_sr.wait(pe, b + 1)
                        c_th.wait(pe, b)
                        pe.sem_inc(t_tick, 1)
                        for j in range(J):
                            last = pe.transpose(psc[:, j * E:(j + 1) * E], sc_t[:, j * P:(j + 1) * P],
                                                ident[0:E, 0:E])
                        last.then_inc(c_sc.sem, 1)

            @block.scalar
            def _(act):
                def high_parts():
                    c_win.wait(act, 64)
                    act.copy(w.wout_h[:, :, :], staged[:, :, :]).then_inc(c_sh.sem, 1)
                    act.copy(w.wc_h[:, :], staged2[:, 0:2, :].rearrange("p a b -> p (a b)")).then_inc(c_sh.sem, 1)
                    c_in.wait(act, 1)
                    act.copy(w.wb[:, :, 0:S], staged2[:, 3, :].rearrange("p (c s) -> p c s", s=S)).then_inc(c_sh.sem, 1)

                def turns(first, end):
                    with act.Fori(first, end) as h:
                        for i in range(2):
                            b = h * 2 + i
                            for k in range(KD):
                                c_t.wait(act, b * KD + k + 1)
                                c_st_.wait(act, b * KD if k < 2 else b * KD + k - 1)
                                act.copy(xnt[k % 2][:, :], pt[k % 2][:, :]).then_inc(c_tc.sem, 1)
                            c_st_.wait(act, (b + 1) * KD)
                            c_sc.wait(act, b)
                            act.copy(sc_t[:, :], pst[:, :]).then_inc(c_sr.sem, 1)
                            c_sc.wait(act, b + 1)
                            c_v.wait(act, b * 2)
                            act.activation(tanh[:, :], psc[:, :], ACT.Tanh).then_inc(c_th.sem, 1)
                            c_v.wait(act, b * 2 + 1)
                            act.dma_start(xn_v[b], ext[i][:, :, :]).then_inc(c_st[i].sem, 16)

                turns(0, NB // 4)
                high_parts()
                turns(NB // 4, NB // 2)
                for i in range(2):
                    c_st[i].wait(act, 16 * (NB // 2))


BIS = 5
BIS_PER_TURN = 2
assert BIS_PER_TURN * NB >= 26


def count_at_or_above(dve, gates, bis, c_cand, c_cnt, n):
    thr, step, cand, ge, cnt, tot = bis
    c_cand.wait(dve, BIS * n + 1)
    c_cnt.wait(dve, 2 * n)
    dve.tensor_tensor(ge[:, :, :], gates[:, :, :],
                      cand[:, :].rearrange("p (e o) -> p e o", o=1).to_broadcast([P, E, NT]),
                      ALU.is_ge).then_inc(c_cnt.sem, 1)
    c_cnt.wait(dve, 2 * n + 1)
    dve.tensor_reduce(cnt[:, :], ge[:, :, :], AX.X, ALU.add).then_inc(c_cnt.sem, 1)


def halve(pool, bis, c_cand, c_cnt, n, hold):
    thr, step, cand, ge, cnt, tot = bis
    c_cnt.wait(pool, 2 * n + 2)
    c_cand.wait(pool, BIS * n + 1)
    hold()
    pool.partition_all_reduce(tot[:, :], cnt[:, :], P, RADD).then_inc(c_cand.sem, 1)
    c_cand.wait(pool, BIS * n + 2)
    hold()
    pool.tensor_scalar(tot[:, :], tot[:, :], float(CAP), step[:, 0:1], ALU.is_ge, ALU.mult).then_inc(c_cand.sem, 1)
    c_cand.wait(pool, BIS * n + 3)
    pool.tensor_tensor(thr[:, :], thr[:, :], tot[:, :], ALU.add).then_inc(c_cand.sem, 1)
    hold()
    pool.tensor_scalar(step[:, :], step[:, :], 0.5, None, ALU.mult).then_inc(c_cand.sem, 1)
    c_cand.wait(pool, BIS * n + 5)
    hold()
    pool.tensor_scalar(cand[:, :], thr[:, :], step[:, 0:1], None, ALU.add).then_inc(c_cand.sem, 1)


def stage_mixer(nc, t, gates, thr, ident, w):
    LATE = 2
    FIN = 2
    TAPS = 3
    with ExitStack() as stack:
        m = Mem(nc, stack)
        wh = [m.sb(f"wh{i}", [P, KD * P], F32R) for i in range(4)]
        wl = [m.sb(f"wl{i}", [P, KD * P], F32R) for i in range(4)]
        xt_h = m.sb("xt_h", [P, KD, TB], F32R)
        xt_l = m.sb("xt_l", [P, KD, TB], F32R)
        rows = m.sb("xn_next", [P, J, D])
        u = m.sb("u", [P, NC_, TB])
        u_h = [m.sb(f"u_h{i}", [P, TB], F32R) for i in range(2)]
        u_l = [m.sb(f"u_l{i}", [P, TB], F32R) for i in range(2)]
        y_h = [m.sb(f"y_h{i}", [P, TB], F32R) for i in range(3)]
        y_l = [m.sb(f"y_l{i}", [P, TB], F32R) for i in range(3)]
        sg = m.sb("sg", [P, NC_, TB])
        xin = [m.sb(f"xin{i}", [P, 3 + TB]) for i in range(2)]
        halo = m.sb("halo", [P, NC_, 3])
        h = m.sb("h", [P, TB])
        h_h = m.sb("h_h", [P, TB], F32R)
        h_l = m.sb("h_l", [P, TB], F32R)
        carry = m.sb("carry", [P, 1])
        decay = m.sb("decay", [P, 1])
        xtail = [m.sb(f"x_tail{i}", [P, D]) for i in range(2)]
        ntail = [m.sb(f"xn_tail{j}", [P, D]) for j in range(J)]
        res = [m.sb(f"res{j}", [P, D]) for j in range(J)]
        stats = m.sb("stats", [P, J, 6])
        mv = m.sb("mv", [P, J, 2])
        std = m.sb("std", [P, J])
        rstd = m.sb("rstd", [P, J])
        half = m.sb("half", [P, 1])
        step = m.sb("bis_step", [P, 1])
        cand = m.sb("bis_cand", [P, E])
        ge = m.sb("bis_ge", [P, E, NT], BF16)
        cnt = m.sb("bis_cnt", [P, E])
        tot = m.sb("bis_tot", [P, E])
        first = m.sb("first", [P, J, NC_])
        bis = (thr, step, cand, ge, cnt, tot)
        ring = [m.ps(f"ring{i}", [P, TB]) for i in range(2)]
        pb = m.ps("pb", [P, TB])
        pc = m.ps("pc", [P, TB])
        po = [m.ps(f"po{j}", [P, D]) for j in range(J)]

        c_rows = m.count("m_rows")
        c_nt = [m.count(f"m_nt{j}") for j in range(J)]
        c_xt = [m.count(f"m_xt{i}") for i in range(2)]
        c_st = [m.pool_count(f"m_st{j}") for j in range(J)]
        c_set = m.count("m_set")
        c_wh = m.count("m_wh")
        c_wl = m.count("m_wl")
        c_ag = m.count("m_ag")
        c_x = m.count("m_x")
        c_ev = m.count("m_ev")
        c_halo = m.count("m_halo")
        c_cv = m.count("m_cv")
        c_u = m.count("m_u")
        c_uh = m.count("m_uh")
        c_ul = m.count("m_ul")
        c_b = m.count("m_b")
        c_h = m.count("m_h")
        c_car = m.count("m_car")
        c_hh = m.count("m_hh")
        c_hl = m.count("m_hl")
        c_c = m.count("m_c")
        c_y1 = m.count("m_y1")
        c_y2 = m.count("m_y2")
        c_yh = m.count("m_yh")
        c_yl = m.count("m_yl")
        c_o = m.count("m_o")
        c_t = m.count("m_t")
        c_th = m.count("m_th")
        c_tl = m.count("m_tl")
        c_r = m.count("m_r")
        c_bn = m.count("m_bn")
        c_mv = m.count("m_mv")
        c_eps = m.count("m_eps")
        c_rs = m.count("m_rs")
        c_g = m.count("m_g")
        c_nm = m.count("m_nm")
        c_fin = m.count("m_fin")
        c_cand = m.count("m_cand")
        c_cnt = m.count("m_cnt")
        z = m.count("m_zero")
        p_tick = m.tick("m_ptick")
        d_tick = m.tick("m_dtick")

        x_v = t["x"].rearrange("(b j p) d -> b j p d", p=P, j=J)
        xn_v = t["xn"].rearrange("(b j p) d -> b j p d", p=P, j=J)
        o_v = t["out"].rearrange("(b j p) d -> b j p d", p=P, j=J)

        def column(s):
            s %= NW
            return s // 2 + NC_ * (s % 2)

        m.start()
        with nc.Block() as block:
            @block.sync
            def _(sp):
                def load_rows(b):
                    sp.dma_start(rows[:, :, :], xn_v[b].rearrange("j p d -> p j d")[:, :, 0:D]).then_inc(c_rows.sem, 16)

                def load_x(b, j, reused=True):
                    if reused:
                        c_fin.wait(sp, FIN * (b * J + j - 1))
                    sp.dma_start(xtail[j % 2][:, :], x_v[b, j]).then_inc(c_xt[j % 2].sem, 16)

                def load_xn(b):
                    c_fin.wait(sp, FIN * J * b)
                    for j in range(J):
                        sp.dma_start(ntail[j][:, :], xn_v[b, j][:, 0:D]).then_inc(c_nt[j].sem, 16)

                load_rows(0)
                c_t.wait(sp, KD)
                load_rows(1)
                load_x(0, 0, False)
                load_x(0, 1, False)
                load_xn(0)
                c_t.wait(sp, 2 * KD)
                load_rows(2)
                with sp.Fori(2, NB - 1) as b:
                    c_t.wait(sp, (b + 1) * KD)
                    load_rows(b + 1)
                    load_x(b - 2, 2)
                    load_x(b - 2, 3)
                    load_x(b - 1, 0)
                    load_x(b - 1, 1)
                    load_xn(b - 1)
                c_t.wait(sp, NB * KD)
                load_rows(0)
                for b in (NB - 3, NB - 2):
                    load_x(b, 2)
                    load_x(b, 3)
                    load_x(b + 1, 0)
                    load_x(b + 1, 1)
                    load_xn(b + 1)
                load_x(NB - 1, 2)
                load_x(NB - 1, 3)

            @block.gpsimd
            def _(pool):
                def hold():
                    pool.sem_inc(p_tick, 1)

                for j in range(J):
                    c_st[j].prime(pool, first[:, j, :], t["conv_b"])
                pool.memset(half[:, :], -0.5).then_inc(c_set.sem, 1)
                pool.memset(decay[:, :], DECAY).then_inc(c_set.sem, 1)
                pool.memset(thr[:, :], 0.0).then_inc(c_set.sem, 1)
                pool.memset(step[:, :], 1.0).then_inc(c_set.sem, 1)
                c_set.wait(pool, 4)
                pool.tensor_scalar(cand[:, :], thr[:, :], step[:, 0:1], None, ALU.add).then_inc(c_cand.sem, 1)

                def w_low(n, s):
                    c_wh.wait(pool, n + 1)
                    pool.tensor_tensor(wl[s % 4][:, :], w.w_in[:, column(s), :], f(wh[s % 4][:, :]),
                                       ALU.subtract).then_inc(c_wl.sem, 1)

                def inverse_std(b, j):
                    n = b * J + j
                    c_mv.wait(pool, n + 1)
                    c_rs.wait(pool, n)
                    hold()
                    pool.tensor_scalar(std[:, j:j + 1], mv[:, j, 1:2], EPS, None, ALU.add).then_inc(c_eps.sem, 1)
                    c_eps.wait(pool, n + 1)
                    pool.tensor_tensor(rstd[:, j:j + 1], std[:, j:j + 1], half[:, :], ALU.pow).then_inc(c_rs.sem, 1)

                def finish(b, j):
                    n = b * J + j
                    c_nm.wait(pool, n + 1)
                    c_xt[j % 2].wait(pool, 16 * (b * (J // 2) + j // 2 + 1))
                    for q, other in enumerate((ntail[j], xtail[j % 2])):
                        c_fin.wait(pool, FIN * n + q)
                        pool.tensor_tensor(res[j][:, :], res[j][:, :], other[:, :], ALU.add).then_inc(c_fin.sem, 1)
                    c_fin.wait(pool, FIN * (n + 1))
                    hold()
                    pool.dma_start(o_v[b, j], res[j][:, :]).then_inc(c_st[j].sem, 16)

                def turn(b, with_end):
                    for s in range(NW):
                        w_low(b * NW + s + 3, s + 3)
                        if with_end and s in (2, 5, 8, 11):
                            inverse_std(b - 2, s // 3)
                        if with_end and s in (4, 7, 10, 13):
                            finish(b - 2, s // 3 - 1)
                    for q in range(BIS_PER_TURN):
                        halve(pool, bis, c_cand, c_cnt, b * BIS_PER_TURN + q, hold)

                for s in range(3):
                    w_low(s, s)
                with pool.Fori(0, 2) as b:
                    turn(b, False)
                with pool.Fori(2, NB) as b:
                    turn(b, True)
                for b in (NB - 2, NB - 1):
                    for j in range(J):
                        inverse_std(b, j)
                    for j in range(J):
                        finish(b, j)
                for j in range(J):
                    c_st[j].wait(pool, 16 * NB)

            @block.scalar
            def _(act):
                def w_high(n, s):
                    act.copy(wh[s % 4][:, :], w.w_in[:, column(s), :]).then_inc(c_wh.sem, 1)

                def t_high(n, k):
                    c_t.wait(act, n + 1)
                    act.copy(xt_h[:, k, :], ring[k % 2][:, :]).then_inc(c_th.sem, 1)

                def u_pair(b, c):
                    n = b * NC_ + c
                    c_cv.wait(act, TAPS * (n + 1))
                    act.activation(u[:, c, :], u[:, c, :], ACT.Silu).then_inc(c_u.sem, 1)
                    c_u.wait(act, n + 1)
                    c_b.wait(act, b * NC_ if c < 2 else n - 1)
                    c_ul.wait(act, b * NC_ if c < 2 else n - 1)
                    act.copy(u_h[c % 2][:, :], u[:, c, :]).then_inc(c_uh.sem, 1)

                def y_high(b, c):
                    n = b * NC_ + c
                    c_o.wait(act, b * NC_ if c < 3 else n - 2)
                    c_yl.wait(act, b * NC_ if c < 3 else n - 2)
                    c_y2.wait(act, n + 1)
                    act.copy(y_h[c % 3][:, :], u[:, c, :]).then_inc(c_yh.sem, 1)

                for s in range(3):
                    w_high(s, s)
                for k in range(KD):
                    t_high(k, k)

                with act.Fori(0, NB) as b:
                    for s in range(NW):
                        n, c = b * NW + s, s // 2
                        c_ag.wait(act, n)
                        c_wl.wait(act, n)
                        w_high(n + 3, s + 3)
                        if s % 2 == 0:
                            c_cv.wait(act, b * (TAPS * NC_) + (TAPS * (c - 1) if c > 1 else 0))
                            c_halo.wait(act, b * (2 * NC_) + (2 * (c - 1) if c > 1 else 0))
                            c_ag.wait(act, n + 1)
                            act.copy(xin[c % 2][:, 3:3 + TB], ring[0][:, :]).then_inc(c_x.sem, 1)
                            c_yl.wait(act, b * NC_)
                            act.activation(u[:, c, :], ring[0][:, :], ACT.Identity, bias=w.cb[:, c:c + 1],
                                           scale=w.cw[:, c, 3:4]).then_inc(c_ev.sem, 1)
                        else:
                            c_y2.wait(act, b * NC_)
                            c_ag.wait(act, n + 1)
                            act.activation(sg[:, c, :], ring[1][:, :], ACT.Silu).then_inc(c_ev.sem, 1)
                            u_pair(b, c)
                    t_high((b + 1) * KD, 0)
                    t_high((b + 1) * KD + 1, 1)
                    c_c.wait(act, b * NC_)
                    c_hl.wait(act, b)
                    c_h.wait(act, b + 1)
                    act.copy(h_h[:, :], h[:, :]).then_inc(c_hh.sem, 1)
                    t_high((b + 1) * KD + 2, 2)
                    y_high(b, 0)
                    t_high((b + 1) * KD + 3, 3)
                    for c in range(1, NC_):
                        y_high(b, c)

            @block.vector
            def _(dve):
                c_set.wait(dve, 4)

                def t_low(n, k):
                    c_th.wait(dve, n + 1)
                    dve.tensor_tensor(xt_l[:, k, :], ring[k % 2][:, :], f(xt_h[:, k, :]),
                                      ALU.subtract).then_inc(c_tl.sem, 1)

                def u_low(b, c):
                    c_uh.wait(dve, b * NC_ + c + 1)
                    dve.tensor_tensor(u_l[c % 2][:, :], u[:, c, :], f(u_h[c % 2][:, :]),
                                      ALU.subtract).then_inc(c_ul.sem, 1)

                def conv(b, c):
                    n = b * NC_ + c
                    x_ = xin[c % 2]
                    c_halo.wait(dve, 2 * n)
                    c_cv.wait(dve, TAPS * (b * NC_ if c < 2 else n - 1))
                    dve.tensor_copy(x_[:, 0:3], halo[:, c, :]).then_inc(c_halo.sem, 1)
                    c_x.wait(dve, n + 1)
                    c_halo.wait(dve, 2 * n + 1)
                    dve.tensor_copy(halo[:, c, :], x_[:, TB:TB + 3]).then_inc(c_halo.sem, 1)
                    c_ev.wait(dve, b * NW + 2 * c + 1)
                    for q in range(1, TAPS + 1):
                        c_cv.wait(dve, TAPS * n + q - 1)
                        dve.scalar_tensor_tensor(out=u[:, c, :], in0=x_[:, 3 - q:3 - q + TB],
                                                 scalar=w.cw[:, c, 3 - q:4 - q], in1=u[:, c, :],
                                                 op0=ALU.mult, op1=ALU.add).then_inc(c_cv.sem, 1)

                def scan(b):
                    c_b.wait(dve, (b + 1) * NC_)
                    c_hh.wait(dve, b)
                    c_hl.wait(dve, b)
                    c_car.wait(dve, b)
                    dve.tensor_tensor_scan(h[:, :], decay[:, 0:1].to_broadcast([P, TB]), pb[:, :], carry[:, 0:1],
                                           ALU.mult, ALU.add).then_inc(c_h.sem, 1)
                    c_h.wait(dve, b + 1)
                    dve.tensor_copy(carry[:, :], h[:, TB - 1:TB]).then_inc(c_car.sem, 1)

                def h_low(b):
                    c_hh.wait(dve, b + 1)
                    dve.tensor_tensor(h_l[:, :], h[:, :], f(h_h[:, :]), ALU.subtract).then_inc(c_hl.sem, 1)

                def y_turn(b, c):
                    n = b * NC_ + c
                    c_c.wait(dve, n + 1)
                    dve.scalar_tensor_tensor(out=u[:, c, :], in0=u[:, c, :], scalar=w.dp[:, c:c + 1],
                                             in1=pc[:, :], op0=ALU.mult, op1=ALU.add).then_inc(c_y1.sem, 1)
                    c_ev.wait(dve, b * NW + 2 * c + 2)
                    c_y1.wait(dve, n + 1)
                    dve.tensor_tensor(u[:, c, :], u[:, c, :], sg[:, c, :], ALU.mult).then_inc(c_y2.sem, 1)

                def y_low(b, c):
                    c_yh.wait(dve, b * NC_ + c + 1)
                    dve.tensor_tensor(y_l[c % 3][:, :], u[:, c, :], f(y_h[c % 3][:, :]),
                                      ALU.subtract).then_inc(c_yl.sem, 1)

                def add_xn(b, j):
                    c_o.wait(dve, (b + 1) * NC_)
                    c_nt[j].wait(dve, 16 * (b + 1))
                    c_st[j].wait(dve, 16 * b)
                    dve.tensor_tensor(res[j][:, :], po[j][:, :], ntail[j][:, :], ALU.add).then_inc(c_r.sem, 1)

                def statistics(b, j):
                    n = b * J + j
                    c_r.wait(dve, n + 1)
                    c_mv.wait(dve, b * J)
                    dve.bn_stats(stats[:, j, :], res[j][:, :]).then_inc(c_bn.sem, 1)
                    c_bn.wait(dve, n + 1)
                    c_rs.wait(dve, b * J)
                    c_nm.wait(dve, b * J)
                    dve.sem_inc(d_tick, 1)
                    dve.bn_aggr(mv[:, j, :], stats[:, j, :]).then_inc(c_mv.sem, 1)

                def norm(b, j):
                    n = b * J + j
                    c_rs.wait(dve, n + 1)
                    c_mv.wait(dve, n + 1)
                    c_g.wait(dve, n)
                    dve.scalar_tensor_tensor(out=res[j][:, :], in0=res[j][:, :], scalar=mv[:, j, 0:1],
                                             in1=w.gamma[:, :], op0=ALU.subtract, op1=ALU.mult).then_inc(c_g.sem, 1)
                    c_g.wait(dve, n + 1)
                    dve.scalar_tensor_tensor(out=res[j][:, :], in0=res[j][:, :], scalar=rstd[:, j:j + 1],
                                             in1=w.beta[:, :], op0=ALU.mult, op1=ALU.add).then_inc(c_nm.sem, 1)

                def turn(b, with_last, with_end):
                    for c in range(NC_):
                        conv(b, c)
                        if with_end and c % 2 == 0:
                            statistics(b - 2, c // 2)
                        u_low(b, c)
                        if with_end and c % 2 == 1:
                            norm(b - 2, c // 2)
                    t_low((b + 1) * KD, 0)
                    t_low((b + 1) * KD + 1, 1)
                    scan(b)
                    if with_last:
                        add_xn(b - 1, 0)
                    h_low(b)
                    if with_last:
                        for j in range(1, J):
                            add_xn(b - 1, j)
                    for c in range(NC_):
                        y_turn(b, c)
                        if c < 2:
                            t_low((b + 1) * KD + 2 + c, 2 + c)
                        y_low(b, c)
                        if c in (2, 5):
                            count_at_or_above(dve, gates, bis, c_cand, c_cnt, b * BIS_PER_TURN + c // 3)

                def new_sequence(b):
                    c_halo.wait(dve, 2 * NC_ * b)
                    c_car.wait(dve, b)
                    c_h.wait(dve, b)
                    dve.memset(halo[:, :, :], 0.0).then_inc(z.sem, 1)
                    dve.memset(carry[:, :], 0.0).then_inc(z.sem, 1)

                for k in range(KD):
                    t_low(k, k)
                new_sequence(0)
                z.wait(dve, 2)
                turn(0, False, False)
                turn(1, True, False)
                with dve.Fori(2, BPS) as b:
                    turn(b, True, True)
                with dve.Fori(1, NB // BPS) as q:
                    new_sequence(q * BPS)
                    z.wait(dve, 2 * q + 2)
                    dve.sem_inc(d_tick, 1)
                    with dve.Fori(0, BPS) as r:
                        turn(q * BPS + r, True, True)
                for b in (NB - 2, NB - 1):
                    if b == NB - 1:
                        for j in range(J):
                            add_xn(b, j)
                    for j in range(J):
                        statistics(b, j)
                    for j in range(J):
                        norm(b, j)

            @block.tensor
            def _(pe):
                def three(dst, ah, al, bh, bl, start, stop):
                    pe.matmul(dst, ah, bh, start=start, stop=False)
                    pe.matmul(dst, ah, bl, start=False, stop=False)
                    return pe.matmul(dst, al, bh, start=False, stop=stop)

                def ag(b, s):
                    n = b * NW + s
                    c_wl.wait(pe, n + 1)
                    if s == 0:
                        c_th.wait(pe, (b + 1) * KD)
                        c_tl.wait(pe, (b + 1) * KD)
                    if s > 1:
                        c_ev.wait(pe, n - 1)
                    for k in range(KD):
                        r = slice(k * P, (k + 1) * P)
                        last = three(ring[s % 2][:, :], wh[s % 4][:, r], wl[s % 4][:, r],
                                     xt_h[:, k, :], xt_l[:, k, :], k == 0, k == KD - 1)
                    last.then_inc(c_ag.sem, 1)

                def share_b(b, c):
                    c_ul.wait(pe, b * NC_ + c + 1)
                    if c == 0:
                        c_h.wait(pe, b)
                    pe.matmul(pb[:, :], w.wb[:, c, :], u_h[c % 2][:, :], start=(c == 0), stop=False)
                    pe.matmul(pb[:, :], w.wb[:, c, :], u_l[c % 2][:, :], start=False,
                              stop=(c == NC_ - 1)).then_inc(c_b.sem, 1)

                def chan(b, c):
                    r = slice(c * P, (c + 1) * P)
                    c_y1.wait(pe, b * NC_ + c)
                    if c == 0:
                        c_hl.wait(pe, b + 1)
                    three(pc[:, :], w.wc_h[:, r], w.wc_l[:, r], h_h[:, :], h_l[:, :], True, True).then_inc(c_c.sem, 1)

                def out_share(b, c):
                    c_yl.wait(pe, b * NC_ + c + 1)
                    if c == 0:
                        c_r.wait(pe, b * J)
                    for j in range(J):
                        r = slice(j * P, (j + 1) * P)
                        last = three(po[j][:, :], y_h[c % 3][:, r], y_l[c % 3][:, r],
                                     w.wout_h[:, c, :], w.wout_l[:, c, :], c == 0, c == NC_ - 1)
                    last.then_inc(c_o.sem, 1)

                def transposes(k):
                    for j in range(J):
                        last = pe.transpose(ring[k % 2][:, j * P:(j + 1) * P], rows[:, j, k * P:(k + 1) * P],
                                            ident[:, :])
                    last.then_inc(c_t.sem, 1)

                def next_turn(b, k):
                    if k == 0:
                        c_rows.wait(pe, 16 * (b + 2))
                    if k < 2:
                        c_ev.wait(pe, b * NW + NW - 1 + k)
                    else:
                        c_th.wait(pe, (b + 1) * KD + k - 1)
                        c_tl.wait(pe, (b + 1) * KD + k - 1)
                    transposes(k)

                def turn(b, with_last):
                    for s in range(NW):
                        ag(b, s)
                        if s % 2 == 1 and s > 1:
                            share_b(b, s // 2 - 1)
                    if with_last:
                        out_share(b - 1, NC_ - 2)
                    next_turn(b, 0)
                    next_turn(b, 1)
                    share_b(b, NC_ - 1)
                    if with_last:
                        out_share(b - 1, NC_ - 1)
                    chan(b, 0)
                    next_turn(b, 2)
                    chan(b, 1)
                    next_turn(b, 3)
                    for c in range(2, NC_):
                        chan(b, c)
                        out_share(b, c - 2)

                c_rows.wait(pe, 16)
                for k in range(KD):
                    if k >= 2:
                        c_th.wait(pe, k - 1)
                        c_tl.wait(pe, k - 1)
                    transposes(k)
                turn(0, False)
                with pe.Fori(1, NB) as b:
                    turn(b, True)
                for c in range(NC_ - LATE, NC_):
                    out_share(NB - 1, c)


def stage_lists(nc, gates, thr, slots_d):
    EN = E * NT
    NONE = 4096.0
    EG = P // HI
    NQ = 4
    TQ = NT // NQ
    with ExitStack() as stack:
        m = Mem(nc, stack)
        gt = m.sb("l_gt", [P, EN], BF16)
        eq = m.sb("l_eq", [P, EN], BF16)
        gt_f = m.sb("l_gt_f", [P, EN])
        eq_f = m.sb("l_eq_f", [P, EN])
        before = m.sb("l_before", [P, P], BF16)
        ones = m.sb("l_ones", [P, P], BF16)
        one = m.sb("l_one", [P, 1])
        run_gt = m.sb("l_run_gt", [P, EN])
        run_eq = m.sb("l_run_eq", [P, EN])
        slot = m.sb("l_slot", [P, EN])
        slot_i = m.sb("l_slot_i", [P, EN], U32)
        hi_i = m.sb("l_hi_i", [P, EN], U32)
        lo_i = m.sb("l_lo_i", [P, EN], U32)
        hi = m.sb("l_hi", [P, E, NT], BF16)
        lo = m.sb("l_lo", [P, E, NT], BF16)
        digit = m.sb("l_digit", [P, LO], BF16)
        tile_no = m.sb("l_tile", [P, NT], BF16)
        row_no = m.sb("l_row", [P, 1])
        hi1 = m.sb("l_hi1", [P, NT, E, HI], BF16)
        lo1 = m.sb("l_lo1", [P, NT, E, LO], BF16)
        lov = m.sb("l_lov", [P, NT, E, 2, LO], BF16)
        both = m.sb("l_both", [P, E // EG, EG * 2 * LO])
        token_f = m.sb("l_token_f", [P, E // EG, LO])
        token = m.sb("l_token", [P, E // EG, LO], U32)
        p_before = [m.ps(f"l_pb{i}", [P, EN]) for i in range(2)]
        p_all = [m.ps(f"l_pa{i}", [P, EN]) for i in range(2)]
        p_tok = [m.ps(f"l_pt{g}", [P, EG * 2 * LO]) for g in range(E // EG)]
        c_set = m.count("l_set")
        c_v = m.count("l_v")
        c_pre = m.count("l_pre")
        c_lo1 = m.count("l_lo1c")
        c_oh = m.count("l_oh")
        c_row = m.count("l_rowc")
        c_tok = m.count("l_tok")
        c_list = m.count("l_list")
        c_out = m.count("l_out")

        def by_expert(ap):
            return ap.rearrange("p (e r) -> p e r", e=E)

        m.start()
        with nc.Block() as block:
            @block.sync
            def _(sp):
                c_list.wait(sp, 1)
                sp.dma_start(slots_d.rearrange("(g q) l -> q g l", q=P), token[:, :, :]).then_inc(c_out.sem, 16)
                c_out.wait(sp, 16)

            @block.gpsimd
            def _(pool):
                pool.memset(ones[:, :], 1.0).then_inc(c_set.sem, 1)
                pool.memset(one[:, :], 1.0).then_inc(c_set.sem, 1)
                c_set.wait(pool, 1)
                pool.affine_select(out=before[:, :], in_=ones[:, :], compare_op=ALU.is_ge, fill=0.0,
                                   base=-1, pattern=[[1, P]], channel_multiplier=-1).then_inc(c_set.sem, 1)
                pool.iota(digit[:, :], [[1, LO]], base=0, channel_multiplier=0,
                          allow_small_or_imprecise_dtypes=True).then_inc(c_set.sem, 1)
                pool.iota(tile_no[:, :], [[1, NT]], base=0, channel_multiplier=0,
                          allow_small_or_imprecise_dtypes=True).then_inc(c_set.sem, 1)
                pool.iota(row_no[:, :], [[0, 1]], base=0, channel_multiplier=1,
                          allow_small_or_imprecise_dtypes=True).then_inc(c_set.sem, 1)

            @block.vector
            def _(dve):
                steps = 0

                def done(ins):
                    nonlocal steps
                    ins.then_inc(c_v.sem, 1)
                    steps += 1

                def chained(ins):
                    done(ins)
                    c_v.wait(dve, steps)

                thr_b = thr[:, :].rearrange("p (e o) -> p e o", o=1).to_broadcast([P, E, NT])
                c_set.wait(dve, 6)
                done(dve.tensor_tensor(by_expert(gt[:, :]), gates[:, :, :], thr_b, ALU.is_gt))
                done(dve.tensor_tensor(by_expert(eq[:, :]), gates[:, :, :], thr_b, ALU.is_equal))
                done(dve.tensor_tensor(by_expert(gt_f[:, :]), gates[:, :, :], thr_b, ALU.is_gt))
                done(dve.tensor_tensor(by_expert(eq_f[:, :]), gates[:, :, :], thr_b, ALU.is_equal))
                for i, run in enumerate((run_gt, run_eq)):
                    c_pre.wait(dve, 2 * i + 2)
                    for e in range(E):
                        w = slice(e * NT, (e + 1) * NT)
                        done(dve.tensor_tensor_scan(run[:, w], one[:, 0:1].to_broadcast([P, NT]), p_all[i][:, w],
                                                    0.0, ALU.mult, ALU.add))
                c_v.wait(dve, steps)
                total_gt = by_expert(run_gt[:, :])[:, :, NT - 1:NT].to_broadcast([P, E, NT])
                chained(dve.tensor_tensor(by_expert(run_eq[:, :]), by_expert(run_eq[:, :]), total_gt, ALU.add))
                for i, run in enumerate((run_gt, run_eq)):
                    done(dve.tensor_tensor(run[:, :], run[:, :], p_all[i][:, :], ALU.subtract))
                c_v.wait(dve, steps)
                for i, run in enumerate((run_gt, run_eq)):
                    done(dve.tensor_tensor(run[:, :], run[:, :], p_before[i][:, :], ALU.add))
                c_v.wait(dve, steps)
                for run, mask in ((run_gt, gt_f), (run_eq, eq_f)):
                    done(dve.scalar_tensor_tensor(out=run[:, :], in0=run[:, :], scalar=NONE, in1=mask[:, :],
                                                  op0=ALU.subtract, op1=ALU.mult))
                c_v.wait(dve, steps)
                chained(dve.scalar_tensor_tensor(out=slot[:, :], in0=run_gt[:, :], scalar=NONE, in1=run_eq[:, :],
                                                 op0=ALU.add, op1=ALU.add))
                chained(dve.tensor_copy(slot_i[:, :], slot[:, :]))
                done(dve.tensor_scalar(hi_i[:, :], slot_i[:, :], 5, None, ALU.logical_shift_right))
                chained(dve.tensor_scalar(lo_i[:, :], slot_i[:, :], LO - 1, None, ALU.bitwise_and))
                done(dve.tensor_copy(hi[:, :, :], by_expert(hi_i[:, :])))
                chained(dve.tensor_copy(lo[:, :, :], by_expert(lo_i[:, :])))
                for q in range(NQ):
                    r = slice(q * TQ, (q + 1) * TQ)

                    def spread(x):
                        return x[:, :, r].rearrange("p e (t o) -> p t e o", o=1).to_broadcast([P, TQ, E, LO])

                    digits = digit[:, :].rearrange("p (a b l) -> p a b l", a=1, b=1).to_broadcast([P, TQ, E, LO])
                    dve.tensor_tensor(lo1[:, r, :, :], spread(lo), digits, ALU.is_equal).then_inc(c_lo1.sem, 1)
                    dve.tensor_tensor(hi1[:, r, :, :], spread(hi), digits, ALU.is_equal).then_inc(c_oh.sem, 1)
                    c_lo1.wait(dve, q + 1)
                    tiles = tile_no[:, r].rearrange("p (t a o) -> p t a o", a=1, o=1).to_broadcast([P, TQ, E, LO])
                    dve.tensor_tensor(lov[:, r, :, 1, :], lo1[:, r, :, :], tiles, ALU.mult).then_inc(c_oh.sem, 1)
                for g in range(E // EG):
                    c_tok.wait(dve, g + 1)
                    done(dve.tensor_copy(both[:, g, :], p_tok[g][:, :]))
                c_v.wait(dve, steps)
                for x in range(EG):
                    q, w = slice(x * HI, (x + 1) * HI), x * 2 * LO
                    done(dve.scalar_tensor_tensor(out=token_f[q, :, :], in0=both[q, :, w + LO:w + 2 * LO],
                                                  scalar=float(P), in1=both[q, :, w:w + LO],
                                                  op0=ALU.mult, op1=ALU.add))
                c_v.wait(dve, steps)
                dve.tensor_copy(token[:, :, :], token_f[:, :, :]).then_inc(c_list.sem, 1)

            @block.scalar
            def _(act):
                for q in range(NQ):
                    r = slice(q * TQ, (q + 1) * TQ)
                    c_lo1.wait(act, q + 1)
                    act.activation(lov[:, r, :, 0, :], lo1[:, r, :, :], ACT.Copy,
                                   scale=row_no[:, 0:1]).then_inc(c_row.sem, 1)

            @block.tensor
            def _(pe):
                c_set.wait(pe, 3)
                for i, mask in enumerate((gt, eq)):
                    c_v.wait(pe, i + 1)
                    pe.matmul(p_before[i][:, :], before[:, :], mask[:, :], start=True, stop=True).then_inc(c_pre.sem, 1)
                    pe.matmul(p_all[i][:, :], ones[:, :], mask[:, :], start=True, stop=True).then_inc(c_pre.sem, 1)
                for q in range(NQ):
                    c_oh.wait(pe, 2 * q + 2)
                    c_row.wait(pe, q + 1)
                    for r in range(q * TQ, (q + 1) * TQ):
                        for g in range(E // EG):
                            ex = slice(g * EG, (g + 1) * EG)
                            last = pe.matmul(p_tok[g][:, :], hi1[:, r, ex, :].rearrange("p e l -> p (e l)"),
                                             lov[:, r, ex, :, :].rearrange("p e v l -> p (e v l)"),
                                             start=(r == 0), stop=(r == NT - 1))
                            if r == NT - 1:
                                last.then_inc(c_tok.sem, 1)


def stage_experts(nc, t, slots_d, ident):
    G = 2 * E
    T_AT = (9, 11, 13, 14)
    with ExitStack() as stack:
        m = Mem(nc, stack)
        w1r = m.sb("w1r", [P, FT, D])
        w2r = m.sb("w2r", [P, FT, D])
        w1h = [m.sb(f"w1h{i}", [P, D], F32R) for i in range(4)]
        w1l = [m.sb(f"w1l{i}", [P, D], F32R) for i in range(4)]
        w2h = [m.sb(f"w2h{i}", [P, D], F32R) for i in range(4)]
        w2l = [m.sb(f"w2l{i}", [P, D], F32R) for i in range(4)]
        yt_h = [m.sb(f"yt_h{i}", [P, KD, TB], F32R) for i in range(2)]
        yt_l = [m.sb(f"yt_l{i}", [P, KD, TB], F32R) for i in range(2)]
        rows = m.sb("rows", [P, J, XW])
        kept = [m.sb(f"kept{i}", [P, J, E]) for i in range(2)]
        hid = [m.sb(f"hid{i}", [P, TB]) for i in range(2)]
        hid_h = [m.sb(f"hid_h{i}", [P, TB], F32R) for i in range(4)]
        hid_l = [m.sb(f"hid_l{i}", [P, TB], F32R) for i in range(4)]
        b1 = m.sb("b1", [P, (E + 1) * FT])
        b1c = [m.sb(f"b1c{i}", [P, FT]) for i in range(2)]
        b2 = m.sb("b2", [P, E, D])
        gamma = m.sb("f_ln_g", [P, D])
        beta = m.sb("f_ln_b", [P, D])
        idx = m.sb("idx", [P, (G + 1) * J], U32)
        idx_c = [m.sb(f"idx_c{i}", [P, J], U32) for i in range(2)]
        res = [m.sb(f"f_res{j}", [P, D]) for j in range(J)]
        stats = m.sb("f_stats", [P, J, 6])
        mv = m.sb("f_mv", [P, J, 2])
        std = m.sb("f_std", [P, J])
        rstd = m.sb("f_rstd", [P, J])
        half = m.sb("f_half", [P, 1])
        first = m.sb("f_first", [P, 2 * J, FT])
        ph = [m.ps(f"ph{i}", [P, TB]) for i in range(2)]
        pt = [m.ps(f"f_pt{i}", [P, TB]) for i in range(2)]
        po = [m.ps(f"f_po{j}", [P, D]) for j in range(J)]

        c_w = [m.count(f"f_w{i}") for i in range(FT)]
        c_small = m.count("f_small")
        c_set = m.count("f_set")
        c_ga = [m.pool_count(f"f_ga{j}") for j in range(J)]
        c_sc = [m.pool_count(f"f_sc{j}") for j in range(J)]
        c_ix = m.count("f_ix")
        c_kp = m.count("f_kp")
        c_b1 = m.count("f_b1")
        c_bn = m.count("f_bn")
        c_mv = m.count("f_mv")
        c_eps = m.count("f_eps")
        c_rs = m.count("f_rs")
        c_nm = m.count("f_nm")
        c_g = m.count("f_g")
        c_t = m.count("f_t")
        c_th = m.count("f_th")
        c_tl = m.count("f_tl")
        c_wh = m.count("f_wh")
        c_wl = m.count("f_wl")
        c_p1 = m.count("f_p1")
        c_p2 = m.count("f_p2")
        c_ge = m.count("f_ge")
        c_hh = m.count("f_hh")
        c_hl = m.count("f_hl")
        c_bw = m.count("f_bw")
        c_rw = m.count("f_rw")
        p_tick = m.tick("f_ptick")
        d_tick = m.tick("f_dtick")

        m.start()
        with nc.Block() as block:
            @block.sync
            def _(sp):

                def load(e, i):
                    sp.dma_start(w1r[:, i, :], t["fc1"][e, i]).then_inc(c_w[i].sem, 16)
                    sp.dma_start(w2r[:, i, :], t["fc2"][e, i]).then_inc(c_w[i].sem, 16)

                sp.dma_start(idx[:, 0:G * J].rearrange("p (e c) -> p e c", e=E),
                             slots_d.rearrange("(e h) l -> e (h l)", e=E)
                             .rearrange("e (p c) -> p e c", p=P)).then_inc(c_small.sem, 16)
                load(0, 0)
                load(0, 1)
                sp.dma_start(gamma[:, :], t["f_ln_g"].to_broadcast([P, D])).then_inc(c_small.sem, 16)
                sp.dma_start(beta[:, :], t["f_ln_b"].to_broadcast([P, D])).then_inc(c_small.sem, 16)
                sp.dma_start(b1[:, 0:E * FT], t["b1"]).then_inc(c_small.sem, 16)
                for i in range(2, 4):
                    load(0, i)
                sp.dma_start(b2[:, :, :].rearrange("p e d -> p (e d)"),
                             t["b2"].to_broadcast([P, E * D])).then_inc(c_small.sem, 16)
                for i in range(4, FT):
                    load(0, i)
                with sp.Fori(0, E - 1) as e:
                    for i in range(FT):
                        c_wl.wait(sp, 2 * ((2 * e + 1) * FT + i + 1))
                        load(e + 1, i)
                for i in range(2):
                    c_wl.wait(sp, 2 * ((G - 1) * FT + i + 1))
                    load(0, i)

            @block.gpsimd
            def _(pool):
                def hold():
                    pool.sem_inc(p_tick, 1)

                for j in range(J):
                    c_ga[j].prime(pool, first[:, j, :], t["b1"][:, 0:FT])
                    c_sc[j].prime(pool, first[:, J + j, :], t["b1"][:, 0:FT])
                pool.memset(half[:, :], -0.5).then_inc(c_set.sem, 1)
                pool.memset(idx[:, G * J:(G + 1) * J], 0).then_inc(c_set.sem, 1)
                pool.memset(b1[:, E * FT:(E + 1) * FT], 0.0).then_inc(c_set.sem, 1)
                c_set.wait(pool, 3)
                c_small.wait(pool, 16 * 5)

                def gather(g, i, first_turn=False):
                    if not first_turn:
                        for j in range(J):
                            c_sc[j].wait(pool, 16 * (g - 1))
                    hold()
                    pool.tensor_copy(idx_c[i][:, :], idx[:, bass.ds(g * J, J)]).then_inc(c_ix.sem, 1)
                    c_ix.wait(pool, g + 1)
                    c_t.wait(pool, g * KD)
                    c_kp.wait(pool, g)
                    hold()
                    for j in range(J):
                        pool.indirect_dma_start(
                            out=rows[:, j, :], out_offset=None, in_=t["xn"][:, :],
                            in_offset=bass.IndirectOffsetOnAxis(ap=idx_c[i][:, j:j + 1], axis=0),
                        ).then_inc(c_ga[j].sem, 16)

                def inverse_std(g):
                    for j in range(J):
                        n = g * J + j
                        c_mv.wait(pool, n + 1)
                        c_rs.wait(pool, n)
                        hold()
                        pool.tensor_scalar(std[:, j:j + 1], mv[:, j, 1:2], EPS, None, ALU.add).then_inc(c_eps.sem, 1)
                        c_eps.wait(pool, n + 1)
                        pool.tensor_tensor(rstd[:, j:j + 1], std[:, j:j + 1], half[:, :], ALU.pow).then_inc(c_rs.sem, 1)

                def scatter(g, i):
                    for j in range(J):
                        c_sc[j].wait(pool, 16 * g)
                    for j in range(J):
                        c_rw.wait(pool, g * J + j + 1)
                        hold()
                        pool.indirect_dma_start(
                            out=t["out"][:, :], in_=res[j][:, :], in_offset=None, compute_op=ALU.add,
                            out_offset=bass.IndirectOffsetOnAxis(ap=idx_c[i][:, j:j + 1], axis=0),
                        ).then_inc(c_sc[j].sem, 16)

                gather(0, 0, True)
                inverse_std(0)
                with pool.Fori(0, E) as e:
                    for i in range(2):
                        g = 2 * e + i
                        gather(g + 1, 1 - i)
                        inverse_std(g + 1)
                        scatter(g, i)
                for j in range(J):
                    c_sc[j].wait(pool, 16 * G)

            @block.scalar
            def _(act):
                def w_high(n, s):
                    act.copy(w1h[s % 4][:, :], w1r[:, s % FT, :]).then_inc(c_wh.sem, 1)
                    act.copy(w2h[s % 4][:, :], w2r[:, s % FT, :]).then_inc(c_wh.sem, 1)

                def t_high(g, k, i):
                    c_t.wait(act, g * KD + k + 1)
                    act.copy(yt_h[i][:, k, :], pt[k % 2][:, :]).then_inc(c_th.sem, 1)

                for s in range(2):
                    c_w[s].wait(act, 32)
                    w_high(s, s)
                for k in range(KD):
                    t_high(0, k, 0)
                with act.Fori(0, E) as e:
                    for i in range(2):
                        g = 2 * e + i
                        for s in range(FT):
                            n = g * FT + s
                            c_p2.wait(act, g * FT if s < 2 else n - 1)
                            if i == 0 or s + 2 < FT:
                                c_w[(s + 2) % FT].wait(act, e * 32 + 32)
                            else:
                                c_w[(s + 2) % FT].wait(act, e * 32 + 64)
                            w_high(n + 2, s + 2)
                            c_hl.wait(act, g * FT if s < 2 else n - 1)
                            c_b1.wait(act, g + 1)
                            c_p1.wait(act, n + 1)
                            act.activation(hid[s % 2][:, :], ph[s % 2][:, :], ACT.Gelu_apprx_tanh,
                                           bias=b1c[i][:, s:s + 1]).then_inc(c_ge.sem, 1)
                            c_p2.wait(act, g * FT if s < 4 else n - 3)
                            c_ge.wait(act, n + 1)
                            act.copy(hid_h[s % 4][:, :], hid[s % 2][:, :]).then_inc(c_hh.sem, 1)
                            if s - 1 in T_AT:
                                t_high(g + 1, T_AT.index(s - 1), 1 - i)

            @block.vector
            def _(dve):
                def w_low(n, s):
                    for q, (r, h, l) in enumerate(((w1r, w1h, w1l), (w2r, w2h, w2l))):
                        c_wh.wait(dve, 2 * n + q + 1)
                        dve.tensor_tensor(l[s % 4][:, :], r[:, s % FT, :], f(h[s % 4][:, :]),
                                          ALU.subtract).then_inc(c_wl.sem, 1)

                def t_low(g, k, i):
                    c_th.wait(dve, g * KD + k + 1)
                    dve.tensor_tensor(yt_l[i][:, k, :], pt[k % 2][:, :], f(yt_h[i][:, k, :]),
                                      ALU.subtract).then_inc(c_tl.sem, 1)

                def statistics(g, j):
                    n = g * J + j
                    c_ga[j].wait(dve, 16 * (g + 1))
                    c_mv.wait(dve, n)
                    dve.bn_stats(stats[:, j, :], rows[:, j, 0:D]).then_inc(c_bn.sem, 1)
                    c_bn.wait(dve, n + 1)
                    c_nm.wait(dve, n)
                    dve.sem_inc(d_tick, 1)
                    dve.bn_aggr(mv[:, j, :], stats[:, j, :]).then_inc(c_mv.sem, 1)

                def normalise(g, j):
                    n = g * J + j
                    c_rs.wait(dve, n + 1)
                    c_mv.wait(dve, n + 1)
                    c_g.wait(dve, n)
                    dve.scalar_tensor_tensor(out=rows[:, j, 0:D], in0=rows[:, j, 0:D], scalar=mv[:, j, 0:1],
                                             in1=gamma[:, :], op0=ALU.subtract, op1=ALU.mult).then_inc(c_g.sem, 1)
                    c_g.wait(dve, n + 1)
                    dve.scalar_tensor_tensor(out=rows[:, j, 0:D], in0=rows[:, j, 0:D], scalar=rstd[:, j:j + 1],
                                             in1=beta[:, :], op0=ALU.mult, op1=ALU.add).then_inc(c_nm.sem, 1)

                def keep(g, e, i, first_turn=False):
                    c_rw.wait(dve, 0 if first_turn else (g - 1) * J)
                    dve.tensor_copy(kept[i][:, :, :], rows[:, :, D:XW]).then_inc(c_kp.sem, 1)
                    c_ge.wait(dve, 0 if first_turn else (g - 1) * FT)
                    dve.sem_inc(d_tick, 1)
                    dve.tensor_copy(b1c[i][:, :], b1[:, bass.ds(e * FT, FT)]).then_inc(c_b1.sem, 1)

                c_small.wait(dve, 16 * 5)
                c_set.wait(dve, 3)
                for j in range(J):
                    statistics(0, j)
                    normalise(0, j)
                keep(0, 0, 0, True)
                for s in range(2):
                    w_low(s, s)
                for k in range(KD):
                    t_low(0, k, 0)
                with dve.Fori(0, E) as e:
                    for i in range(2):
                        g = 2 * e + i
                        for s in range(FT):
                            n = g * FT + s
                            w_low(n + 2, s + 2)
                            if 3 <= s < 3 + J:
                                statistics(g + 1, s - 3)
                            c_hh.wait(dve, n + 1)
                            dve.tensor_tensor(hid_l[s % 4][:, :], hid[s % 2][:, :], f(hid_h[s % 4][:, :]),
                                              ALU.subtract).then_inc(c_hl.sem, 1)
                            if 3 <= s < 3 + J:
                                normalise(g + 1, s - 3)
                            if s == J + 3:
                                keep(g + 1, e + i, 1 - i)
                            if 8 <= s < 8 + J:
                                j = s - 8
                                c_sc[j].wait(dve, 16 * g)
                                c_kp.wait(dve, g + 1)
                                dve.tensor_scalar(res[j][:, :], b2[:, bass.ds(e, 1), :].rearrange("p o d -> p (o d)"),
                                                  kept[i][:, j, bass.ds(e, 1)], None, ALU.mult).then_inc(c_bw.sem, 1)
                            if s - 1 in T_AT:
                                t_low(g + 1, T_AT.index(s - 1), 1 - i)
                        c_p2.wait(dve, (g + 1) * FT)
                        c_bw.wait(dve, (g + 1) * J)
                        for j in range(J):
                            dve.scalar_tensor_tensor(out=res[j][:, :], in0=po[j][:, :],
                                                     scalar=kept[i][:, j, bass.ds(e, 1)], in1=res[j][:, :],
                                                     op0=ALU.mult, op1=ALU.add).then_inc(c_rw.sem, 1)

            @block.tensor
            def _(pe):
                def three(dst, ah, al, bh, bl, start, stop):
                    pe.matmul(dst, ah, bh, start=start, stop=False)
                    pe.matmul(dst, ah, bl, start=False, stop=False)
                    return pe.matmul(dst, al, bh, start=False, stop=stop)

                def trn(g, k):
                    if k == 0:
                        c_nm.wait(pe, J * (g + 1))
                    c_tl.wait(pe, g * KD + (k - 1 if k >= 2 else 0))
                    for j in range(J):
                        last = pe.transpose(pt[k % 2][:, j * P:(j + 1) * P], rows[:, j, k * P:(k + 1) * P],
                                            ident[:, :])
                    last.then_inc(c_t.sem, 1)

                def hidden(g, s, i):
                    n = g * FT + s
                    c_wl.wait(pe, 2 * n + 2)
                    if s == 0:
                        c_tl.wait(pe, (g + 1) * KD)
                    c_ge.wait(pe, g * FT if s < 2 else n - 1)
                    for k in range(KD):
                        w = slice(k * P, (k + 1) * P)
                        last = three(ph[s % 2][:, :], w1h[s % 4][:, w], w1l[s % 4][:, w],
                                     yt_h[i][:, k, :], yt_l[i][:, k, :], k == 0, k == KD - 1)
                    last.then_inc(c_p1.sem, 1)

                def out_share(g, s):
                    c_hl.wait(pe, g * FT + s + 1)
                    if s == 0:
                        c_rw.wait(pe, g * J)
                    for j in range(J):
                        w = slice(j * P, (j + 1) * P)
                        last = three(po[j][:, :], hid_h[s % 4][:, w], hid_l[s % 4][:, w],
                                     w2h[s % 4][:, :], w2l[s % 4][:, :], s == 0, s == FT - 1)
                    last.then_inc(c_p2.sem, 1)

                for k in range(KD):
                    trn(0, k)
                with pe.Fori(0, E) as e:
                    for i in range(2):
                        g = 2 * e + i
                        hidden(g, 0, i)
                        for s in range(1, FT + 1):
                            if s < FT:
                                hidden(g, s, i)
                            out_share(g, s - 1)
                            if s - 1 in T_AT:
                                trn(g + 1, T_AT.index(s - 1))


def build(nc, t):
    t["xn"] = nc.dram_tensor("xn_rows", (N, XW), F32, kind="Internal").ap()
    slots_d = nc.dram_tensor("slots", (E * HI, LO), U32, kind="Internal").ap()
    with ExitStack() as stack:
        m = Mem(nc, stack)
        gates = m.sb("gates", [P, E, NT])
        thr = m.sb("threshold", [P, E])
        ident = m.sb("ident", [P, P])
        with ExitStack() as mixer:
            w = MixerWeights(Mem(nc, mixer))
            stage_gate(nc, t, gates, ident, w)
            stage_mixer(nc, t, gates, thr, ident, w)
        stage_lists(nc, gates, thr, slots_d)
        stage_experts(nc, t, slots_d, ident)


SHAPES = {
    "x": (N, D), "gate_w": (P, KD, E), "w_in": (P, NW, KD * P), "conv_w": (P, NC_, 4), "conv_b": (P, NC_),
    "d_param": (P, NC_), "ln_g": (1, D), "ln_b": (1, D), "w_out": (P, NC_, D), "w_c": (S, 2, D), "w_b": (P, NC_ * S),
    "fc1": (E, FT, P, D), "fc2": (E, FT, P, D), "b1": (P, E * FT), "b2": (1, E * D), "f_ln_g": (1, D), "f_ln_b": (1, D),
}


def kernel(**i):
    import numpy as np
    import concourse.bacc as bacc
    from concourse.bass_utils import run_bass_kernel_spmd as run

    a = {k.replace("L0_", ""): np.asarray(v) for k, v in i.items()}

    def by_channel(v):
        return v.reshape(NC_, P, -1).transpose(1, 0, 2)

    arrays = {
        "x": a["attn_x"].reshape(N, D),
        "gate_w": a["ffn_gate_w"].reshape(E, KD, P).transpose(2, 1, 0),
        "w_in": a["attn_W_in"].reshape(NW, P, KD, P).transpose(3, 0, 2, 1).reshape(P, NW, KD * P),
        "conv_w": by_channel(a["attn_conv_w"]),
        "conv_b": by_channel(a["attn_conv_b"]).reshape(P, NC_),
        "d_param": by_channel(a["attn_D_param"]).reshape(P, NC_),
        "ln_g": a["attn_ln_gamma"].reshape(1, D),
        "ln_b": a["attn_ln_beta"].reshape(1, D),
        "w_out": by_channel(a["attn_W_out"].T),
        "w_c": a["attn_W_C"].T.reshape(S, 2, D),
        "w_b": by_channel(a["attn_W_B"].T).reshape(P, NC_ * S),
        "fc1": a["ffn_fc1s"].reshape(E, FT, P, KD, P).transpose(0, 1, 4, 3, 2).reshape(E, FT, P, D),
        "fc2": a["ffn_fc2s"].transpose(0, 2, 1).reshape(E, FT, P, D),
        "b1": a["ffn_b1s"].reshape(E, FT, P).transpose(2, 0, 1).reshape(P, E * FT),
        "b2": a["ffn_b2s"].reshape(1, E * D),
        "f_ln_g": a["ffn_ln_gamma"].reshape(1, D),
        "f_ln_b": a["ffn_ln_beta"].reshape(1, D),
    }
    arrays = {f"{k}_in": np.ascontiguousarray(v) for k, v in arrays.items()}
    nc = bacc.Bacc("TRN2", target_bir_lowering=False, num_devices=1)
    t = {k: nc.dram_tensor(f"{k}_in", s, F32, kind="ExternalInput").ap() for k, s in SHAPES.items()}
    t["out"] = nc.dram_tensor("out_dram", (N, D), F32, kind="ExternalOutput").ap()
    build(nc, t)
    r = run(nc, [arrays], core_ids=[0])
    return r.results[0]["out_dram"].reshape(a["attn_x"].shape)
```

```python
from contextlib import ExitStack

import concourse.bass as bass
from concourse import mybir
from concourse.alu_op_type import AluOpType as ALU

F32 = mybir.dt.float32
F32R = mybir.dt.float32r
BF16 = mybir.dt.bfloat16
U32 = mybir.dt.uint32
ACT = mybir.ActivationFunctionType
AX = mybir.AxisListType
RADD = bass.bass_isa.ReduceOp.add

P = 128
N, D, C, S, E, F = 8192, 512, 1024, 64, 8, 2048
SEQ = 2048
TB = 512
NB = N // TB
BPS = SEQ // TB
J = TB // P
NT = N // P
KD = D // P
NC_ = C // P
NW = 2 * NC_
FT = F // P
CAP = N // E
CH = CAP // P
XW = D + E
EPS = 1e-5
DECAY, INPUT_FACTOR = 0.95, 0.05
LO = 32
HI = CAP // LO


class Count:

    def __init__(self, sem):
        self.sem = sem

    def start(self, eng):
        eng.sem_inc(self.sem, 1)

    def wait(self, eng, pieces):
        eng.wait_ge(self.sem, pieces + 1)


class PoolCount(Count):

    def start(self, eng):
        pass

    def prime(self, pool, dst, src):
        pool.dma_start(dst, src).then_inc(self.sem, 16)

    def wait(self, eng, pieces):
        eng.wait_ge(self.sem, pieces + 16)


class Mem:

    def __init__(self, nc, stack):
        self.nc, self.stack, self.counts = nc, stack, []
        self.ticks = {}

    def sb(self, name, shape, dt=F32):
        return self.stack.enter_context(self.nc.sbuf_tensor(name, shape, dt))

    def ps(self, name, shape, dt=F32):
        return self.stack.enter_context(self.nc.psum_tensor(name, shape, dt))

    def count(self, name):
        c = Count(self.stack.enter_context(self.nc.semaphore(name)))
        self.counts.append(c)
        return c

    def pool_count(self, name):
        return PoolCount(self.stack.enter_context(self.nc.semaphore(name)))

    def start(self):
        with self.nc.Block() as block:
            @block.sync
            def _(sp):
                for c in self.counts:
                    c.start(sp)

    def tick(self, name):
        return self.stack.enter_context(self.nc.semaphore(name))


def f(ap):
    return ap.bitcast(F32)


class RowEnds:

    STEPS = 2

    def __init__(self, m, t):
        self.m = m
        self.x = t["x"].rearrange("(b j p) d -> b j p d", p=P, j=J)
        self.xn = t["xn"].rearrange("(b j p) d -> b j p d", p=P, j=J)
        self.out = t["out"].rearrange("(b j p) d -> b j p d", p=P, j=J)
        self.x_rows = [m.sb(f"x_tail{i}", [P, D]) for i in range(2)]
        self.xn_rows = [m.sb(f"xn_tail{j}", [P, D]) for j in range(J)]
        self.res = [m.sb(f"res{j}", [P, D]) for j in range(J)]
        self.gamma = m.sb("ln_g", [P, D])
        self.beta = m.sb("ln_b", [P, D])
        self.stats = m.sb("stats", [P, J, 6])
        self.mv = m.sb("mv", [P, J, 2])
        self.std = m.sb("std", [P, J])
        self.rstd = m.sb("rstd", [P, J])
        self.half = m.sb("half", [P, 1])
        self.c_nt = [m.count(f"m_nt{j}") for j in range(J)]
        self.c_xt = [m.count(f"m_xt{i}") for i in range(2)]
        self.c_st = [m.count(f"m_st{j}") for j in range(J)]
        self.c_o = m.count("m_o")
        self.c_po = m.count("m_po")
        self.c_r = m.count("m_r")
        self.c_bn = m.count("m_bn")
        self.c_mv = m.count("m_mv")
        self.c_eps = m.count("m_eps")
        self.c_rs = m.count("m_rs")
        self.c_g = m.count("m_g")
        self.c_nm = m.count("m_nm")
        self.c_fin = m.count("m_fin")
        self.p_tick = m.tick("m_ptick")
        self.d_tick = m.tick("m_dtick")

    def banks(self):
        self.po = [self.m.ps(f"po{j}", [P, D]) for j in range(J)]

    def load_x(self, sp, b, j, reused=True):
        if reused:
            self.c_fin.wait(sp, self.STEPS * (b * J + j - 1))
        sp.dma_start(self.x_rows[j % 2][:, :], self.x[b, j]).then_inc(self.c_xt[j % 2].sem, 16)

    def load_xn(self, sp, b):
        self.c_fin.wait(sp, self.STEPS * J * b)
        for j in range(J):
            sp.dma_start(self.xn_rows[j][:, :], self.xn[b, j][:, 0:D]).then_inc(self.c_nt[j].sem, 16)

    def store_and_load(self, sp, b, more):
        for j in range(J):
            self.c_fin.wait(sp, self.STEPS * (b * J + j + 1))
            sp.dma_start(self.out[b, j], self.res[j][:, :]).then_inc(self.c_st[j].sem, 16)
            if j < 2:
                self.load_x(sp, b, j + 2)
            elif more:
                self.load_x(sp, b + 1, j - 2)
        if more:
            self.load_xn(sp, b + 1)

    def rows_out(self, act, b, j):
        self.c_o.wait(act, (b + 1) * NC_)
        self.c_st[j].wait(act, 16 * b)
        act.copy(self.res[j][:, :], self.po[j][:, :]).then_inc(self.c_po.sem, 1)

    def add_xn(self, pool, b, j):
        self.c_po.wait(pool, b * J + j + 1)
        self.c_nt[j].wait(pool, 16 * (b + 1))
        pool.tensor_tensor(self.res[j][:, :], self.res[j][:, :], self.xn_rows[j][:, :],
                           ALU.add).then_inc(self.c_r.sem, 1)

    def inverse_std(self, pool, b, j):
        n = b * J + j
        self.c_mv.wait(pool, n + 1)
        self.c_rs.wait(pool, n)
        pool.sem_inc(self.p_tick, 1)
        pool.tensor_scalar(self.std[:, j:j + 1], self.mv[:, j, 1:2], EPS, None, ALU.add).then_inc(self.c_eps.sem, 1)
        self.c_eps.wait(pool, n + 1)
        pool.tensor_tensor(self.rstd[:, j:j + 1], self.std[:, j:j + 1], self.half[:, :],
                           ALU.pow).then_inc(self.c_rs.sem, 1)

    def finish(self, pool, b, j, q):
        n = b * J + j
        if q == 0:
            self.c_nm.wait(pool, n + 1)
        else:
            self.c_xt[j % 2].wait(pool, 16 * (b * (J // 2) + j // 2 + 1))
        self.c_fin.wait(pool, self.STEPS * n + q)
        pool.tensor_tensor(self.res[j][:, :], self.res[j][:, :], (self.xn_rows[j], self.x_rows[j % 2])[q][:, :],
                           ALU.add).then_inc(self.c_fin.sem, 1)

    def statistics(self, dve, b, j):
        n = b * J + j
        self.c_r.wait(dve, n + 1)
        self.c_mv.wait(dve, b * J)
        dve.bn_stats(self.stats[:, j, :], self.res[j][:, :]).then_inc(self.c_bn.sem, 1)
        self.c_bn.wait(dve, n + 1)
        self.c_rs.wait(dve, b * J)
        self.c_nm.wait(dve, b * J)
        dve.sem_inc(self.d_tick, 1)
        dve.bn_aggr(self.mv[:, j, :], self.stats[:, j, :]).then_inc(self.c_mv.sem, 1)

    def norm(self, dve, b, j):
        n = b * J + j
        self.c_rs.wait(dve, n + 1)
        self.c_mv.wait(dve, n + 1)
        self.c_g.wait(dve, n)
        dve.scalar_tensor_tensor(out=self.res[j][:, :], in0=self.res[j][:, :], scalar=self.mv[:, j, 0:1],
                                 in1=self.gamma[:, :], op0=ALU.subtract, op1=ALU.mult).then_inc(self.c_g.sem, 1)
        self.c_g.wait(dve, n + 1)
        dve.scalar_tensor_tensor(out=self.res[j][:, :], in0=self.res[j][:, :], scalar=self.rstd[:, j:j + 1],
                                 in1=self.beta[:, :], op0=ALU.mult, op1=ALU.add).then_inc(self.c_nm.sem, 1)


class MixerWeights:

    def __init__(self, m):
        self.w_in = m.sb("w_in", [P, NW, KD * P])
        self.wout_h = m.sb("wout_h", [P, NC_, D], F32R)
        self.wout_l = m.sb("wout_l", [P, NC_, D], F32R)
        self.wb = m.sb("wb", [P, NC_, 2 * S], F32R)
        self.wc_h = m.sb("wc_h", [P, C], F32R)
        self.wc_l = m.sb("wc_l", [P, C], F32R)
        self.cw = m.sb("cw", [P, NC_, 4])
        self.cb = m.sb("cb", [P, NC_])
        self.dp = m.sb("dp", [P, NC_])


def stage_gate(nc, t, gates, ident, w, ends):
    R = 4
    NG = NB // R
    with ExitStack() as stack:
        m = Mem(nc, stack)
        xt = [m.sb(f"g_x{i}", [P, J, D]) for i in range(R)]
        ext = [m.sb(f"g_ext{i}", [P, J, XW]) for i in range(R)]
        stats = m.sb("g_stats", [P, J, 6])
        mv = [m.sb(f"g_mv{i}", [P, J, 2]) for i in range(2)]
        std = m.sb("g_std", [P, J])
        rstd = [m.sb(f"g_rstd{i}", [P, J]) for i in range(2)]
        half = m.sb("g_half", [P, J])
        xnt = [m.sb(f"g_xnt{k}", [P, TB]) for k in range(KD)]
        sc_t = m.sb("g_sc_t", [E, TB])
        staged = m.sb("g_staged", [P, NC_, TB])
        staged2 = m.sb("g_staged2", [P, 4, TB])
        tanh = m.sb("g_tanh", [P, J * E])
        gw = m.sb("g_gw", [P, KD, E])
        pt = [m.ps(f"g_pt{k}", [P, TB]) for k in range(KD)]
        pst = m.ps("g_pst", [E, TB])
        psc = m.ps("g_psc", [P, J * E])

        c_id = m.count("g_id")
        c_gw = m.count("g_gw_in")
        c_x = [m.count(f"g_x_in{i}") for i in range(R)]
        c_st = [m.count(f"g_out{i}") for i in range(R)]
        c_bn = m.count("g_bn")
        c_mv = m.count("g_mv_set")
        c_eps = m.count("g_eps")
        c_rs = m.count("g_rs")
        c_xn = m.count("g_xn")
        c_t = m.count("g_t")
        c_tc = m.count("g_tc")
        c_se = m.count("g_se")
        c_sr = m.count("g_sr")
        c_sc = m.count("g_sc")
        c_win = m.count("g_win")
        c_in = m.count("g_infac")
        c_sh = m.count("g_sh")
        c_sl = m.count("g_sl")
        c_th = m.count("g_th")
        c_v = m.count("g_v")
        d_tick = m.tick("g_dtick")
        p_tick = m.tick("g_ptick")
        t_tick = m.tick("g_ttick")

        x_v = t["x"].rearrange("(b j p) d -> b p j d", p=P, j=J)
        xn_v = t["xn"].rearrange("(b j p) d -> b p j d", p=P, j=J)

        m.start()
        with nc.Block() as block:
            @block.sync
            def _(sp):
                def store(b, i):
                    c_v.wait(sp, b * 2 + 1)
                    sp.dma_start(xn_v[b], ext[i][:, :, :]).then_inc(c_st[i].sem, 16)

                def groups(first, end):
                    with sp.Fori(first, end) as h:
                        for i in range(R):
                            b = h * R + i
                            c_xn.wait(sp, (b + 1) * J)
                            sp.dma_start(xt[i][:, :, :], x_v[b + R]).then_inc(c_x[i].sem, 16)
                            store(b, i)

                sp.dma_start(xt[0][:, :, :], x_v[0]).then_inc(c_x[0].sem, 16)
                sp.dma_start(gw[:, :, :], t["gate_w"]).then_inc(c_gw.sem, 16)
                for i in range(1, R):
                    sp.dma_start(xt[i][:, :, :], x_v[i]).then_inc(c_x[i].sem, 16)
                groups(0, 1)
                sp.dma_start(staged[:, :, :], t["w_out"]).then_inc(c_win.sem, 16)
                sp.dma_start(staged2[0:S, 0:2, :], t["w_c"]).then_inc(c_win.sem, 16)
                sp.dma_start(staged2[S:P, 0:2, :], t["w_c"]).then_inc(c_win.sem, 16)
                sp.dma_start(staged2[:, 2, :], t["w_b"]).then_inc(c_win.sem, 16)
                groups(1, NG - 1)
                sp.dma_start(w.w_in[:, :, :], t["w_in"]).then_inc(c_win.sem, 16)
                sp.dma_start(w.cw[:, :, :], t["conv_w"]).then_inc(c_win.sem, 16)
                sp.dma_start(w.cb[:, :], t["conv_b"]).then_inc(c_win.sem, 16)
                sp.dma_start(w.dp[:, :], t["d_param"]).then_inc(c_win.sem, 16)
                sp.dma_start(ends.gamma[:, :], t["ln_g"].to_broadcast([P, D])).then_inc(c_win.sem, 16)
                sp.dma_start(ends.beta[:, :], t["ln_b"].to_broadcast([P, D])).then_inc(c_win.sem, 16)
                for i in range(R):
                    store(NB - R + i, i)
                c_win.wait(sp, 16 * 10)
                for i in range(R):
                    c_st[i].wait(sp, 16 * NG)

            @block.gpsimd
            def _(pool):
                c_id.wait(pool, 0)
                pool.memset(ident[:, :], 0.0).then_inc(c_id.sem, 1)
                pool.memset(half[:, :], -0.5).then_inc(c_id.sem, 1)
                c_id.wait(pool, 2)
                pool.affine_select(out=ident[:, :], in_=ident[:, :], compare_op=ALU.not_equal, fill=1.0,
                                   base=0, pattern=[[-1, P]], channel_multiplier=1).then_inc(c_id.sem, 1)
                with pool.Fori(0, NB // 2) as h:
                    for i in range(2):
                        b = h * 2 + i
                        c_mv.wait(pool, (b + 1) * J)
                        c_rs.wait(pool, b)
                        pool.sem_inc(p_tick, 1)
                        pool.tensor_scalar(std[:, :], mv[i][:, :, 1], EPS, None, ALU.add).then_inc(c_eps.sem, 1)
                        c_eps.wait(pool, b + 1)
                        pool.tensor_tensor(rstd[i][:, :], std[:, :], half[:, :], ALU.pow).then_inc(c_rs.sem, 1)

            @block.vector
            def _(dve):
                def statistics(b, h, i):
                    c_x[i].wait(dve, h * 16 + 16)
                    c_mv.wait(dve, b * J)
                    for j in range(J):
                        dve.bn_stats(stats[:, j, :], xt[i][:, j, :]).then_inc(c_bn.sem, 1)
                    c_bn.wait(dve, (b + 1) * J)
                    c_rs.wait(dve, b)
                    c_xn.wait(dve, b * J)
                    dve.sem_inc(d_tick, 1)
                    for j in range(J):
                        dve.bn_aggr(mv[i % 2][:, j, :], stats[:, j, :]).then_inc(c_mv.sem, 1)

                def normalise(b, h, i):
                    c_rs.wait(dve, b + 1)
                    c_mv.wait(dve, (b + 1) * J)
                    c_st[i].wait(dve, h * 16)
                    for j in range(J):
                        dve.tensor_scalar(ext[i][:, j, 0:D], xt[i][:, j, :], mv[i % 2][:, j, 0:1],
                                          rstd[i % 2][:, j:j + 1], ALU.subtract, ALU.mult).then_inc(c_xn.sem, 1)

                def gate_values(b, i):
                    c_th.wait(dve, b + 1)
                    half_tanh = tanh[:, :].rearrange("p (j e) -> p j e", e=E)
                    dve.tensor_scalar(ext[i][:, :, D:XW], half_tanh, 1.0, 0.5,
                                      ALU.add, ALU.mult).then_inc(c_v.sem, 1)
                    dve.tensor_scalar(gates[:, :, bass.ds(b * J, J)], tanh[:, :].rearrange("p (j e) -> p e j", e=E),
                                      1.0, 0.5, ALU.add, ALU.mult).then_inc(c_v.sem, 1)

                def low_parts():
                    c_win.wait(dve, 64)
                    dve.tensor_scalar(staged2[:, 3, :], staged2[:, 2, :], INPUT_FACTOR, None,
                                      ALU.mult).then_inc(c_in.sem, 1)
                    c_sh.wait(dve, 1)
                    dve.tensor_tensor(w.wout_l[:, :, :], staged[:, :, :], f(w.wout_h[:, :, :]),
                                      ALU.subtract).then_inc(c_sl.sem, 1)
                    c_sh.wait(dve, 2)
                    dve.tensor_tensor(w.wc_l[:, :], staged2[:, 0:2, :].rearrange("p a b -> p (a b)"),
                                      f(w.wc_h[:, :]), ALU.subtract).then_inc(c_sl.sem, 1)
                    c_sh.wait(dve, 3)
                    dve.tensor_tensor(w.wb[:, :, S:2 * S], staged2[:, 3, :].rearrange("p (c s) -> p c s", s=S),
                                      f(w.wb[:, :, 0:S]), ALU.subtract).then_inc(c_sl.sem, 1)

                def group(h, first=False, last=False):
                    for i in range(R):
                        b = h * R + i
                        normalise(b, h, i)
                        if not (last and i == R - 1):
                            statistics(b + 1, h + 1 if i == R - 1 else h, (i + 1) % R)
                        if not (first and i == 0):
                            gate_values(b - 1, (i - 1) % R)

                statistics(0, 0, 0)
                group(0, first=True)
                with dve.Fori(1, NG - 1) as h:
                    group(h)
                low_parts()
                group(NG - 1, last=True)
                gate_values(NB - 1, R - 1)

            @block.tensor
            def _(pe):
                def turn_scores(b):
                    c_sr.wait(pe, b + 1)
                    c_th.wait(pe, b)
                    pe.sem_inc(t_tick, 1)
                    for j in range(J):
                        last = pe.transpose(psc[:, j * E:(j + 1) * E], sc_t[:, j * P:(j + 1) * P],
                                            ident[0:E, 0:E])
                    last.then_inc(c_sc.sem, 1)

                def group(h, first=False):
                    for i in range(R):
                        b = h * R + i
                        for k in range(KD):
                            c_tc.wait(pe, (b - 1) * KD + k + 1 if not (first and i == 0) else 0)
                            for j in range(J):
                                if k == 0:
                                    c_xn.wait(pe, b * J + j + 1)
                                last = pe.transpose(pt[k][:, j * P:(j + 1) * P],
                                                    ext[i][:, j, k * P:(k + 1) * P], ident[:, :])
                            last.then_inc(c_t.sem, 1)
                        if not (first and i == 0):
                            turn_scores(b - 1)
                        c_sr.wait(pe, b)
                        for k in range(KD):
                            c_tc.wait(pe, b * KD + k + 1)
                            pe.matmul(pst[:, :], gw[:, k, :], xnt[k][:, :], start=(k == 0),
                                      stop=(k == KD - 1)).then_inc(c_se.sem, 1)

                c_id.wait(pe, 3)
                c_gw.wait(pe, 16)
                group(0, first=True)
                with pe.Fori(1, NG) as h:
                    group(h)
                turn_scores(NB - 1)

            @block.scalar
            def _(act):
                def high_parts():
                    c_win.wait(act, 64)
                    act.copy(w.wout_h[:, :, :], staged[:, :, :]).then_inc(c_sh.sem, 1)
                    act.copy(w.wc_h[:, :], staged2[:, 0:2, :].rearrange("p a b -> p (a b)")).then_inc(c_sh.sem, 1)
                    c_in.wait(act, 1)
                    act.copy(w.wb[:, :, 0:S], staged2[:, 3, :].rearrange("p (c s) -> p c s", s=S)).then_inc(c_sh.sem, 1)

                def turn_tanh(b):
                    c_sc.wait(act, b + 1)
                    c_v.wait(act, b * 2)
                    act.activation(tanh[:, :], psc[:, :], ACT.Tanh).then_inc(c_th.sem, 1)

                def group(h, first=False):
                    for i in range(R):
                        b = h * R + i
                        for k in range(KD):
                            c_t.wait(act, b * KD + k + 1)
                            c_se.wait(act, (b - 1) * KD + k + 1 if not (first and i == 0) else 0)
                            act.copy(xnt[k][:, :], pt[k][:, :]).then_inc(c_tc.sem, 1)
                        if not (first and i == 0):
                            turn_tanh(b - 1)
                        c_se.wait(act, (b + 1) * KD)
                        c_sc.wait(act, b)
                        act.copy(sc_t[:, :], pst[:, :]).then_inc(c_sr.sem, 1)

                group(0, first=True)
                with act.Fori(1, NG - 1) as h:
                    group(h)
                high_parts()
                group(NG - 1)
                turn_tanh(NB - 1)


BIS = 5
BIS_PER_TURN = 2
assert BIS_PER_TURN * NB >= 26


def count_at_or_above(dve, gates, bis, c_cand, c_cnt, n):
    thr, step, cand, ge, cnt, tot = bis
    c_cand.wait(dve, BIS * n + 1)
    c_cnt.wait(dve, 2 * n)
    dve.tensor_tensor(ge[:, :, :], gates[:, :, :],
                      cand[:, :].rearrange("p (e o) -> p e o", o=1).to_broadcast([P, E, NT]),
                      ALU.is_ge).then_inc(c_cnt.sem, 1)
    c_cnt.wait(dve, 2 * n + 1)
    dve.tensor_reduce(cnt[:, :], ge[:, :, :], AX.X, ALU.add).then_inc(c_cnt.sem, 1)


def halve(pool, bis, c_cand, c_cnt, n, hold):
    thr, step, cand, ge, cnt, tot = bis
    c_cnt.wait(pool, 2 * n + 2)
    c_cand.wait(pool, BIS * n + 1)
    hold()
    pool.partition_all_reduce(tot[:, :], cnt[:, :], P, RADD).then_inc(c_cand.sem, 1)
    c_cand.wait(pool, BIS * n + 2)
    hold()
    pool.tensor_scalar(tot[:, :], tot[:, :], float(CAP), step[:, 0:1], ALU.is_ge, ALU.mult).then_inc(c_cand.sem, 1)
    c_cand.wait(pool, BIS * n + 3)
    pool.tensor_tensor(thr[:, :], thr[:, :], tot[:, :], ALU.add).then_inc(c_cand.sem, 1)
    hold()
    pool.tensor_scalar(step[:, :], step[:, :], 0.5, None, ALU.mult).then_inc(c_cand.sem, 1)
    c_cand.wait(pool, BIS * n + 5)
    hold()
    pool.tensor_scalar(cand[:, :], thr[:, :], step[:, 0:1], None, ALU.add).then_inc(c_cand.sem, 1)


def stage_mixer(nc, t, gates, thr, ident, w, ends):
    LATE = 2
    TAPS = 3
    with ExitStack() as stack:
        m = Mem(nc, stack)
        wh = [m.sb(f"wh{i}", [P, KD * P], F32R) for i in range(4)]
        wl = [m.sb(f"wl{i}", [P, KD * P], F32R) for i in range(4)]
        xt_h = m.sb("xt_h", [P, KD, TB], F32R)
        xt_l = m.sb("xt_l", [P, KD, TB], F32R)
        rows = m.sb("xn_next", [P, J, D])
        u = m.sb("u", [P, NC_, TB])
        u_h = [m.sb(f"u_h{i}", [P, TB], F32R) for i in range(2)]
        u_l = [m.sb(f"u_l{i}", [P, TB], F32R) for i in range(2)]
        y_h = [m.sb(f"y_h{i}", [P, TB], F32R) for i in range(3)]
        y_l = [m.sb(f"y_l{i}", [P, TB], F32R) for i in range(3)]
        sg = m.sb("sg", [P, NC_, TB])
        xin = [m.sb(f"xin{i}", [P, 3 + TB]) for i in range(2)]
        halo = m.sb("halo", [P, NC_, 3])
        h = m.sb("h", [P, TB])
        h_h = m.sb("h_h", [P, TB], F32R)
        h_l = m.sb("h_l", [P, TB], F32R)
        carry = m.sb("carry", [P, 1])
        decay = m.sb("decay", [P, 1])
        step = m.sb("bis_step", [P, 1])
        cand = m.sb("bis_cand", [P, E])
        ge = m.sb("bis_ge", [P, E, NT], BF16)
        cnt = m.sb("bis_cnt", [P, E])
        tot = m.sb("bis_tot", [P, E])
        bis = (thr, step, cand, ge, cnt, tot)
        ring = [m.ps(f"ring{i}", [P, TB]) for i in range(2)]
        pb = m.ps("pb", [P, TB])
        pcb = [m.ps("pc", [P, TB]), pb]
        po, c_o, c_po = ends.po, ends.c_o, ends.c_po
        p_tick, d_tick = ends.p_tick, ends.d_tick

        c_rows = m.count("m_rows")
        c_set = m.count("m_set")
        c_wh = m.count("m_wh")
        c_wl = m.count("m_wl")
        c_ag = m.count("m_ag")
        c_x = m.count("m_x")
        c_ev = m.count("m_ev")
        c_halo = m.count("m_halo")
        c_cv = m.count("m_cv")
        c_u = m.count("m_u")
        c_uh = m.count("m_uh")
        c_ul = m.count("m_ul")
        c_b = m.count("m_b")
        c_h = m.count("m_h")
        c_car = m.count("m_car")
        c_hh = m.count("m_hh")
        c_hl = m.count("m_hl")
        c_c = m.count("m_c")
        c_y1 = m.count("m_y1")
        c_y2 = m.count("m_y2")
        c_yh = m.count("m_yh")
        c_yl = m.count("m_yl")
        c_t = m.count("m_t")
        c_th = m.count("m_th")
        c_tl = m.count("m_tl")
        c_cand = m.count("m_cand")
        c_cnt = m.count("m_cnt")
        z = m.count("m_zero")

        xn_v = t["xn"].rearrange("(b j p) d -> b j p d", p=P, j=J)

        def column(s):
            s %= NW
            return (NC_, 0)[s] if s < 2 else s // 2 + NC_ * (s % 2)

        def a_step(c):
            return 2 * c if c else 1

        def g_step(c):
            return 2 * c + 1 if c else 0

        m.start()
        with nc.Block() as block:
            @block.sync
            def _(sp):
                def load_rows(b):
                    sp.dma_start(rows[:, :, :], xn_v[b].rearrange("j p d -> p j d")[:, :, 0:D]).then_inc(c_rows.sem, 16)

                load_rows(0)
                c_t.wait(sp, KD)
                load_rows(1)
                ends.load_x(sp, 0, 0, False)
                ends.load_x(sp, 0, 1, False)
                ends.load_xn(sp, 0)
                c_t.wait(sp, 2 * KD)
                load_rows(2)
                with sp.Fori(2, NB - 1) as b:
                    c_t.wait(sp, (b + 1) * KD)
                    load_rows(b + 1)
                    ends.store_and_load(sp, b - 2, True)
                c_t.wait(sp, NB * KD)
                load_rows(0)
                ends.store_and_load(sp, NB - 3, True)

            @block.gpsimd
            def _(pool):
                def hold():
                    pool.sem_inc(p_tick, 1)

                pool.memset(ends.half[:, :], -0.5).then_inc(c_set.sem, 1)
                pool.memset(decay[:, :], DECAY).then_inc(c_set.sem, 1)
                pool.memset(thr[:, :], 0.0).then_inc(c_set.sem, 1)
                pool.memset(step[:, :], 1.0).then_inc(c_set.sem, 1)
                c_set.wait(pool, 4)
                pool.tensor_scalar(cand[:, :], thr[:, :], step[:, 0:1], None, ALU.add).then_inc(c_cand.sem, 1)

                def w_low(n, s):
                    c_wh.wait(pool, n + 1)
                    pool.tensor_tensor(wl[s % 4][:, :], w.w_in[:, column(s), :], f(wh[s % 4][:, :]),
                                       ALU.subtract).then_inc(c_wl.sem, 1)

                def turn(b, with_last, with_end):
                    for s in range(NW):
                        w_low(b * NW + s + 3, s + 3)
                        if with_end and s in (2, 4, 6, 8):
                            ends.inverse_std(pool, b - 2, s // 2 - 1)
                        if with_end and s in range(4, 4 + 2 * J):
                            ends.finish(pool, b - 2, s // 2 - 2, s % 2)
                    if with_last:
                        for j in range(J):
                            ends.add_xn(pool, b - 1, j)
                    for q in range(BIS_PER_TURN):
                        halve(pool, bis, c_cand, c_cnt, b * BIS_PER_TURN + q, hold)

                for s in range(3):
                    w_low(s, s)
                turn(0, False, False)
                turn(1, True, False)
                with pool.Fori(2, NB) as b:
                    turn(b, True, True)

            @block.scalar
            def _(act):
                def w_high(n, s):
                    act.copy(wh[s % 4][:, :], w.w_in[:, column(s), :]).then_inc(c_wh.sem, 1)

                def t_high(n, k):
                    c_t.wait(act, n + 1)
                    act.copy(xt_h[:, k, :], ring[k % 2][:, :]).then_inc(c_th.sem, 1)

                def u_pair(b, c):
                    n = b * NC_ + c
                    c_cv.wait(act, TAPS * (n + 1))
                    act.activation(u[:, c, :], u[:, c, :], ACT.Silu).then_inc(c_u.sem, 1)
                    c_u.wait(act, n + 1)
                    c_b.wait(act, b * NC_ if c < 2 else n - 1)
                    c_ul.wait(act, b * NC_ if c < 2 else n - 1)
                    act.copy(u_h[c % 2][:, :], u[:, c, :]).then_inc(c_uh.sem, 1)

                def y_high(b, c):
                    n = b * NC_ + c
                    c_o.wait(act, b * NC_ if c < 3 else n - 2)
                    c_yl.wait(act, b * NC_ if c < 3 else n - 2)
                    c_y2.wait(act, n + 1)
                    act.copy(y_h[c % 3][:, :], u[:, c, :]).then_inc(c_yh.sem, 1)

                for s in range(3):
                    w_high(s, s)
                for k in range(KD):
                    t_high(k, k)

                def turn(b, with_last):
                    for s in range(NW):
                        n, c = b * NW + s, s // 2
                        c_ag.wait(act, n)
                        c_wl.wait(act, n)
                        w_high(n + 3, s + 3)
                        if s == 2:
                            u_pair(b, 0)
                        if s == a_step(c):
                            c_cv.wait(act, b * (TAPS * NC_) + (TAPS * (c - 1) if c > 1 else 0))
                            c_halo.wait(act, b * (2 * NC_) + (2 * (c - 1) if c > 1 else 0))
                            c_ag.wait(act, n + 1)
                            act.copy(xin[c % 2][:, 3:3 + TB], ring[s % 2][:, :]).then_inc(c_x.sem, 1)
                            c_yl.wait(act, b * NC_)
                            act.activation(u[:, c, :], ring[s % 2][:, :], ACT.Identity, bias=w.cb[:, c:c + 1],
                                           scale=w.cw[:, c, 3:4]).then_inc(c_ev.sem, 1)
                        else:
                            c_y2.wait(act, b * NC_)
                            c_ag.wait(act, n + 1)
                            act.activation(sg[:, c, :], ring[s % 2][:, :], ACT.Silu).then_inc(c_ev.sem, 1)
                            if c:
                                u_pair(b, c)
                    t_high((b + 1) * KD, 0)
                    t_high((b + 1) * KD + 1, 1)
                    c_c.wait(act, b * NC_)
                    c_hl.wait(act, b)
                    c_h.wait(act, b + 1)
                    act.copy(h_h[:, :], h[:, :]).then_inc(c_hh.sem, 1)
                    if with_last:
                        ends.rows_out(act, b - 1, 0)
                    t_high((b + 1) * KD + 2, 2)
                    if with_last:
                        ends.rows_out(act, b - 1, 1)
                        ends.rows_out(act, b - 1, 2)
                        ends.rows_out(act, b - 1, 3)
                    y_high(b, 0)
                    t_high((b + 1) * KD + 3, 3)
                    for c in range(1, NC_):
                        y_high(b, c)

                turn(0, False)
                with act.Fori(1, NB) as b:
                    turn(b, True)

            @block.vector
            def _(dve):
                c_set.wait(dve, 4)

                def t_low(n, k):
                    c_th.wait(dve, n + 1)
                    dve.tensor_tensor(xt_l[:, k, :], ring[k % 2][:, :], f(xt_h[:, k, :]),
                                      ALU.subtract).then_inc(c_tl.sem, 1)

                def u_low(b, c):
                    c_uh.wait(dve, b * NC_ + c + 1)
                    dve.tensor_tensor(u_l[c % 2][:, :], u[:, c, :], f(u_h[c % 2][:, :]),
                                      ALU.subtract).then_inc(c_ul.sem, 1)

                def conv(b, c):
                    n = b * NC_ + c
                    x_ = xin[c % 2]
                    c_halo.wait(dve, 2 * n)
                    c_cv.wait(dve, TAPS * (b * NC_ if c < 2 else n - 1))
                    dve.tensor_copy(x_[:, 0:3], halo[:, c, :]).then_inc(c_halo.sem, 1)
                    c_x.wait(dve, n + 1)
                    c_halo.wait(dve, 2 * n + 1)
                    dve.tensor_copy(halo[:, c, :], x_[:, TB:TB + 3]).then_inc(c_halo.sem, 1)
                    c_ev.wait(dve, b * NW + a_step(c) + 1)
                    for q in range(1, TAPS + 1):
                        c_cv.wait(dve, TAPS * n + q - 1)
                        dve.scalar_tensor_tensor(out=u[:, c, :], in0=x_[:, 3 - q:3 - q + TB],
                                                 scalar=w.cw[:, c, 3 - q:4 - q], in1=u[:, c, :],
                                                 op0=ALU.mult, op1=ALU.add).then_inc(c_cv.sem, 1)

                def scan(b):
                    c_b.wait(dve, (b + 1) * NC_)
                    c_hh.wait(dve, b)
                    c_hl.wait(dve, b)
                    c_car.wait(dve, b)
                    dve.tensor_tensor_scan(h[:, :], decay[:, 0:1].to_broadcast([P, TB]), pb[:, :], carry[:, 0:1],
                                           ALU.mult, ALU.add).then_inc(c_h.sem, 1)
                    c_h.wait(dve, b + 1)
                    dve.tensor_copy(carry[:, :], h[:, TB - 1:TB]).then_inc(c_car.sem, 1)

                def h_low(b):
                    c_hh.wait(dve, b + 1)
                    dve.tensor_tensor(h_l[:, :], h[:, :], f(h_h[:, :]), ALU.subtract).then_inc(c_hl.sem, 1)

                def y_turn(b, c):
                    n = b * NC_ + c
                    c_c.wait(dve, n + 1)
                    dve.scalar_tensor_tensor(out=u[:, c, :], in0=u[:, c, :], scalar=w.dp[:, c:c + 1],
                                             in1=pcb[c % 2][:, :], op0=ALU.mult, op1=ALU.add).then_inc(c_y1.sem, 1)
                    c_ev.wait(dve, b * NW + g_step(c) + 1)
                    c_y1.wait(dve, n + 1)
                    dve.tensor_tensor(u[:, c, :], u[:, c, :], sg[:, c, :], ALU.mult).then_inc(c_y2.sem, 1)

                def y_low(b, c):
                    c_yh.wait(dve, b * NC_ + c + 1)
                    dve.tensor_tensor(y_l[c % 3][:, :], u[:, c, :], f(y_h[c % 3][:, :]),
                                      ALU.subtract).then_inc(c_yl.sem, 1)

                def turn(b, with_end):
                    for c in range(NC_):
                        conv(b, c)
                        if with_end and c < J:
                            ends.statistics(dve, b - 2, c)
                        u_low(b, c)
                        if with_end and 1 <= c <= J:
                            ends.norm(dve, b - 2, c - 1)
                    scan(b)
                    t_low((b + 1) * KD, 0)
                    h_low(b)
                    t_low((b + 1) * KD + 1, 1)
                    for c in range(NC_):
                        y_turn(b, c)
                        if c < 2:
                            t_low((b + 1) * KD + 2 + c, 2 + c)
                        y_low(b, c)
                        if c in (2, 5):
                            count_at_or_above(dve, gates, bis, c_cand, c_cnt, b * BIS_PER_TURN + c // 3)

                def new_sequence(b):
                    c_halo.wait(dve, 2 * NC_ * b)
                    c_car.wait(dve, b)
                    c_h.wait(dve, b)
                    dve.memset(halo[:, :, :], 0.0).then_inc(z.sem, 1)
                    dve.memset(carry[:, :], 0.0).then_inc(z.sem, 1)

                for k in range(KD):
                    t_low(k, k)
                new_sequence(0)
                z.wait(dve, 2)
                turn(0, False)
                turn(1, False)
                with dve.Fori(2, BPS) as b:
                    turn(b, True)
                with dve.Fori(1, NB // BPS) as q:
                    new_sequence(q * BPS)
                    z.wait(dve, 2 * q + 2)
                    dve.sem_inc(d_tick, 1)
                    with dve.Fori(0, BPS) as r:
                        turn(q * BPS + r, True)

            @block.tensor
            def _(pe):
                def three(dst, ah, al, bh, bl, start, stop):
                    pe.matmul(dst, ah, bh, start=start, stop=False)
                    pe.matmul(dst, ah, bl, start=False, stop=False)
                    return pe.matmul(dst, al, bh, start=False, stop=stop)

                def ag(b, s):
                    n = b * NW + s
                    c_wl.wait(pe, n + 1)
                    if s == 0:
                        c_th.wait(pe, (b + 1) * KD)
                        c_tl.wait(pe, (b + 1) * KD)
                    if s > 1:
                        c_ev.wait(pe, n - 1)
                    for k in range(KD):
                        r = slice(k * P, (k + 1) * P)
                        last = three(ring[s % 2][:, :], wh[s % 4][:, r], wl[s % 4][:, r],
                                     xt_h[:, k, :], xt_l[:, k, :], k == 0, k == KD - 1)
                    last.then_inc(c_ag.sem, 1)

                def share_b(b, c):
                    c_ul.wait(pe, b * NC_ + c + 1)
                    if c == 0:
                        c_y1.wait(pe, b * NC_)
                    pe.matmul(pb[:, :], w.wb[:, c, :], u_h[c % 2][:, :], start=(c == 0), stop=False)
                    pe.matmul(pb[:, :], w.wb[:, c, :], u_l[c % 2][:, :], start=False,
                              stop=(c == NC_ - 1)).then_inc(c_b.sem, 1)

                def chan(b, c):
                    r = slice(c * P, (c + 1) * P)
                    if c == 0:
                        c_y1.wait(pe, b * NC_)
                        c_hl.wait(pe, b + 1)
                    elif c > 1:
                        c_y1.wait(pe, b * NC_ + c - 1)
                    three(pcb[c % 2][:, :], w.wc_h[:, r], w.wc_l[:, r], h_h[:, :], h_l[:, :],
                          True, True).then_inc(c_c.sem, 1)

                def out_share(b, c):
                    c_yl.wait(pe, b * NC_ + c + 1)
                    if c == 0:
                        c_po.wait(pe, b * J)
                    for j in range(J):
                        r = slice(j * P, (j + 1) * P)
                        last = three(po[j][:, :], y_h[c % 3][:, r], y_l[c % 3][:, r],
                                     w.wout_h[:, c, :], w.wout_l[:, c, :], c == 0, c == NC_ - 1)
                    last.then_inc(c_o.sem, 1)

                def transposes(k):
                    for j in range(J):
                        last = pe.transpose(ring[k % 2][:, j * P:(j + 1) * P], rows[:, j, k * P:(k + 1) * P],
                                            ident[:, :])
                    last.then_inc(c_t.sem, 1)

                def next_turn(b, k):
                    if k == 0:
                        c_rows.wait(pe, 16 * (b + 2))
                    if k < 2:
                        c_ev.wait(pe, b * NW + NW - 1 + k)
                    else:
                        c_th.wait(pe, (b + 1) * KD + k - 1)
                        c_tl.wait(pe, (b + 1) * KD + k - 1)
                    transposes(k)

                def turn(b, with_last):
                    for s in range(NW):
                        ag(b, s)
                        if s % 2 == 1 and s > 1:
                            share_b(b, s // 2 - 1)
                    if with_last:
                        out_share(b - 1, NC_ - 2)
                    next_turn(b, 0)
                    next_turn(b, 1)
                    share_b(b, NC_ - 1)
                    if with_last:
                        out_share(b - 1, NC_ - 1)
                    chan(b, 0)
                    next_turn(b, 2)
                    chan(b, 1)
                    next_turn(b, 3)
                    for c in range(2, NC_):
                        chan(b, c)
                        out_share(b, c - 2)

                c_rows.wait(pe, 16)
                for k in range(KD):
                    if k >= 2:
                        c_th.wait(pe, k - 1)
                        c_tl.wait(pe, k - 1)
                    transposes(k)
                turn(0, False)
                with pe.Fori(1, NB) as b:
                    turn(b, True)
                for c in range(NC_ - LATE, NC_):
                    out_share(NB - 1, c)


class ExpertWeights:

    def __init__(self, m, t):
        self.m, self.t = m, t
        self.w1 = m.sb("w1r", [P, FT, D])
        self.w2 = m.sb("w2r", [P, FT, D])
        self.b1 = m.sb("b1", [P, (E + 1) * FT])
        self.b2 = m.sb("b2", [P, E, D])
        self.gamma = m.sb("f_ln_g", [P, D])
        self.beta = m.sb("f_ln_b", [P, D])
        self.idx = m.sb("idx", [P, (2 * E + 1) * J], U32)
        self.c_w = [m.count(f"f_w{i}") for i in range(FT)]
        self.c_small = m.count("f_small")
        self.c_idx = m.count("f_idx")
        self.c_ga = [m.pool_count(f"f_ga{j}") for j in range(J)]
        self.c_sc = [m.pool_count(f"f_sc{j}") for j in range(J)]
        self.c_pad = m.count("f_pad")
        self.first = m.sb("f_first", [P, 2 * J, FT])

    def load(self, sp, e, i):
        sp.dma_start(self.w1[:, i, :], self.t["fc1"][e, i]).then_inc(self.c_w[i].sem, 16)
        sp.dma_start(self.w2[:, i, :], self.t["fc2"][e, i]).then_inc(self.c_w[i].sem, 16)

    def prime(self, pool):
        for n, c in enumerate(self.c_ga + self.c_sc):
            c.prime(pool, self.first[:, n, :], self.t["b1"][:, 0:FT])
        pool.memset(self.idx[:, 2 * E * J:(2 * E + 1) * J], 0).then_inc(self.c_pad.sem, 1)
        pool.memset(self.b1[:, E * FT:(E + 1) * FT], 0.0).then_inc(self.c_pad.sem, 1)

    def load_first(self, sp):
        for i in range(2):
            self.load(sp, 0, i)
        for dst, src in ((self.gamma[:, :], self.t["f_ln_g"].to_broadcast([P, D])),
                         (self.beta[:, :], self.t["f_ln_b"].to_broadcast([P, D])),
                         (self.b1[:, 0:E * FT], self.t["b1"]),
                         (self.b2[:, :, :].rearrange("p e d -> p (e d)"), self.t["b2"].to_broadcast([P, E * D]))):
            sp.dma_start(dst, src).then_inc(self.c_small.sem, 16)
        for i in range(2, FT):
            self.load(sp, 0, i)


def stage_lists(nc, gates, thr, slots_d, ends, ew):
    EN = E * NT
    NONE = 4096.0
    EG = P // HI
    NQ = 4
    TQ = NT // NQ
    with ExitStack() as stack:
        m = Mem(nc, stack)
        gt = m.sb("l_gt", [P, EN], BF16)
        eq = m.sb("l_eq", [P, EN], BF16)
        gt_f = m.sb("l_gt_f", [P, EN])
        eq_f = m.sb("l_eq_f", [P, EN])
        before = m.sb("l_before", [P, P], BF16)
        ones = m.sb("l_ones", [P, P], BF16)
        one = m.sb("l_one", [P, 1])
        run_gt = m.sb("l_run_gt", [P, EN])
        run_eq = m.sb("l_run_eq", [P, EN])
        slot = m.sb("l_slot", [P, EN])
        slot_i = m.sb("l_slot_i", [P, EN], U32)
        hi_i = m.sb("l_hi_i", [P, EN], U32)
        lo_i = m.sb("l_lo_i", [P, EN], U32)
        hi = m.sb("l_hi", [P, E, NT], BF16)
        lo = m.sb("l_lo", [P, E, NT], BF16)
        digit = m.sb("l_digit", [P, LO], BF16)
        tile_no = m.sb("l_tile", [P, NT])
        row_no = m.sb("l_row", [P, 1])
        hi1 = [m.sb(f"l_hi1_{i}", [P, TQ, E, HI], BF16) for i in range(2)]
        lo1 = [m.sb(f"l_lo1_{i}", [P, TQ, E, LO], BF16) for i in range(2)]
        lov = [m.sb(f"l_lov_{i}", [P, TQ, E, 2, LO], BF16) for i in range(2)]
        both = m.sb("l_both", [P, E // EG, EG * 2 * LO])
        token_f = m.sb("l_token_f", [P, E // EG, LO])
        token = m.sb("l_token", [P, E // EG, LO], U32)
        p_before = [m.ps(f"l_pb{i}", [P, EN]) for i in range(2)]
        p_all = [m.ps(f"l_pa{i}", [P, EN]) for i in range(2)]
        p_tok = [p[:, 0:EG * 2 * LO] for p in p_before]
        c_set = m.count("l_set")
        c_v = m.count("l_v")
        c_pre = m.count("l_pre")
        c_lo1 = m.count("l_lo1c")
        c_hi1 = m.count("l_hi1c")
        c_row = m.count("l_rowc")
        c_til = m.count("l_tilc")
        c_q = m.count("l_q")
        c_list = m.count("l_list")
        c_out = m.count("l_out")

        def by_expert(ap):
            return ap.rearrange("p (e r) -> p e r", e=E)

        m.counts += ew.m.counts
        m.start()
        with nc.Block() as block:
            @block.sync
            def _(sp):
                ends.store_and_load(sp, NB - 2, True)
                ew.load_first(sp)
                ends.store_and_load(sp, NB - 1, False)
                c_list.wait(sp, 1)
                sp.dma_start(slots_d.rearrange("(g q) l -> q g l", q=P), token[:, :, :]).then_inc(c_out.sem, 16)
                c_out.wait(sp, 16)
                sp.dma_start(ew.idx[:, 0:2 * E * J].rearrange("p (e c) -> p e c", e=E),
                             slots_d.rearrange("(e h) l -> e (h l)", e=E)
                             .rearrange("e (p c) -> p e c", p=P)).then_inc(ew.c_idx.sem, 16)
                for j in range(J):
                    ends.c_st[j].wait(sp, 16 * NB)

            @block.gpsimd
            def _(pool):
                pool.memset(ones[:, :], 1.0).then_inc(c_set.sem, 1)
                pool.memset(one[:, :], 1.0).then_inc(c_set.sem, 1)
                c_set.wait(pool, 1)
                pool.affine_select(out=before[:, :], in_=ones[:, :], compare_op=ALU.is_ge, fill=0.0,
                                   base=-1, pattern=[[1, P]], channel_multiplier=-1).then_inc(c_set.sem, 1)
                pool.iota(digit[:, :], [[1, LO]], base=0, channel_multiplier=0,
                          allow_small_or_imprecise_dtypes=True).then_inc(c_set.sem, 1)
                pool.iota(tile_no[:, :], [[1, NT]], base=0, channel_multiplier=0,
                          allow_small_or_imprecise_dtypes=True).then_inc(c_set.sem, 1)
                pool.iota(row_no[:, :], [[0, 1]], base=0, channel_multiplier=1,
                          allow_small_or_imprecise_dtypes=True).then_inc(c_set.sem, 1)
                for b in (NB - 2, NB - 1):
                    if b == NB - 1:
                        for j in range(J):
                            ends.add_xn(pool, b, j)
                    for j in range(J):
                        ends.inverse_std(pool, b, j)
                    for j in range(J):
                        for q in range(ends.STEPS):
                            ends.finish(pool, b, j, q)
                ew.prime(pool)

            @block.vector
            def _(dve):
                steps = 0

                def done(ins):
                    nonlocal steps
                    ins.then_inc(c_v.sem, 1)
                    steps += 1

                def chained(ins):
                    done(ins)
                    c_v.wait(dve, steps)

                def statistics(b):
                    for j in range(J):
                        ends.statistics(dve, b, j)

                def norm(b):
                    for j in range(J):
                        ends.norm(dve, b, j)

                statistics(NB - 2)
                thr_b = thr[:, :].rearrange("p (e o) -> p e o", o=1).to_broadcast([P, E, NT])
                c_set.wait(dve, 6)
                done(dve.tensor_tensor(by_expert(gt[:, :]), gates[:, :, :], thr_b, ALU.is_gt))
                done(dve.tensor_tensor(by_expert(eq[:, :]), gates[:, :, :], thr_b, ALU.is_equal))
                done(dve.tensor_tensor(by_expert(gt_f[:, :]), gates[:, :, :], thr_b, ALU.is_gt))
                done(dve.tensor_tensor(by_expert(eq_f[:, :]), gates[:, :, :], thr_b, ALU.is_equal))
                norm(NB - 2)
                for i, run in enumerate((run_gt, run_eq)):
                    c_pre.wait(dve, 2 * i + 2)
                    for e in range(E):
                        w = slice(e * NT, (e + 1) * NT)
                        done(dve.tensor_tensor_scan(run[:, w], one[:, 0:1].to_broadcast([P, NT]), p_all[i][:, w],
                                                    0.0, ALU.mult, ALU.add))
                c_v.wait(dve, steps)
                total_gt = by_expert(run_gt[:, :])[:, :, NT - 1:NT].to_broadcast([P, E, NT])
                chained(dve.tensor_tensor(by_expert(run_eq[:, :]), by_expert(run_eq[:, :]), total_gt, ALU.add))
                for i, run in enumerate((run_gt, run_eq)):
                    done(dve.tensor_tensor(run[:, :], run[:, :], p_all[i][:, :], ALU.subtract))
                c_v.wait(dve, steps)
                for i, run in enumerate((run_gt, run_eq)):
                    done(dve.tensor_tensor(run[:, :], run[:, :], p_before[i][:, :], ALU.add))
                c_v.wait(dve, steps)
                for run, mask in ((run_gt, gt_f), (run_eq, eq_f)):
                    done(dve.scalar_tensor_tensor(out=run[:, :], in0=run[:, :], scalar=NONE, in1=mask[:, :],
                                                  op0=ALU.subtract, op1=ALU.mult))
                c_v.wait(dve, steps)
                chained(dve.scalar_tensor_tensor(out=slot[:, :], in0=run_gt[:, :], scalar=NONE, in1=run_eq[:, :],
                                                 op0=ALU.add, op1=ALU.add))
                chained(dve.tensor_copy(slot_i[:, :], slot[:, :]))
                done(dve.tensor_scalar(hi_i[:, :], slot_i[:, :], 5, None, ALU.logical_shift_right))
                chained(dve.tensor_scalar(lo_i[:, :], slot_i[:, :], LO - 1, None, ALU.bitwise_and))
                done(dve.tensor_copy(hi[:, :, :], by_expert(hi_i[:, :])))
                chained(dve.tensor_copy(lo[:, :, :], by_expert(lo_i[:, :])))
                digits = digit[:, :].rearrange("p (a b l) -> p a b l", a=1, b=1).to_broadcast([P, TQ, E, LO])
                for q in range(NQ):
                    def spread(x):
                        tiles = x[:, :, q * TQ:(q + 1) * TQ]
                        return tiles.rearrange("p e (t o) -> p t e o", o=1).to_broadcast([P, TQ, E, LO])

                    c_row.wait(dve, max(q - 1, 0))
                    c_til.wait(dve, max(q - 1, 0) * TQ)
                    c_q.wait(dve, max(q - 1, 0))
                    dve.tensor_tensor(lo1[q % 2][:, :, :, :], spread(lo), digits, ALU.is_equal).then_inc(c_lo1.sem, 1)
                    dve.tensor_tensor(hi1[q % 2][:, :, :, :], spread(hi), digits, ALU.is_equal).then_inc(c_hi1.sem, 1)
                    if q == 1:
                        statistics(NB - 1)
                    if q == 2:
                        norm(NB - 1)
                c_q.wait(dve, NQ)
                for g in range(E // EG):
                    done(dve.tensor_copy(both[:, g, :], p_tok[g]))
                c_v.wait(dve, steps)
                for x in range(EG):
                    q, w = slice(x * HI, (x + 1) * HI), x * 2 * LO
                    done(dve.scalar_tensor_tensor(out=token_f[q, :, :], in0=both[q, :, w + LO:w + 2 * LO],
                                                  scalar=float(P), in1=both[q, :, w:w + LO],
                                                  op0=ALU.mult, op1=ALU.add))
                c_v.wait(dve, steps)
                dve.tensor_copy(token[:, :, :], token_f[:, :, :]).then_inc(c_list.sem, 1)

            @block.scalar
            def _(act):
                for j in range(J):
                    ends.rows_out(act, NB - 1, j)
                for q in range(NQ):
                    c_lo1.wait(act, q + 1)
                    c_q.wait(act, max(q - 1, 0))
                    act.activation(lov[q % 2][:, :, :, 0, :], lo1[q % 2][:, :, :, :], ACT.Copy,
                                   scale=row_no[:, 0:1]).then_inc(c_row.sem, 1)
                    with act.Fori(0, TQ) as r:
                        tile = bass.ds(r, 1)
                        act.activation(lov[q % 2][:, tile, :, 1, :], lo1[q % 2][:, tile, :, :], ACT.Copy,
                                       scale=tile_no[:, bass.ds(r + q * TQ, 1)]).then_inc(c_til.sem, 1)

            @block.tensor
            def _(pe):
                c_set.wait(pe, 3)
                for i, mask in enumerate((gt, eq)):
                    c_v.wait(pe, i + 1)
                    pe.matmul(p_before[i][:, :], before[:, :], mask[:, :], start=True, stop=True).then_inc(c_pre.sem, 1)
                    pe.matmul(p_all[i][:, :], ones[:, :], mask[:, :], start=True, stop=True).then_inc(c_pre.sem, 1)
                for q in range(NQ):
                    c_hi1.wait(pe, q + 1)
                    c_row.wait(pe, q + 1)
                    for r in range(TQ):
                        c_til.wait(pe, q * TQ + r + 1)
                        for g in range(E // EG):
                            ex = slice(g * EG, (g + 1) * EG)
                            last = pe.matmul(p_tok[g], hi1[q % 2][:, r, ex, :].rearrange("p e l -> p (e l)"),
                                             lov[q % 2][:, r, ex, :, :].rearrange("p e v l -> p (e v l)"),
                                             start=(q + r == 0), stop=(q == NQ - 1 and r == TQ - 1))
                    last.then_inc(c_q.sem, 1)


def stage_experts(nc, t, ident, ends, ew):
    G = 2 * E
    T_AT = (9, 11, 13, 14)
    with ExitStack() as stack:
        m = Mem(nc, stack)
        w1h = [m.sb(f"w1h{i}", [P, D], F32R) for i in range(4)]
        w1l = [m.sb(f"w1l{i}", [P, D], F32R) for i in range(4)]
        w2h = [m.sb(f"w2h{i}", [P, D], F32R) for i in range(4)]
        w2l = [m.sb(f"w2l{i}", [P, D], F32R) for i in range(4)]
        yt_h = [m.sb(f"yt_h{i}", [P, KD, TB], F32R) for i in range(2)]
        yt_l = [m.sb(f"yt_l{i}", [P, KD, TB], F32R) for i in range(2)]
        rows = m.sb("rows", [P, J, XW])
        kept = [m.sb(f"kept{i}", [P, J, E]) for i in range(2)]
        hid = [m.sb(f"hid{i}", [P, TB]) for i in range(2)]
        hid_h = [m.sb(f"hid_h{i}", [P, TB], F32R) for i in range(4)]
        hid_l = [m.sb(f"hid_l{i}", [P, TB], F32R) for i in range(4)]
        b1c = [m.sb(f"b1c{i}", [P, FT]) for i in range(2)]
        idx_c = [m.sb(f"idx_c{i}", [P, J], U32) for i in range(2)]
        stats = m.sb("f_stats", [P, J, 6])
        mv = m.sb("f_mv", [P, J, 2])
        std = m.sb("f_std", [P, J])
        rstd = m.sb("f_rstd", [P, J])
        ph = [m.ps(f"ph{i}", [P, TB]) for i in range(2)]
        pt = [m.ps(f"f_pt{i}", [P, TB]) for i in range(2)]

        w1r, w2r, b1, b2, gamma, beta, idx = ew.w1, ew.w2, ew.b1, ew.b2, ew.gamma, ew.beta, ew.idx
        c_w, c_small, c_ga, c_sc, c_pad = ew.c_w, ew.c_small, ew.c_ga, ew.c_sc, ew.c_pad
        res, po = ends.res, ends.po
        c_ix = m.count("f_ix")
        c_kp = m.count("f_kp")
        c_b1 = m.count("f_b1")
        c_bn = m.count("f_bn")
        c_mv = m.count("f_mv")
        c_eps = m.count("f_eps")
        c_rs = m.count("f_rs")
        c_nm = m.count("f_nm")
        c_g = m.count("f_g")
        c_t = m.count("f_t")
        c_th = m.count("f_th")
        c_tl = m.count("f_tl")
        c_wh = m.count("f_wh")
        c_wl = m.count("f_wl")
        c_p1 = m.count("f_p1")
        c_p2 = m.count("f_p2")
        c_ge = m.count("f_ge")
        c_hh = m.count("f_hh")
        c_hl = m.count("f_hl")
        c_bw = m.count("f_bw")
        c_rw = m.count("f_rw")
        p_tick = m.tick("f_ptick")
        d_tick = m.tick("f_dtick")

        m.start()
        with nc.Block() as block:
            @block.sync
            def _(sp):
                with sp.Fori(0, E - 1) as e:
                    for i in range(FT):
                        c_wl.wait(sp, 2 * ((2 * e + 1) * FT + i + 1))
                        ew.load(sp, e + 1, i)
                for i in range(2):
                    c_wl.wait(sp, 2 * ((G - 1) * FT + i + 1))
                    ew.load(sp, 0, i)

            @block.gpsimd
            def _(pool):
                def hold():
                    pool.sem_inc(p_tick, 1)

                c_pad.wait(pool, 2)
                ew.c_idx.wait(pool, 16)

                def gather(g, i, first_turn=False):
                    if not first_turn:
                        for j in range(J):
                            c_sc[j].wait(pool, 16 * (g - 1))
                    hold()
                    pool.tensor_copy(idx_c[i][:, :], idx[:, bass.ds(g * J, J)]).then_inc(c_ix.sem, 1)
                    c_ix.wait(pool, g + 1)
                    c_t.wait(pool, g * KD)
                    c_kp.wait(pool, g)
                    hold()
                    for j in range(J):
                        pool.indirect_dma_start(
                            out=rows[:, j, :], out_offset=None, in_=t["xn"][:, :],
                            in_offset=bass.IndirectOffsetOnAxis(ap=idx_c[i][:, j:j + 1], axis=0),
                        ).then_inc(c_ga[j].sem, 16)

                def inverse_std(g):
                    for j in range(J):
                        n = g * J + j
                        c_mv.wait(pool, n + 1)
                        c_rs.wait(pool, n)
                        hold()
                        pool.tensor_scalar(std[:, j:j + 1], mv[:, j, 1:2], EPS, None, ALU.add).then_inc(c_eps.sem, 1)
                        c_eps.wait(pool, n + 1)
                        pool.tensor_tensor(rstd[:, j:j + 1], std[:, j:j + 1], ends.half[:, :], ALU.pow).then_inc(c_rs.sem, 1)

                def scatter(g, i):
                    for j in range(J):
                        c_sc[j].wait(pool, 16 * g)
                    for j in range(J):
                        c_rw.wait(pool, g * J + j + 1)
                        hold()
                        pool.indirect_dma_start(
                            out=t["out"][:, :], in_=res[j][:, :], in_offset=None, compute_op=ALU.add,
                            out_offset=bass.IndirectOffsetOnAxis(ap=idx_c[i][:, j:j + 1], axis=0),
                        ).then_inc(c_sc[j].sem, 16)

                gather(0, 0, True)
                inverse_std(0)
                with pool.Fori(0, E) as e:
                    for i in range(2):
                        g = 2 * e + i
                        gather(g + 1, 1 - i)
                        inverse_std(g + 1)
                        scatter(g, i)
                for j in range(J):
                    c_sc[j].wait(pool, 16 * G)

            @block.scalar
            def _(act):
                def w_high(n, s):
                    act.copy(w1h[s % 4][:, :], w1r[:, s % FT, :]).then_inc(c_wh.sem, 1)
                    act.copy(w2h[s % 4][:, :], w2r[:, s % FT, :]).then_inc(c_wh.sem, 1)

                def t_high(g, k, i):
                    c_t.wait(act, g * KD + k + 1)
                    act.copy(yt_h[i][:, k, :], pt[k % 2][:, :]).then_inc(c_th.sem, 1)

                for s in range(2):
                    c_w[s].wait(act, 32)
                    w_high(s, s)
                for k in range(KD):
                    t_high(0, k, 0)
                with act.Fori(0, E) as e:
                    for i in range(2):
                        g = 2 * e + i
                        for s in range(FT):
                            n = g * FT + s
                            c_p2.wait(act, g * FT if s < 2 else n - 1)
                            if i == 0 or s + 2 < FT:
                                c_w[(s + 2) % FT].wait(act, e * 32 + 32)
                            else:
                                c_w[(s + 2) % FT].wait(act, e * 32 + 64)
                            w_high(n + 2, s + 2)
                            c_hl.wait(act, g * FT if s < 2 else n - 1)
                            c_b1.wait(act, g + 1)
                            c_p1.wait(act, n + 1)
                            act.activation(hid[s % 2][:, :], ph[s % 2][:, :], ACT.Gelu_apprx_tanh,
                                           bias=b1c[i][:, s:s + 1]).then_inc(c_ge.sem, 1)
                            c_p2.wait(act, g * FT if s < 4 else n - 3)
                            c_ge.wait(act, n + 1)
                            act.copy(hid_h[s % 4][:, :], hid[s % 2][:, :]).then_inc(c_hh.sem, 1)
                            if s - 1 in T_AT:
                                t_high(g + 1, T_AT.index(s - 1), 1 - i)

            @block.vector
            def _(dve):
                def w_low(n, s):
                    for q, (r, h, l) in enumerate(((w1r, w1h, w1l), (w2r, w2h, w2l))):
                        c_wh.wait(dve, 2 * n + q + 1)
                        dve.tensor_tensor(l[s % 4][:, :], r[:, s % FT, :], f(h[s % 4][:, :]),
                                          ALU.subtract).then_inc(c_wl.sem, 1)

                def t_low(g, k, i):
                    c_th.wait(dve, g * KD + k + 1)
                    dve.tensor_tensor(yt_l[i][:, k, :], pt[k % 2][:, :], f(yt_h[i][:, k, :]),
                                      ALU.subtract).then_inc(c_tl.sem, 1)

                def statistics(g, j):
                    n = g * J + j
                    c_ga[j].wait(dve, 16 * (g + 1))
                    c_mv.wait(dve, n)
                    dve.bn_stats(stats[:, j, :], rows[:, j, 0:D]).then_inc(c_bn.sem, 1)
                    c_bn.wait(dve, n + 1)
                    c_nm.wait(dve, g * J)
                    dve.sem_inc(d_tick, 1)
                    dve.bn_aggr(mv[:, j, :], stats[:, j, :]).then_inc(c_mv.sem, 1)

                def normalise(g, j):
                    n = g * J + j
                    c_rs.wait(dve, n + 1)
                    c_mv.wait(dve, n + 1)
                    c_g.wait(dve, n)
                    dve.scalar_tensor_tensor(out=rows[:, j, 0:D], in0=rows[:, j, 0:D], scalar=mv[:, j, 0:1],
                                             in1=gamma[:, :], op0=ALU.subtract, op1=ALU.mult).then_inc(c_g.sem, 1)
                    c_g.wait(dve, n + 1)
                    dve.scalar_tensor_tensor(out=rows[:, j, 0:D], in0=rows[:, j, 0:D], scalar=rstd[:, j:j + 1],
                                             in1=beta[:, :], op0=ALU.mult, op1=ALU.add).then_inc(c_nm.sem, 1)

                def keep(g, e, i, first_turn=False):
                    c_rw.wait(dve, 0 if first_turn else (g - 1) * J)
                    dve.tensor_copy(kept[i][:, :, :], rows[:, :, D:XW]).then_inc(c_kp.sem, 1)
                    c_ge.wait(dve, 0 if first_turn else (g - 1) * FT)
                    dve.sem_inc(d_tick, 1)
                    dve.tensor_copy(b1c[i][:, :], b1[:, bass.ds(e * FT, FT)]).then_inc(c_b1.sem, 1)

                c_small.wait(dve, 16 * 4)
                c_pad.wait(dve, 2)
                for s in range(2):
                    w_low(s, s)
                statistics(0, 0)
                for j in range(1, J):
                    statistics(0, j)
                    normalise(0, j - 1)
                normalise(0, J - 1)
                keep(0, 0, 0, True)
                for k in range(KD):
                    t_low(0, k, 0)
                with dve.Fori(0, E) as e:
                    for i in range(2):
                        g = 2 * e + i
                        for s in range(FT):
                            n = g * FT + s
                            w_low(n + 2, s + 2)
                            if 3 <= s < 3 + J:
                                statistics(g + 1, s - 3)
                            c_hh.wait(dve, n + 1)
                            dve.tensor_tensor(hid_l[s % 4][:, :], hid[s % 2][:, :], f(hid_h[s % 4][:, :]),
                                              ALU.subtract).then_inc(c_hl.sem, 1)
                            if 3 <= s < 3 + J:
                                normalise(g + 1, s - 3)
                            if s == J + 3:
                                keep(g + 1, e + i, 1 - i)
                            if 8 <= s < 8 + J:
                                j = s - 8
                                c_sc[j].wait(dve, 16 * g)
                                c_kp.wait(dve, g + 1)
                                dve.tensor_scalar(res[j][:, :], b2[:, bass.ds(e, 1), :].rearrange("p o d -> p (o d)"),
                                                  kept[i][:, j, bass.ds(e, 1)], None, ALU.mult).then_inc(c_bw.sem, 1)
                            if s - 1 in T_AT:
                                t_low(g + 1, T_AT.index(s - 1), 1 - i)
                        c_p2.wait(dve, (g + 1) * FT)
                        c_bw.wait(dve, (g + 1) * J)
                        for j in range(J):
                            dve.scalar_tensor_tensor(out=res[j][:, :], in0=po[j][:, :],
                                                     scalar=kept[i][:, j, bass.ds(e, 1)], in1=res[j][:, :],
                                                     op0=ALU.mult, op1=ALU.add).then_inc(c_rw.sem, 1)

            @block.tensor
            def _(pe):
                def three(dst, ah, al, bh, bl, start, stop):
                    pe.matmul(dst, ah, bh, start=start, stop=False)
                    pe.matmul(dst, ah, bl, start=False, stop=False)
                    return pe.matmul(dst, al, bh, start=False, stop=stop)

                def trn(g, k):
                    if k == 0:
                        c_nm.wait(pe, J * (g + 1))
                    c_tl.wait(pe, g * KD + (k - 1 if k >= 2 else 0))
                    for j in range(J):
                        last = pe.transpose(pt[k % 2][:, j * P:(j + 1) * P], rows[:, j, k * P:(k + 1) * P],
                                            ident[:, :])
                    last.then_inc(c_t.sem, 1)

                def hidden(g, s, i):
                    n = g * FT + s
                    c_wl.wait(pe, 2 * n + 2)
                    if s == 0:
                        c_tl.wait(pe, (g + 1) * KD)
                    c_ge.wait(pe, g * FT if s < 2 else n - 1)
                    for k in range(KD):
                        w = slice(k * P, (k + 1) * P)
                        last = three(ph[s % 2][:, :], w1h[s % 4][:, w], w1l[s % 4][:, w],
                                     yt_h[i][:, k, :], yt_l[i][:, k, :], k == 0, k == KD - 1)
                    last.then_inc(c_p1.sem, 1)

                def out_share(g, s):
                    c_hl.wait(pe, g * FT + s + 1)
                    if s == 0:
                        c_rw.wait(pe, g * J)
                    for j in range(J):
                        w = slice(j * P, (j + 1) * P)
                        last = three(po[j][:, :], hid_h[s % 4][:, w], hid_l[s % 4][:, w],
                                     w2h[s % 4][:, :], w2l[s % 4][:, :], s == 0, s == FT - 1)
                    last.then_inc(c_p2.sem, 1)

                for k in range(KD):
                    trn(0, k)
                with pe.Fori(0, E) as e:
                    for i in range(2):
                        g = 2 * e + i
                        hidden(g, 0, i)
                        for s in range(1, FT + 1):
                            if s < FT:
                                hidden(g, s, i)
                            out_share(g, s - 1)
                            if s - 1 in T_AT:
                                trn(g + 1, T_AT.index(s - 1))


def build(nc, t):
    t["xn"] = nc.dram_tensor("xn_rows", (N, XW), F32, kind="Internal").ap()
    slots_d = nc.dram_tensor("slots", (E * HI, LO), U32, kind="Internal").ap()
    with ExitStack() as stack:
        m = Mem(nc, stack)
        gates = m.sb("gates", [P, E, NT])
        thr = m.sb("threshold", [P, E])
        ident = m.sb("ident", [P, P])
        ends = RowEnds(m, t)
        m.start()
        with ExitStack() as mixer:
            w = MixerWeights(Mem(nc, mixer))
            stage_gate(nc, t, gates, ident, w, ends)
            ends.banks()
            stage_mixer(nc, t, gates, thr, ident, w, ends)
        ew = ExpertWeights(Mem(nc, stack), t)
        stage_lists(nc, gates, thr, slots_d, ends, ew)
        stage_experts(nc, t, ident, ends, ew)


SHAPES = {
    "x": (N, D), "gate_w": (P, KD, E), "w_in": (P, NW, KD * P), "conv_w": (P, NC_, 4), "conv_b": (P, NC_),
    "d_param": (P, NC_), "ln_g": (1, D), "ln_b": (1, D), "w_out": (P, NC_, D), "w_c": (S, 2, D), "w_b": (P, NC_ * S),
    "fc1": (E, FT, P, D), "fc2": (E, FT, P, D), "b1": (P, E * FT), "b2": (1, E * D), "f_ln_g": (1, D), "f_ln_b": (1, D),
}


def kernel(**i):
    import numpy as np
    import concourse.bacc as bacc
    from concourse.bass_utils import run_bass_kernel_spmd as run

    a = {k.replace("L0_", ""): np.asarray(v) for k, v in i.items()}

    def by_channel(v):
        return v.reshape(NC_, P, -1).transpose(1, 0, 2)

    arrays = {
        "x": a["attn_x"].reshape(N, D),
        "gate_w": a["ffn_gate_w"].reshape(E, KD, P).transpose(2, 1, 0),
        "w_in": a["attn_W_in"].reshape(NW, P, KD, P).transpose(3, 0, 2, 1).reshape(P, NW, KD * P),
        "conv_w": by_channel(a["attn_conv_w"]),
        "conv_b": by_channel(a["attn_conv_b"]).reshape(P, NC_),
        "d_param": by_channel(a["attn_D_param"]).reshape(P, NC_),
        "ln_g": a["attn_ln_gamma"].reshape(1, D),
        "ln_b": a["attn_ln_beta"].reshape(1, D),
        "w_out": by_channel(a["attn_W_out"].T),
        "w_c": a["attn_W_C"].T.reshape(S, 2, D),
        "w_b": by_channel(a["attn_W_B"].T).reshape(P, NC_ * S),
        "fc1": a["ffn_fc1s"].reshape(E, FT, P, KD, P).transpose(0, 1, 4, 3, 2).reshape(E, FT, P, D),
        "fc2": a["ffn_fc2s"].transpose(0, 2, 1).reshape(E, FT, P, D),
        "b1": a["ffn_b1s"].reshape(E, FT, P).transpose(2, 0, 1).reshape(P, E * FT),
        "b2": a["ffn_b2s"].reshape(1, E * D),
        "f_ln_g": a["ffn_ln_gamma"].reshape(1, D),
        "f_ln_b": a["ffn_ln_beta"].reshape(1, D),
    }
    arrays = {f"{k}_in": np.ascontiguousarray(v) for k, v in arrays.items()}
    nc = bacc.Bacc("TRN2", target_bir_lowering=False, num_devices=1)
    t = {k: nc.dram_tensor(f"{k}_in", s, F32, kind="ExternalInput").ap() for k, s in SHAPES.items()}
    t["out"] = nc.dram_tensor("out_dram", (N, D), F32, kind="ExternalOutput").ap()
    build(nc, t)
    r = run(nc, [arrays], core_ids=[0])
    return r.results[0]["out_dram"].reshape(a["attn_x"].shape)
```

```python
from contextlib import ExitStack

import concourse.bass as bass
from concourse import mybir
from concourse.alu_op_type import AluOpType as ALU

F32 = mybir.dt.float32
F32R = mybir.dt.float32r
BF16 = mybir.dt.bfloat16
U32 = mybir.dt.uint32
ACT = mybir.ActivationFunctionType
AX = mybir.AxisListType
RADD = bass.bass_isa.ReduceOp.add

P = 128
N, D, C, S, E, F = 8192, 512, 1024, 64, 8, 2048
SEQ = 2048
TB = 512
NB = N // TB
BPS = SEQ // TB
J = TB // P
NT = N // P
KD = D // P
NC_ = C // P
NW = 2 * NC_
FT = F // P
CAP = N // E
XW = D + E
EPS = 1e-5
DECAY, INPUT_FACTOR = 0.95, 0.05
LO = 32
HI = CAP // LO


class Count:

    def __init__(self, sem):
        self.sem = sem

    def start(self, eng):
        eng.sem_inc(self.sem, 1)

    def wait(self, eng, pieces):
        eng.wait_ge(self.sem, pieces + 1)


class PoolCount(Count):

    def start(self, eng):
        pass

    def prime(self, pool, dst, src):
        pool.dma_start(dst, src).then_inc(self.sem, 16)

    def wait(self, eng, pieces):
        eng.wait_ge(self.sem, pieces + 16)


class Mem:

    def __init__(self, nc, stack):
        self.nc, self.stack, self.counts = nc, stack, []
        self.ticks = {}

    def sb(self, name, shape, dt=F32):
        return self.stack.enter_context(self.nc.sbuf_tensor(name, shape, dt))

    def ps(self, name, shape, dt=F32):
        return self.stack.enter_context(self.nc.psum_tensor(name, shape, dt))

    def count(self, name):
        c = Count(self.stack.enter_context(self.nc.semaphore(name)))
        self.counts.append(c)
        return c

    def pool_count(self, name):
        return PoolCount(self.stack.enter_context(self.nc.semaphore(name)))

    def start(self):
        with self.nc.Block() as block:
            @block.sync
            def _(sp):
                for c in self.counts:
                    c.start(sp)

    def tick(self, name):
        return self.stack.enter_context(self.nc.semaphore(name))


def f(ap):
    return ap.bitcast(F32)


class RowEnds:

    def __init__(self, m, t):
        self.m = m
        self.x = t["x"].rearrange("(b j p) d -> b j p d", p=P, j=J)
        self.xn = t["xn"].rearrange("(b j p) d -> b j p d", p=P, j=J)
        self.out = t["out"].rearrange("(b j p) d -> b j p d", p=P, j=J)
        self.x_rows = [m.sb(f"x_tail{j}", [P, D]) for j in range(J)]
        self.xn_rows = [m.sb(f"xn_tail{i}", [P, D]) for i in range(2)]
        self.res = [m.sb(f"res{j}", [P, D]) for j in range(J)]
        self.gamma = m.sb("ln_g", [P, D])
        self.beta = m.sb("ln_b", [P, D])
        self.stats = m.sb("stats", [P, J, 6])
        self.mv = m.sb("mv", [P, J, 2])
        self.std = m.sb("std", [P, J])
        self.rstd = m.sb("rstd", [P, J])
        self.half = m.sb("half", [P, 1])
        self.c_nt = [m.count(f"m_nt{i}") for i in range(2)]
        self.c_xt = [m.count(f"m_xt{j}") for j in range(J)]
        self.c_st = [m.count(f"m_st{j}") for j in range(J)]
        self.c_o = m.count("m_o")
        self.c_po = m.count("m_po")
        self.c_r = m.count("m_r")
        self.c_bn = m.count("m_bn")
        self.c_mv = m.count("m_mv")
        self.c_eps = m.count("m_eps")
        self.c_rs = m.count("m_rs")
        self.c_g = m.count("m_g")
        self.c_s = m.count("m_s")
        self.c_sb = m.count("m_sb")
        self.c_fin = m.count("m_fin")
        self.p_tick = m.tick("m_ptick")
        self.d_tick = m.tick("m_dtick")

    def banks(self):
        self.po = [self.m.ps(f"po{j}", [P, D]) for j in range(J)]

    def load_x(self, sp, b, j):
        sp.dma_start(self.x_rows[j][:, :], self.x[b, j]).then_inc(self.c_xt[j].sem, 16)

    def load_xn(self, sp, b, j):
        self.c_s.wait(sp, b * J + j - 1 if j > 1 else b * J)
        sp.dma_start(self.xn_rows[j % 2][:, :], self.xn[b, j][:, 0:D]).then_inc(self.c_nt[j % 2].sem, 16)

    def store(self, sp, b, j):
        self.c_fin.wait(sp, b * J + j + 1)
        sp.dma_start(self.out[b, j], self.res[j][:, :]).then_inc(self.c_st[j].sem, 16)

    def store_and_load(self, sp, b):
        self.load_xn(sp, b + 1, 0)
        self.load_xn(sp, b + 1, 1)
        for j in range(J):
            self.store(sp, b, j)
            self.load_x(sp, b + 1, j)

    def rows_out(self, act, b, j):
        self.c_o.wait(act, (b + 1) * NC_)
        self.c_st[j].wait(act, 16 * b)
        act.copy(self.res[j][:, :], self.po[j][:, :]).then_inc(self.c_po.sem, 1)

    def add_xn(self, pool, b, j):
        n = b * J + j
        self.c_po.wait(pool, n + 1)
        self.c_nt[j % 2].wait(pool, 16 * (b * (J // 2) + j // 2 + 1))
        pool.tensor_tensor(self.res[j][:, :], self.res[j][:, :], self.xn_rows[j % 2][:, :],
                           ALU.add).then_inc(self.c_r.sem, 1)
        self.c_xt[j].wait(pool, 16 * (b + 1))
        pool.tensor_tensor(self.x_rows[j][:, :], self.x_rows[j][:, :], self.xn_rows[j % 2][:, :],
                           ALU.add).then_inc(self.c_s.sem, 1)

    def add_beta(self, pool, b, j):
        self.c_s.wait(pool, b * J + j + 1)
        pool.tensor_tensor(self.x_rows[j][:, :], self.x_rows[j][:, :], self.beta[:, :],
                           ALU.add).then_inc(self.c_sb.sem, 1)

    def add_pair(self, pool, b, j):
        self.add_xn(pool, b, j)
        self.add_xn(pool, b, j + 1)
        self.add_beta(pool, b, j)
        self.add_beta(pool, b, j + 1)

    def inverse_std(self, pool, b, j):
        n = b * J + j
        self.c_mv.wait(pool, n + 1)
        self.c_rs.wait(pool, n)
        pool.sem_inc(self.p_tick, 1)
        pool.tensor_scalar(self.std[:, j:j + 1], self.mv[:, j, 1:2], EPS, None, ALU.add).then_inc(self.c_eps.sem, 1)
        self.c_eps.wait(pool, n + 1)
        pool.tensor_tensor(self.rstd[:, j:j + 1], self.std[:, j:j + 1], self.half[:, :],
                           ALU.pow).then_inc(self.c_rs.sem, 1)

    def statistics(self, dve, b, j):
        n = b * J + j
        self.c_r.wait(dve, n + 1)
        self.c_mv.wait(dve, b * J)
        dve.bn_stats(self.stats[:, j, :], self.res[j][:, :]).then_inc(self.c_bn.sem, 1)
        self.c_bn.wait(dve, n + 1)
        self.c_rs.wait(dve, b * J)
        self.c_fin.wait(dve, b * J)
        dve.sem_inc(self.d_tick, 1)
        dve.bn_aggr(self.mv[:, j, :], self.stats[:, j, :]).then_inc(self.c_mv.sem, 1)

    def scale(self, dve, b, j):
        n = b * J + j
        self.c_rs.wait(dve, n + 1)
        self.c_mv.wait(dve, n + 1)
        self.c_g.wait(dve, n)
        dve.scalar_tensor_tensor(out=self.res[j][:, :], in0=self.res[j][:, :], scalar=self.mv[:, j, 0:1],
                                 in1=self.gamma[:, :], op0=ALU.subtract, op1=ALU.mult).then_inc(self.c_g.sem, 1)

    def finish(self, dve, b, j):
        n = b * J + j
        self.c_g.wait(dve, n + 1)
        self.c_sb.wait(dve, n + 1)
        dve.scalar_tensor_tensor(out=self.res[j][:, :], in0=self.res[j][:, :], scalar=self.rstd[:, j:j + 1],
                                 in1=self.x_rows[j][:, :], op0=ALU.mult, op1=ALU.add).then_inc(self.c_fin.sem, 1)


class MixerWeights:

    def __init__(self, m):
        self.w_in = m.sb("w_in", [P, NW, KD * P])
        self.wout_h = m.sb("wout_h", [P, NC_, D], F32R)
        self.wout_l = m.sb("wout_l", [P, NC_, D], F32R)
        self.wb = m.sb("wb", [P, NC_, 2 * S], F32R)
        self.wc_h = m.sb("wc_h", [P, C], F32R)
        self.wc_l = m.sb("wc_l", [P, C], F32R)
        self.cw = m.sb("cw", [P, NC_, 4])
        self.cb = m.sb("cb", [P, NC_])
        self.dp = m.sb("dp", [P, NC_])


def stage_gate(nc, t, gates, ident, w, ends):
    R = 4
    NG = NB // R
    MID = NB // 2
    assert NC_ == NB - MID
    with ExitStack() as stack:
        m = Mem(nc, stack)
        xt = [m.sb(f"g_x{i}", [P, J, D]) for i in range(R)]
        ext = [m.sb(f"g_ext{i}", [P, J, XW]) for i in range(R)]
        stats = m.sb("g_stats", [P, J, 6])
        mv = [m.sb(f"g_mv{i}", [P, J, 2]) for i in range(2)]
        std = m.sb("g_std", [P, J])
        rstd = [m.sb(f"g_rstd{i}", [P, J]) for i in range(2)]
        half = m.sb("g_half", [P, J])
        xnt = [m.sb(f"g_xnt{k}", [P, TB]) for k in range(KD)]
        sc_t = m.sb("g_sc_t", [E, TB])
        staged = m.sb("g_staged", [P, NC_, TB])
        staged2 = m.sb("g_staged2", [P, 4, TB])
        tanh = m.sb("g_tanh", [P, J * E])
        gw = m.sb("g_gw", [P, KD, E])
        pt = [m.ps(f"g_pt{k}", [P, TB]) for k in range(KD)]
        pst = m.ps("g_pst", [E, TB])
        psc = m.ps("g_psc", [P, J * E])

        c_id = m.count("g_id")
        c_gw = m.count("g_gw_in")
        c_x = [m.count(f"g_x_in{i}") for i in range(R)]
        c_st = [m.count(f"g_out{i}") for i in range(R)]
        c_bn = m.count("g_bn")
        c_mv = m.count("g_mv_set")
        c_eps = m.count("g_eps")
        c_rs = m.count("g_rs")
        c_xn = m.count("g_xn")
        c_t = m.count("g_t")
        c_tc = m.count("g_tc")
        c_se = m.count("g_se")
        c_sr = m.count("g_sr")
        c_sc = m.count("g_sc")
        c_win = m.count("g_win")
        c_in = m.count("g_infac")
        c_sh = m.count("g_sh")
        c_sl = m.count("g_sl")
        c_th = m.count("g_th")
        c_v = m.count("g_v")
        d_tick = m.tick("g_dtick")
        p_tick = m.tick("g_ptick")
        t_tick = m.tick("g_ttick")

        x_v = t["x"].rearrange("(b j p) d -> b p j d", p=P, j=J)
        xn_v = t["xn"].rearrange("(b j p) d -> b p j d", p=P, j=J)

        m.start()
        with nc.Block() as block:
            @block.sync
            def _(sp):
                def store(b, i):
                    c_v.wait(sp, b * 2 + 1)
                    sp.dma_start(xn_v[b], ext[i][:, :, :]).then_inc(c_st[i].sem, 16)

                def groups(first, end):
                    with sp.Fori(first, end) as h:
                        for i in range(R):
                            b = h * R + i
                            c_xn.wait(sp, (b + 1) * J)
                            sp.dma_start(xt[i][:, :, :], x_v[b + R]).then_inc(c_x[i].sem, 16)
                            store(b, i)

                sp.dma_start(xt[0][:, :, :], x_v[0]).then_inc(c_x[0].sem, 16)
                sp.dma_start(gw[:, :, :], t["gate_w"]).then_inc(c_gw.sem, 16)
                for i in range(1, R):
                    sp.dma_start(xt[i][:, :, :], x_v[i]).then_inc(c_x[i].sem, 16)
                groups(0, 1)
                sp.dma_start(staged[:, :, :], t["w_out"]).then_inc(c_win.sem, 16)
                sp.dma_start(staged2[0:S, 0:2, :], t["w_c"]).then_inc(c_win.sem, 16)
                sp.dma_start(staged2[S:P, 0:2, :], t["w_c"]).then_inc(c_win.sem, 16)
                sp.dma_start(staged2[:, 2, :], t["w_b"]).then_inc(c_win.sem, 16)
                groups(1, NG - 1)
                sp.dma_start(w.cw[:, :, :], t["conv_w"]).then_inc(c_win.sem, 16)
                sp.dma_start(w.cb[:, :], t["conv_b"]).then_inc(c_win.sem, 16)
                sp.dma_start(w.dp[:, :], t["d_param"]).then_inc(c_win.sem, 16)
                sp.dma_start(ends.gamma[:, :], t["ln_g"].to_broadcast([P, D])).then_inc(c_win.sem, 16)
                sp.dma_start(ends.beta[:, :], t["ln_b"].to_broadcast([P, D])).then_inc(c_win.sem, 16)
                for i in range(R):
                    store(NB - R + i, i)
                c_win.wait(sp, 16 * 9)
                for i in range(R):
                    c_st[i].wait(sp, 16 * NG)

            @block.gpsimd
            def _(pool):
                c_id.wait(pool, 0)
                pool.memset(ident[:, :], 0.0).then_inc(c_id.sem, 1)
                pool.memset(half[:, :], -0.5).then_inc(c_id.sem, 1)
                c_id.wait(pool, 2)
                pool.affine_select(out=ident[:, :], in_=ident[:, :], compare_op=ALU.not_equal, fill=1.0,
                                   base=0, pattern=[[-1, P]], channel_multiplier=1).then_inc(c_id.sem, 1)

                def pair(h):
                    for i in range(2):
                        b = h * 2 + i
                        c_mv.wait(pool, (b + 1) * J)
                        c_rs.wait(pool, b)
                        pool.sem_inc(p_tick, 1)
                        pool.tensor_scalar(std[:, :], mv[i][:, :, 1], EPS, None, ALU.add).then_inc(c_eps.sem, 1)
                        c_eps.wait(pool, b + 1)
                        pool.tensor_tensor(rstd[i][:, :], std[:, :], half[:, :], ALU.pow).then_inc(c_rs.sem, 1)

                def low_tiles(first):
                    for i in range(2):
                        tile = bass.ds(first + i, 1)
                        c_sh.wait(pool, first + i + 2)
                        pool.sem_inc(p_tick, 1)
                        pool.tensor_tensor(w.wout_l[:, tile, :], staged[:, tile, :], f(w.wout_h[:, tile, :]),
                                           ALU.subtract).then_inc(c_sl.sem, 1)

                with pool.Fori(0, MID // 2 + 1) as h:
                    pair(h)
                with pool.Fori(MID // 2 + 1, NB // 2) as h:
                    pair(h)
                    low_tiles((h - 1) * 2 - MID)
                low_tiles(NC_ - 2)
                pool.tensor_tensor(w.wc_l[:, :], staged2[:, 0:2, :].rearrange("p a b -> p (a b)"),
                                   f(w.wc_h[:, :]), ALU.subtract).then_inc(c_sl.sem, 1)
                c_sh.wait(pool, NC_ + 2)
                pool.tensor_tensor(w.wb[:, :, S:2 * S], staged2[:, 3, :].rearrange("p (c s) -> p c s", s=S),
                                   f(w.wb[:, :, 0:S]), ALU.subtract).then_inc(c_sl.sem, 1)

            @block.vector
            def _(dve):
                def statistics(b, h, i, done):
                    c_x[i].wait(dve, h * 16 + 16)
                    c_mv.wait(dve, b * J)
                    for j in range(J):
                        dve.bn_stats(stats[:, j, :], xt[i][:, j, :]).then_inc(c_bn.sem, 1)
                    c_bn.wait(dve, (b + 1) * J)
                    c_rs.wait(dve, done)
                    c_xn.wait(dve, done * J)
                    dve.sem_inc(d_tick, 1)
                    for j in range(J):
                        dve.bn_aggr(mv[i % 2][:, j, :], stats[:, j, :]).then_inc(c_mv.sem, 1)

                def normalise(b, h, i):
                    c_rs.wait(dve, b + 1)
                    c_mv.wait(dve, (b + 1) * J)
                    c_st[i].wait(dve, h * 16)
                    for j in range(J):
                        dve.tensor_scalar(ext[i][:, j, 0:D], xt[i][:, j, :], mv[i % 2][:, j, 0:1],
                                          rstd[i % 2][:, j:j + 1], ALU.subtract, ALU.mult).then_inc(c_xn.sem, 1)

                def gate_values(b, i):
                    c_th.wait(dve, b + 1)
                    half_tanh = tanh[:, :].rearrange("p (j e) -> p j e", e=E)
                    dve.tensor_scalar(ext[i][:, :, D:XW], half_tanh, 1.0, 0.5,
                                      ALU.add, ALU.mult).then_inc(c_v.sem, 1)
                    dve.tensor_scalar(gates[:, :, bass.ds(b * J, J)], tanh[:, :].rearrange("p (j e) -> p e j", e=E),
                                      1.0, 0.5, ALU.add, ALU.mult).then_inc(c_v.sem, 1)

                def group(h, first=False, last=False):
                    for i in range(R):
                        b = h * R + i
                        normalise(b, h, i)
                        if first and i == 0:
                            statistics(1, 0, 1, 1)
                        if not (last and i >= R - 2):
                            statistics(b + 2, h + 1 if i >= R - 2 else h, (i + 2) % R, b + 1)
                        if not (first and i == 0):
                            gate_values(b - 1, (i - 1) % R)

                statistics(0, 0, 0, 0)
                group(0, first=True)
                with dve.Fori(1, NG - 1) as h:
                    group(h)
                c_win.wait(dve, 64)
                dve.tensor_scalar(staged2[:, 3, :], staged2[:, 2, :], INPUT_FACTOR, None,
                                  ALU.mult).then_inc(c_in.sem, 1)
                group(NG - 1, last=True)
                gate_values(NB - 1, R - 1)

            @block.tensor
            def _(pe):
                def turn_scores(b):
                    c_sr.wait(pe, b + 1)
                    c_th.wait(pe, b)
                    pe.sem_inc(t_tick, 1)
                    for j in range(J):
                        last = pe.transpose(psc[:, j * E:(j + 1) * E], sc_t[:, j * P:(j + 1) * P],
                                            ident[0:E, 0:E])
                    last.then_inc(c_sc.sem, 1)

                def group(h, first=False):
                    for i in range(R):
                        b = h * R + i
                        for k in range(KD):
                            c_tc.wait(pe, (b - 1) * KD + k + 1 if not (first and i == 0) else 0)
                            for j in range(J):
                                if k == 0:
                                    c_xn.wait(pe, b * J + j + 1)
                                last = pe.transpose(pt[k][:, j * P:(j + 1) * P],
                                                    ext[i][:, j, k * P:(k + 1) * P], ident[:, :])
                            last.then_inc(c_t.sem, 1)
                        if not (first and i == 0):
                            turn_scores(b - 1)
                        c_sr.wait(pe, b)
                        for k in range(KD):
                            c_tc.wait(pe, b * KD + k + 1)
                            pe.matmul(pst[:, :], gw[:, k, :], xnt[k][:, :], start=(k == 0),
                                      stop=(k == KD - 1)).then_inc(c_se.sem, 1)

                c_id.wait(pe, 3)
                c_gw.wait(pe, 16)
                group(0, first=True)
                with pe.Fori(1, NG) as h:
                    group(h)
                turn_scores(NB - 1)

            @block.scalar
            def _(act):
                def turn_tanh(b):
                    c_sc.wait(act, b + 1)
                    c_v.wait(act, b * 2)
                    act.activation(tanh[:, :], psc[:, :], ACT.Tanh).then_inc(c_th.sem, 1)

                def group(h, first=False, split=False):
                    for i in range(R):
                        b = h * R + i
                        if split:
                            tile = bass.ds(b - MID, 1)
                            act.copy(w.wout_h[:, tile, :], staged[:, tile, :]).then_inc(c_sh.sem, 1)
                        for k in range(KD):
                            c_t.wait(act, b * KD + k + 1)
                            c_se.wait(act, (b - 1) * KD + k + 1 if not (first and i == 0) else 0)
                            act.copy(xnt[k][:, :], pt[k][:, :]).then_inc(c_tc.sem, 1)
                        if not (first and i == 0):
                            turn_tanh(b - 1)
                        c_se.wait(act, (b + 1) * KD)
                        c_sc.wait(act, b)
                        act.copy(sc_t[:, :], pst[:, :]).then_inc(c_sr.sem, 1)

                group(0, first=True)
                with act.Fori(1, NG // 2) as h:
                    group(h)
                c_win.wait(act, 64)
                act.copy(w.wc_h[:, :], staged2[:, 0:2, :].rearrange("p a b -> p (a b)")).then_inc(c_sh.sem, 1)
                with act.Fori(NG // 2, NG) as h:
                    group(h, split=True)
                c_in.wait(act, 1)
                act.copy(w.wb[:, :, 0:S], staged2[:, 3, :].rearrange("p (c s) -> p c s", s=S)).then_inc(c_sh.sem, 1)
                turn_tanh(NB - 1)


BIS = 5
BIS_PER_TURN = 2
assert BIS_PER_TURN * NB >= 26


def count_at_or_above(dve, gates, bis, c_cand, c_cnt, n):
    thr, step, cand, ge, cnt, tot = bis
    c_cand.wait(dve, BIS * n + 1)
    c_cnt.wait(dve, 2 * n)
    dve.tensor_tensor(ge[:, :, :], gates[:, :, :],
                      cand[:, :].rearrange("p (e o) -> p e o", o=1).to_broadcast([P, E, NT]),
                      ALU.is_ge).then_inc(c_cnt.sem, 1)
    c_cnt.wait(dve, 2 * n + 1)
    dve.tensor_reduce(cnt[:, :], ge[:, :, :], AX.X, ALU.add).then_inc(c_cnt.sem, 1)


def halve(pool, bis, c_cand, c_cnt, n, hold):
    thr, step, cand, ge, cnt, tot = bis
    c_cnt.wait(pool, 2 * n + 2)
    c_cand.wait(pool, BIS * n + 1)
    hold()
    pool.partition_all_reduce(tot[:, :], cnt[:, :], P, RADD).then_inc(c_cand.sem, 1)
    c_cand.wait(pool, BIS * n + 2)
    hold()
    pool.tensor_scalar(tot[:, :], tot[:, :], float(CAP), step[:, 0:1], ALU.is_ge, ALU.mult).then_inc(c_cand.sem, 1)
    c_cand.wait(pool, BIS * n + 3)
    pool.tensor_tensor(thr[:, :], thr[:, :], tot[:, :], ALU.add).then_inc(c_cand.sem, 1)
    hold()
    pool.tensor_scalar(step[:, :], step[:, :], 0.5, None, ALU.mult).then_inc(c_cand.sem, 1)
    c_cand.wait(pool, BIS * n + 5)
    hold()
    pool.tensor_scalar(cand[:, :], thr[:, :], step[:, 0:1], None, ALU.add).then_inc(c_cand.sem, 1)


def stage_mixer(nc, t, gates, thr, ident, w, ends):
    LATE = 2
    TAPS = 3
    with ExitStack() as stack:
        m = Mem(nc, stack)
        wh = [m.sb(f"wh{i}", [P, KD * P], F32R) for i in range(4)]
        wl = [m.sb(f"wl{i}", [P, KD * P], F32R) for i in range(4)]
        xt_h = m.sb("xt_h", [P, KD, TB], F32R)
        xt_l = m.sb("xt_l", [P, KD, TB], F32R)
        rows = m.sb("xn_next", [P, J, D])
        u = m.sb("u", [P, NC_, TB])
        u_h = [m.sb(f"u_h{i}", [P, TB], F32R) for i in range(2)]
        u_l = [m.sb(f"u_l{i}", [P, TB], F32R) for i in range(2)]
        y_h = [m.sb(f"y_h{i}", [P, TB], F32R) for i in range(3)]
        y_l = [m.sb(f"y_l{i}", [P, TB], F32R) for i in range(3)]
        sg = m.sb("sg", [P, NC_, TB])
        xin = [m.sb(f"xin{i}", [P, 3 + TB]) for i in range(2)]
        halo = m.sb("halo", [P, NC_, 3])
        h = m.sb("h", [P, TB])
        h_h = m.sb("h_h", [P, TB], F32R)
        h_l = m.sb("h_l", [P, TB], F32R)
        carry = m.sb("carry", [P, 1])
        decay = m.sb("decay", [P, 1])
        step = m.sb("bis_step", [P, 1])
        cand = m.sb("bis_cand", [P, E])
        ge = m.sb("bis_ge", [P, E, NT], BF16)
        cnt = m.sb("bis_cnt", [P, E])
        tot = m.sb("bis_tot", [P, E])
        bis = (thr, step, cand, ge, cnt, tot)
        ring = [m.ps(f"ring{i}", [P, TB]) for i in range(2)]
        pb = m.ps("pb", [P, TB])
        pcb = [m.ps("pc", [P, TB]), pb]
        po, c_o, c_po = ends.po, ends.c_o, ends.c_po
        p_tick, d_tick = ends.p_tick, ends.d_tick

        c_win = [m.count(f"m_win{s}") for s in range(NW)]
        c_rows = m.count("m_rows")
        c_set = m.count("m_set")
        c_wh = m.count("m_wh")
        c_wl = m.count("m_wl")
        c_ag = m.count("m_ag")
        c_x = m.count("m_x")
        c_ev = m.count("m_ev")
        c_halo = m.count("m_halo")
        c_cv = m.count("m_cv")
        c_u = m.count("m_u")
        c_uh = m.count("m_uh")
        c_ul = m.count("m_ul")
        c_b = m.count("m_b")
        c_h = m.count("m_h")
        c_car = m.count("m_car")
        c_hh = m.count("m_hh")
        c_hl = m.count("m_hl")
        c_c = m.count("m_c")
        c_y1 = m.count("m_y1")
        c_y2 = m.count("m_y2")
        c_yh = m.count("m_yh")
        c_yl = m.count("m_yl")
        c_t = m.count("m_t")
        c_th = m.count("m_th")
        c_tl = m.count("m_tl")
        c_cand = m.count("m_cand")
        c_cnt = m.count("m_cnt")
        z = m.count("m_zero")

        xn_v = t["xn"].rearrange("(b j p) d -> b j p d", p=P, j=J)

        order = [("G", 0), ("A", 0), ("A", 1), ("A", 2)]
        for c in range(1, NC_ - 2):
            order += [("G", c), ("A", c + 2)]
        order += [("G", NC_ - 2), ("G", NC_ - 1)]
        u_after = {2: 0, 4: 1, 5: 2, 7: 3, 9: 4, 11: 5, 13: 6, 15: 7}
        b_after = {5: 0, 6: 1, 8: 2, 9: 3, 11: 4, 13: 5, 15: 6}

        def column(s):
            kind, c = order[s % NW]
            return c + (NC_ if kind == "G" else 0)

        def a_step(c):
            return order.index(("A", c))

        def g_step(c):
            return order.index(("G", c))

        m.start()
        with nc.Block() as block:
            @block.sync
            def _(sp):
                def load_rows(b):
                    sp.dma_start(rows[:, :, :], xn_v[b].rearrange("j p d -> p j d")[:, :, 0:D]).then_inc(c_rows.sem, 16)

                load_rows(0)
                for s in range(NW):
                    sp.dma_start(w.w_in[:, column(s), :], t["w_in"][:, column(s), :]).then_inc(c_win[s].sem, 16)
                c_t.wait(sp, KD)
                load_rows(1)
                for j in range(J):
                    ends.load_x(sp, 0, j)
                ends.load_xn(sp, 0, 0)
                ends.load_xn(sp, 0, 1)
                c_t.wait(sp, 2 * KD)
                load_rows(2)
                ends.load_xn(sp, 0, 2)
                ends.load_xn(sp, 0, 3)
                with sp.Fori(2, NB - 1) as b:
                    c_t.wait(sp, (b + 1) * KD)
                    load_rows(b + 1)
                    ends.store_and_load(sp, b - 2)
                    ends.load_xn(sp, b - 1, 2)
                    ends.load_xn(sp, b - 1, 3)
                c_t.wait(sp, NB * KD)
                load_rows(0)
                ends.store_and_load(sp, NB - 3)
                ends.load_xn(sp, NB - 2, 2)
                ends.load_xn(sp, NB - 2, 3)

            @block.gpsimd
            def _(pool):
                def hold():
                    pool.sem_inc(p_tick, 1)

                pool.memset(ends.half[:, :], -0.5).then_inc(c_set.sem, 1)
                pool.memset(decay[:, :], DECAY).then_inc(c_set.sem, 1)
                pool.memset(thr[:, :], 0.0).then_inc(c_set.sem, 1)
                pool.memset(step[:, :], 1.0).then_inc(c_set.sem, 1)
                c_set.wait(pool, 4)
                pool.tensor_scalar(cand[:, :], thr[:, :], step[:, 0:1], None, ALU.add).then_inc(c_cand.sem, 1)

                def w_low(n, s):
                    c_wh.wait(pool, n + 1)
                    pool.tensor_tensor(wl[s % 4][:, :], w.w_in[:, column(s), :], f(wh[s % 4][:, :]),
                                       ALU.subtract).then_inc(c_wl.sem, 1)

                def turn(b, with_last, with_end):
                    for s in range(NW):
                        w_low(b * NW + s + 3, s + 3)
                        if with_end and s < J:
                            ends.inverse_std(pool, b - 2, s)
                    for q in range(BIS_PER_TURN):
                        if with_last:
                            ends.add_pair(pool, b - 1, 2 * q)
                        halve(pool, bis, c_cand, c_cnt, b * BIS_PER_TURN + q, hold)

                for s in range(3):
                    w_low(s, s)
                turn(0, False, False)
                turn(1, True, False)
                with pool.Fori(2, NB) as b:
                    turn(b, True, True)

            @block.scalar
            def _(act):
                def w_high(n, s, first_turn=False):
                    if first_turn and s < NW:
                        c_win[s].wait(act, 16)
                    act.copy(wh[s % 4][:, :], w.w_in[:, column(s), :]).then_inc(c_wh.sem, 1)

                def t_high(n, k):
                    c_t.wait(act, n + 1)
                    act.copy(xt_h[:, k, :], ring[k % 2][:, :]).then_inc(c_th.sem, 1)

                def u_pair(b, c):
                    n = b * NC_ + c
                    c_cv.wait(act, TAPS * (n + 1))
                    act.activation(u[:, c, :], u[:, c, :], ACT.Silu).then_inc(c_u.sem, 1)
                    c_u.wait(act, n + 1)
                    c_b.wait(act, b * NC_ if c < 2 else n - 1)
                    c_ul.wait(act, b * NC_ if c < 2 else n - 1)
                    act.copy(u_h[c % 2][:, :], u[:, c, :]).then_inc(c_uh.sem, 1)

                def y_high(b, c, with_last):
                    n = b * NC_ + c
                    if c >= 3:
                        c_o.wait(act, n - 2)
                        c_yl.wait(act, n - 2)
                    elif with_last:
                        c_o.wait(act, b * NC_ - (1 if c == 0 else 0))
                        c_yl.wait(act, b * NC_)
                    c_y2.wait(act, n + 1)
                    act.copy(y_h[c % 3][:, :], u[:, c, :]).then_inc(c_yh.sem, 1)

                for s in range(3):
                    w_high(s, s, True)
                for k in range(KD):
                    t_high(k, k)

                def turn(b, with_last):
                    for s in range(NW):
                        n = b * NW + s
                        c_ag.wait(act, n)
                        c_wl.wait(act, n)
                        w_high(n + 3, s + 3, not with_last)
                        kind, c = order[s]
                        if kind == "A":
                            c_cv.wait(act, b * (TAPS * NC_) + (TAPS * (c - 1) if c > 1 else 0))
                            c_halo.wait(act, b * (2 * NC_) + (2 * (c - 1) if c > 1 else 0))
                            c_ag.wait(act, n + 1)
                            act.copy(xin[c % 2][:, 3:3 + TB], ring[s % 2][:, :]).then_inc(c_x.sem, 1)
                            c_yl.wait(act, b * NC_)
                            act.activation(u[:, c, :], ring[s % 2][:, :], ACT.Identity, bias=w.cb[:, c:c + 1],
                                           scale=w.cw[:, c, 3:4]).then_inc(c_ev.sem, 1)
                        else:
                            c_y2.wait(act, b * NC_)
                            c_ag.wait(act, n + 1)
                            act.activation(sg[:, c, :], ring[s % 2][:, :], ACT.Silu).then_inc(c_ev.sem, 1)
                        if s in u_after:
                            u_pair(b, u_after[s])
                    t_high((b + 1) * KD, 0)
                    t_high((b + 1) * KD + 1, 1)
                    c_c.wait(act, b * NC_)
                    c_hl.wait(act, b)
                    c_h.wait(act, b + 1)
                    act.copy(h_h[:, :], h[:, :]).then_inc(c_hh.sem, 1)
                    t_high((b + 1) * KD + 2, 2)
                    t_high((b + 1) * KD + 3, 3)
                    y_high(b, 0, with_last)
                    if with_last:
                        for j in range(J):
                            ends.rows_out(act, b - 1, j)
                    for c in range(1, NC_):
                        y_high(b, c, with_last)

                turn(0, False)
                with act.Fori(1, NB) as b:
                    turn(b, True)

            @block.vector
            def _(dve):
                c_set.wait(dve, 4)

                def t_low(n, k):
                    c_th.wait(dve, n + 1)
                    dve.tensor_tensor(xt_l[:, k, :], ring[k % 2][:, :], f(xt_h[:, k, :]),
                                      ALU.subtract).then_inc(c_tl.sem, 1)

                def u_low(b, c):
                    c_uh.wait(dve, b * NC_ + c + 1)
                    dve.tensor_tensor(u_l[c % 2][:, :], u[:, c, :], f(u_h[c % 2][:, :]),
                                      ALU.subtract).then_inc(c_ul.sem, 1)

                def conv(b, c):
                    n = b * NC_ + c
                    x_ = xin[c % 2]
                    c_halo.wait(dve, 2 * n)
                    c_cv.wait(dve, TAPS * (b * NC_ if c < 2 else n - 1))
                    dve.tensor_copy(x_[:, 0:3], halo[:, c, :]).then_inc(c_halo.sem, 1)
                    c_x.wait(dve, n + 1)
                    c_halo.wait(dve, 2 * n + 1)
                    dve.tensor_copy(halo[:, c, :], x_[:, TB:TB + 3]).then_inc(c_halo.sem, 1)
                    c_ev.wait(dve, b * NW + a_step(c) + 1)
                    for q in range(1, TAPS + 1):
                        c_cv.wait(dve, TAPS * n + q - 1)
                        dve.scalar_tensor_tensor(out=u[:, c, :], in0=x_[:, 3 - q:3 - q + TB],
                                                 scalar=w.cw[:, c, 3 - q:4 - q], in1=u[:, c, :],
                                                 op0=ALU.mult, op1=ALU.add).then_inc(c_cv.sem, 1)

                def scan(b):
                    c_b.wait(dve, (b + 1) * NC_)
                    c_hh.wait(dve, b)
                    c_hl.wait(dve, b)
                    c_car.wait(dve, b)
                    dve.tensor_tensor_scan(h[:, :], decay[:, 0:1].to_broadcast([P, TB]), pb[:, :], carry[:, 0:1],
                                           ALU.mult, ALU.add).then_inc(c_h.sem, 1)
                    c_h.wait(dve, b + 1)
                    dve.tensor_copy(carry[:, :], h[:, TB - 1:TB]).then_inc(c_car.sem, 1)

                def h_low(b):
                    c_hh.wait(dve, b + 1)
                    dve.tensor_tensor(h_l[:, :], h[:, :], f(h_h[:, :]), ALU.subtract).then_inc(c_hl.sem, 1)

                def y_turn(b, c):
                    n = b * NC_ + c
                    c_c.wait(dve, n + 1)
                    dve.scalar_tensor_tensor(out=u[:, c, :], in0=u[:, c, :], scalar=w.dp[:, c:c + 1],
                                             in1=pcb[c % 2][:, :], op0=ALU.mult, op1=ALU.add).then_inc(c_y1.sem, 1)
                    c_ev.wait(dve, b * NW + g_step(c) + 1)
                    c_y1.wait(dve, n + 1)
                    dve.tensor_tensor(u[:, c, :], u[:, c, :], sg[:, c, :], ALU.mult).then_inc(c_y2.sem, 1)

                def y_low(b, c):
                    c_yh.wait(dve, b * NC_ + c + 1)
                    dve.tensor_tensor(y_l[c % 3][:, :], u[:, c, :], f(y_h[c % 3][:, :]),
                                      ALU.subtract).then_inc(c_yl.sem, 1)

                stats_after = {3: 0, 4: 1, 6: 2, 7: 3}

                def turn(b, with_last, with_end):
                    for c in range(NC_):
                        conv(b, c)
                        if with_end and c < NC_ - 1:
                            (ends.scale, ends.finish)[c % 2](dve, b - 2, c // 2)
                        u_low(b, c)
                    if with_end:
                        ends.finish(dve, b - 2, J - 1)
                    scan(b)
                    t_low((b + 1) * KD, 0)
                    h_low(b)
                    t_low((b + 1) * KD + 1, 1)
                    for c in range(NC_):
                        y_turn(b, c)
                        if c < 2:
                            t_low((b + 1) * KD + 2 + c, 2 + c)
                        if with_last and c in stats_after:
                            ends.statistics(dve, b - 1, stats_after[c])
                        y_low(b, c)
                        if c in (2, 5):
                            count_at_or_above(dve, gates, bis, c_cand, c_cnt, b * BIS_PER_TURN + c // 3)

                def new_sequence(b):
                    c_halo.wait(dve, 2 * NC_ * b)
                    c_car.wait(dve, b)
                    c_h.wait(dve, b)
                    dve.memset(halo[:, :, :], 0.0).then_inc(z.sem, 1)
                    dve.memset(carry[:, :], 0.0).then_inc(z.sem, 1)

                for k in range(KD):
                    t_low(k, k)
                new_sequence(0)
                z.wait(dve, 2)
                turn(0, False, False)
                turn(1, True, False)
                with dve.Fori(2, BPS) as b:
                    turn(b, True, True)
                with dve.Fori(1, NB // BPS) as q:
                    new_sequence(q * BPS)
                    z.wait(dve, 2 * q + 2)
                    dve.sem_inc(d_tick, 1)
                    with dve.Fori(0, BPS) as r:
                        turn(q * BPS + r, True, True)

            @block.tensor
            def _(pe):
                def three(dst, ah, al, bh, bl, start, stop):
                    pe.matmul(dst, ah, bh, start=start, stop=False)
                    pe.matmul(dst, ah, bl, start=False, stop=False)
                    return pe.matmul(dst, al, bh, start=False, stop=stop)

                def ag(b, s):
                    n = b * NW + s
                    c_wl.wait(pe, n + 1)
                    if s == 0:
                        c_th.wait(pe, (b + 1) * KD)
                        c_tl.wait(pe, (b + 1) * KD)
                    if s > 1:
                        c_ev.wait(pe, n - 1)
                    for k in range(KD):
                        r = slice(k * P, (k + 1) * P)
                        last = three(ring[s % 2][:, :], wh[s % 4][:, r], wl[s % 4][:, r],
                                     xt_h[:, k, :], xt_l[:, k, :], k == 0, k == KD - 1)
                    last.then_inc(c_ag.sem, 1)

                def share_b(b, c):
                    c_ul.wait(pe, b * NC_ + c + 1)
                    if c == 0:
                        c_y1.wait(pe, b * NC_)
                    pe.matmul(pb[:, :], w.wb[:, c, :], u_h[c % 2][:, :], start=(c == 0), stop=False)
                    pe.matmul(pb[:, :], w.wb[:, c, :], u_l[c % 2][:, :], start=False,
                              stop=(c == NC_ - 1)).then_inc(c_b.sem, 1)

                def chan(b, c):
                    r = slice(c * P, (c + 1) * P)
                    if c == 0:
                        c_y1.wait(pe, b * NC_)
                        c_hl.wait(pe, b + 1)
                    elif c > 1:
                        c_y1.wait(pe, b * NC_ + c - 1)
                    three(pcb[c % 2][:, :], w.wc_h[:, r], w.wc_l[:, r], h_h[:, :], h_l[:, :],
                          True, True).then_inc(c_c.sem, 1)

                def out_share(b, c, with_last=True, tiles=range(J)):
                    c_yl.wait(pe, b * NC_ + c + 1)
                    for j in tiles:
                        if c == 0 and with_last:
                            c_po.wait(pe, (b - 1) * J + j + 1)
                        r = slice(j * P, (j + 1) * P)
                        last = three(po[j][:, :], y_h[c % 3][:, r], y_l[c % 3][:, r],
                                     w.wout_h[:, c, :], w.wout_l[:, c, :], c == 0, c == NC_ - 1)
                    if J - 1 in tiles:
                        last.then_inc(c_o.sem, 1)

                def transposes(k):
                    for j in range(J):
                        last = pe.transpose(ring[k % 2][:, j * P:(j + 1) * P], rows[:, j, k * P:(k + 1) * P],
                                            ident[:, :])
                    last.then_inc(c_t.sem, 1)

                def next_turn(b, k):
                    if k == 0:
                        c_rows.wait(pe, 16 * (b + 2))
                    if k < 2:
                        c_ev.wait(pe, b * NW + NW - 1 + k)
                    else:
                        c_th.wait(pe, (b + 1) * KD + k - 1)
                        c_tl.wait(pe, (b + 1) * KD + k - 1)
                    transposes(k)

                def turn(b, with_last):
                    for s in range(NW):
                        ag(b, s)
                        if s in b_after:
                            share_b(b, b_after[s])
                    front, back = range(J // 2), range(J // 2, J)
                    next_turn(b, 0)
                    if with_last:
                        out_share(b - 1, NC_ - 2, tiles=front)
                    next_turn(b, 1)
                    share_b(b, NC_ - 1)
                    if with_last:
                        out_share(b - 1, NC_ - 2, tiles=back)
                        out_share(b - 1, NC_ - 1, tiles=front)
                    chan(b, 0)
                    next_turn(b, 2)
                    next_turn(b, 3)
                    chan(b, 1)
                    if with_last:
                        out_share(b - 1, NC_ - 1, tiles=back)
                    for c in range(2, NC_):
                        chan(b, c)
                        out_share(b, c - 2, with_last)

                c_rows.wait(pe, 16)
                for k in range(KD):
                    if k >= 2:
                        c_th.wait(pe, k - 1)
                        c_tl.wait(pe, k - 1)
                    transposes(k)
                turn(0, False)
                with pe.Fori(1, NB) as b:
                    turn(b, True)
                for c in range(NC_ - LATE, NC_):
                    out_share(NB - 1, c)


class ExpertWeights:

    def __init__(self, m, t):
        self.m, self.t = m, t
        self.w1 = m.sb("w1r", [P, FT, D])
        self.w2 = m.sb("w2r", [P, FT, D])
        self.b1 = m.sb("b1", [P, (E + 1) * FT])
        self.b2 = m.sb("b2", [P, E, D])
        self.gamma = m.sb("f_ln_g", [P, D])
        self.beta = m.sb("f_ln_b", [P, D])
        self.idx = m.sb("idx", [P, (2 * E + 1) * J], U32)
        self.c_w = [m.count(f"f_w{i}") for i in range(FT)]
        self.c_small = m.count("f_small")
        self.c_idx = m.count("f_idx")
        self.c_ga = [m.pool_count(f"f_ga{j}") for j in range(J)]
        self.c_sc = [m.pool_count(f"f_sc{j}") for j in range(J)]
        self.c_pad = m.count("f_pad")
        self.first = m.sb("f_first", [P, 2 * J, FT])

    def load(self, sp, e, i):
        sp.dma_start(self.w1[:, i, :], self.t["fc1"][e, i]).then_inc(self.c_w[i].sem, 16)
        sp.dma_start(self.w2[:, i, :], self.t["fc2"][e, i]).then_inc(self.c_w[i].sem, 16)

    def prime(self, pool):
        for n, c in enumerate(self.c_ga + self.c_sc):
            c.prime(pool, self.first[:, n, :], self.t["b1"][:, 0:FT])
        pool.memset(self.idx[:, 2 * E * J:(2 * E + 1) * J], 0).then_inc(self.c_pad.sem, 1)
        pool.memset(self.b1[:, E * FT:(E + 1) * FT], 0.0).then_inc(self.c_pad.sem, 1)

    def load_first(self, sp):
        for i in range(2):
            self.load(sp, 0, i)
        for dst, src in ((self.gamma[:, :], self.t["f_ln_g"].to_broadcast([P, D])),
                         (self.beta[:, :], self.t["f_ln_b"].to_broadcast([P, D])),
                         (self.b1[:, 0:E * FT], self.t["b1"]),
                         (self.b2[:, :, :].rearrange("p e d -> p (e d)"), self.t["b2"].to_broadcast([P, E * D]))):
            sp.dma_start(dst, src).then_inc(self.c_small.sem, 16)
        for i in range(2, FT):
            self.load(sp, 0, i)


def stage_lists(nc, gates, thr, slots_d, ends, ew):
    EN = E * NT
    NONE = 4096.0
    EG = P // HI
    NQ = 4
    TQ = NT // NQ
    with ExitStack() as stack:
        m = Mem(nc, stack)
        gt = m.sb("l_gt", [P, EN], BF16)
        eq = m.sb("l_eq", [P, EN], BF16)
        before = m.sb("l_before", [P, P], BF16)
        ones = m.sb("l_ones", [P, P], BF16)
        one = m.sb("l_one", [P, 1])
        run_gt = m.sb("l_run_gt", [P, EN])
        run_eq = m.sb("l_run_eq", [P, EN])
        slot = m.sb("l_slot", [P, EN])
        slot_i = m.sb("l_slot_i", [P, EN], U32)
        hi_i = m.sb("l_hi_i", [P, EN], U32)
        lo_i = m.sb("l_lo_i", [P, EN], U32)
        hi = m.sb("l_hi", [P, E, NT], BF16)
        lo = m.sb("l_lo", [P, E, NT], BF16)
        digit = m.sb("l_digit", [P, LO], BF16)
        tile_no = m.sb("l_tile", [P, NT])
        row_no = m.sb("l_row", [P, 1])
        hi1 = [m.sb(f"l_hi1_{i}", [P, TQ, E, HI], BF16) for i in range(2)]
        lo1 = [m.sb(f"l_lo1_{i}", [P, TQ, E, LO], BF16) for i in range(2)]
        lov = [m.sb(f"l_lov_{i}", [P, TQ, E, 2, LO], BF16) for i in range(2)]
        both = m.sb("l_both", [P, E // EG, EG * 2 * LO])
        token_f = m.sb("l_token_f", [P, E // EG, LO])
        token = m.sb("l_token", [P, E // EG, LO], U32)
        p_before = [m.ps(f"l_pb{i}", [P, EN]) for i in range(2)]
        p_all = [m.ps(f"l_pa{i}", [P, EN]) for i in range(2)]
        p_tok = [p[:, 0:EG * 2 * LO] for p in p_before]
        c_set = m.count("l_set")
        c_v = m.count("l_v")
        c_pre = m.count("l_pre")
        c_lo1 = m.count("l_lo1c")
        c_hi1 = m.count("l_hi1c")
        c_row = m.count("l_rowc")
        c_til = m.count("l_tilc")
        c_q = m.count("l_q")
        c_list = m.count("l_list")
        c_out = m.count("l_out")

        def by_expert(ap):
            return ap.rearrange("p (e r) -> p e r", e=E)

        m.counts += ew.m.counts
        m.start()
        with nc.Block() as block:
            @block.sync
            def _(sp):
                ew.load_first(sp)
                ends.store_and_load(sp, NB - 2)
                ends.load_xn(sp, NB - 1, 2)
                ends.load_xn(sp, NB - 1, 3)
                c_list.wait(sp, 1)
                sp.dma_start(slots_d.rearrange("(g q) l -> q g l", q=P), token[:, :, :]).then_inc(c_out.sem, 16)
                c_out.wait(sp, 16)
                sp.dma_start(ew.idx[:, 0:2 * E * J].rearrange("p (e c) -> p e c", e=E),
                             slots_d.rearrange("(e h) l -> e (h l)", e=E)
                             .rearrange("e (p c) -> p e c", p=P)).then_inc(ew.c_idx.sem, 16)
                for j in range(J):
                    ends.store(sp, NB - 1, j)
                for j in range(J):
                    ends.c_st[j].wait(sp, 16 * NB)

            @block.gpsimd
            def _(pool):
                pool.memset(ones[:, :], 1.0).then_inc(c_set.sem, 1)
                pool.memset(one[:, :], 1.0).then_inc(c_set.sem, 1)
                c_set.wait(pool, 1)
                pool.affine_select(out=before[:, :], in_=ones[:, :], compare_op=ALU.is_ge, fill=0.0,
                                   base=-1, pattern=[[1, P]], channel_multiplier=-1).then_inc(c_set.sem, 1)
                pool.iota(digit[:, :], [[1, LO]], base=0, channel_multiplier=0,
                          allow_small_or_imprecise_dtypes=True).then_inc(c_set.sem, 1)
                pool.iota(tile_no[:, :], [[1, NT]], base=0, channel_multiplier=0,
                          allow_small_or_imprecise_dtypes=True).then_inc(c_set.sem, 1)
                pool.iota(row_no[:, :], [[0, 1]], base=0, channel_multiplier=1,
                          allow_small_or_imprecise_dtypes=True).then_inc(c_set.sem, 1)
                ew.prime(pool)
                for j in range(J):
                    ends.inverse_std(pool, NB - 2, j)
                for j in (0, 2):
                    ends.add_pair(pool, NB - 1, j)
                for j in range(J):
                    ends.inverse_std(pool, NB - 1, j)

            @block.vector
            def _(dve):
                steps = 0

                def done(ins):
                    nonlocal steps
                    ins.then_inc(c_v.sem, 1)
                    steps += 1

                def chained(ins):
                    done(ins)
                    c_v.wait(dve, steps)

                def finish(b):
                    for j in range(J):
                        ends.scale(dve, b, j)
                        ends.finish(dve, b, j)

                thr_b = thr[:, :].rearrange("p (e o) -> p e o", o=1).to_broadcast([P, E, NT])
                c_set.wait(dve, 6)
                done(dve.tensor_tensor(by_expert(gt[:, :]), gates[:, :, :], thr_b, ALU.is_gt))
                done(dve.tensor_tensor(by_expert(eq[:, :]), gates[:, :, :], thr_b, ALU.is_equal))
                for i, run in enumerate((run_gt, run_eq)):
                    c_pre.wait(dve, 2 * i + 2)
                    for e in range(E):
                        w = slice(e * NT, (e + 1) * NT)
                        done(dve.tensor_tensor_scan(run[:, w], one[:, 0:1].to_broadcast([P, NT]), p_all[i][:, w],
                                                    0.0, ALU.mult, ALU.add))
                c_v.wait(dve, steps)
                total_gt = by_expert(run_gt[:, :])[:, :, NT - 1:NT].to_broadcast([P, E, NT])
                chained(dve.tensor_tensor(by_expert(run_eq[:, :]), by_expert(run_eq[:, :]), total_gt, ALU.add))
                for i, run in enumerate((run_gt, run_eq)):
                    done(dve.tensor_tensor(run[:, :], run[:, :], p_all[i][:, :], ALU.subtract))
                c_v.wait(dve, steps)
                for i, run in enumerate((run_gt, run_eq)):
                    done(dve.tensor_tensor(run[:, :], run[:, :], p_before[i][:, :], ALU.add))
                c_v.wait(dve, steps)
                for run, mask in ((run_gt, gt), (run_eq, eq)):
                    done(dve.scalar_tensor_tensor(out=run[:, :], in0=run[:, :], scalar=NONE, in1=mask[:, :],
                                                  op0=ALU.subtract, op1=ALU.mult))
                c_v.wait(dve, steps)
                chained(dve.scalar_tensor_tensor(out=slot[:, :], in0=run_gt[:, :], scalar=NONE, in1=run_eq[:, :],
                                                 op0=ALU.add, op1=ALU.add))
                chained(dve.tensor_copy(slot_i[:, :], slot[:, :]))
                done(dve.tensor_scalar(hi_i[:, :], slot_i[:, :], 5, None, ALU.logical_shift_right))
                chained(dve.tensor_scalar(lo_i[:, :], slot_i[:, :], LO - 1, None, ALU.bitwise_and))
                done(dve.tensor_copy(hi[:, :, :], by_expert(hi_i[:, :])))
                chained(dve.tensor_copy(lo[:, :, :], by_expert(lo_i[:, :])))
                digits = digit[:, :].rearrange("p (a b l) -> p a b l", a=1, b=1).to_broadcast([P, TQ, E, LO])
                for q in range(NQ):
                    def spread(x):
                        tiles = x[:, :, q * TQ:(q + 1) * TQ]
                        return tiles.rearrange("p e (t o) -> p t e o", o=1).to_broadcast([P, TQ, E, LO])

                    c_row.wait(dve, max(q - 1, 0))
                    c_til.wait(dve, max(q - 1, 0) * TQ)
                    c_q.wait(dve, max(q - 1, 0))
                    dve.tensor_tensor(lo1[q % 2][:, :, :, :], spread(lo), digits, ALU.is_equal).then_inc(c_lo1.sem, 1)
                    if q == 1:
                        finish(NB - 2)
                    dve.tensor_tensor(hi1[q % 2][:, :, :, :], spread(hi), digits, ALU.is_equal).then_inc(c_hi1.sem, 1)
                for j in range(J):
                    ends.statistics(dve, NB - 1, j)
                finish(NB - 1)
                c_q.wait(dve, NQ)
                for g in range(E // EG):
                    done(dve.tensor_copy(both[:, g, :], p_tok[g]))
                c_v.wait(dve, steps)
                for x in range(EG):
                    q, w = slice(x * HI, (x + 1) * HI), x * 2 * LO
                    done(dve.scalar_tensor_tensor(out=token_f[q, :, :], in0=both[q, :, w + LO:w + 2 * LO],
                                                  scalar=float(P), in1=both[q, :, w:w + LO],
                                                  op0=ALU.mult, op1=ALU.add))
                c_v.wait(dve, steps)
                dve.tensor_copy(token[:, :, :], token_f[:, :, :]).then_inc(c_list.sem, 1)

            @block.scalar
            def _(act):
                for q in range(NQ):
                    c_lo1.wait(act, q + 1)
                    c_q.wait(act, max(q - 1, 0))
                    act.activation(lov[q % 2][:, :, :, 0, :], lo1[q % 2][:, :, :, :], ACT.Copy,
                                   scale=row_no[:, 0:1]).then_inc(c_row.sem, 1)
                    with act.Fori(0, TQ) as r:
                        tile = bass.ds(r, 1)
                        act.activation(lov[q % 2][:, tile, :, 1, :], lo1[q % 2][:, tile, :, :], ACT.Copy,
                                       scale=tile_no[:, bass.ds(r + q * TQ, 1)]).then_inc(c_til.sem, 1)
                    if q == 1:
                        for j in range(J):
                            ends.rows_out(act, NB - 1, j)

            @block.tensor
            def _(pe):
                c_set.wait(pe, 3)
                for i, mask in enumerate((gt, eq)):
                    c_v.wait(pe, i + 1)
                    pe.matmul(p_before[i][:, :], before[:, :], mask[:, :], start=True, stop=True).then_inc(c_pre.sem, 1)
                    pe.matmul(p_all[i][:, :], ones[:, :], mask[:, :], start=True, stop=True).then_inc(c_pre.sem, 1)
                for q in range(NQ):
                    c_hi1.wait(pe, q + 1)
                    c_row.wait(pe, q + 1)
                    for r in range(TQ):
                        c_til.wait(pe, q * TQ + r + 1)
                        for g in range(E // EG):
                            ex = slice(g * EG, (g + 1) * EG)
                            last = pe.matmul(p_tok[g], hi1[q % 2][:, r, ex, :].rearrange("p e l -> p (e l)"),
                                             lov[q % 2][:, r, ex, :, :].rearrange("p e v l -> p (e v l)"),
                                             start=(q + r == 0), stop=(q == NQ - 1 and r == TQ - 1))
                    last.then_inc(c_q.sem, 1)


def stage_experts(nc, t, ident, ends, ew):
    G = 2 * E
    T_AT = (9, 11, 13, 14)
    with ExitStack() as stack:
        m = Mem(nc, stack)
        w1h = [m.sb(f"w1h{i}", [P, D], F32R) for i in range(4)]
        w1l = [m.sb(f"w1l{i}", [P, D], F32R) for i in range(4)]
        w2h = [m.sb(f"w2h{i}", [P, D], F32R) for i in range(4)]
        w2l = [m.sb(f"w2l{i}", [P, D], F32R) for i in range(4)]
        yt_h = [m.sb(f"yt_h{i}", [P, KD, TB], F32R) for i in range(2)]
        yt_l = [m.sb(f"yt_l{i}", [P, KD, TB], F32R) for i in range(2)]
        rows = m.sb("rows", [P, J, XW])
        kept = [m.sb(f"kept{i}", [P, J, E]) for i in range(2)]
        hid = [m.sb(f"hid{i}", [P, TB]) for i in range(2)]
        hid_h = [m.sb(f"hid_h{i}", [P, TB], F32R) for i in range(4)]
        hid_l = [m.sb(f"hid_l{i}", [P, TB], F32R) for i in range(4)]
        b1c = [m.sb(f"b1c{i}", [P, FT]) for i in range(2)]
        idx_c = [m.sb(f"idx_c{i}", [P, J], U32) for i in range(2)]
        stats = m.sb("f_stats", [P, J, 6])
        mv = m.sb("f_mv", [P, J, 2])
        std = m.sb("f_std", [P, J])
        rstd = m.sb("f_rstd", [P, J])
        ph = [m.ps(f"ph{i}", [P, TB]) for i in range(2)]
        pt = [m.ps(f"f_pt{i}", [P, TB]) for i in range(2)]

        w1r, w2r, b1, b2, gamma, beta, idx = ew.w1, ew.w2, ew.b1, ew.b2, ew.gamma, ew.beta, ew.idx
        c_w, c_small, c_ga, c_sc, c_pad = ew.c_w, ew.c_small, ew.c_ga, ew.c_sc, ew.c_pad
        res, po = ends.res, ends.po
        c_ix = m.count("f_ix")
        c_kp = m.count("f_kp")
        c_b1 = m.count("f_b1")
        c_bn = m.count("f_bn")
        c_mv = m.count("f_mv")
        c_eps = m.count("f_eps")
        c_rs = m.count("f_rs")
        c_nm = m.count("f_nm")
        c_g = m.count("f_g")
        c_t = m.count("f_t")
        c_th = m.count("f_th")
        c_tl = m.count("f_tl")
        c_wh = m.count("f_wh")
        c_wl = m.count("f_wl")
        c_p1 = m.count("f_p1")
        c_p2 = m.count("f_p2")
        c_ge = m.count("f_ge")
        c_hh = m.count("f_hh")
        c_hl = m.count("f_hl")
        c_bw = m.count("f_bw")
        c_rw = m.count("f_rw")
        p_tick = m.tick("f_ptick")
        d_tick = m.tick("f_dtick")

        m.start()
        with nc.Block() as block:
            @block.sync
            def _(sp):
                with sp.Fori(0, E - 1) as e:
                    for i in range(FT):
                        c_wl.wait(sp, 2 * ((2 * e + 1) * FT + i + 1))
                        ew.load(sp, e + 1, i)
                for i in range(2):
                    c_wl.wait(sp, 2 * ((G - 1) * FT + i + 1))
                    ew.load(sp, 0, i)

            @block.gpsimd
            def _(pool):
                def hold():
                    pool.sem_inc(p_tick, 1)

                c_pad.wait(pool, 2)
                ew.c_idx.wait(pool, 16)

                def gather(g, i, first_turn=False):
                    if not first_turn:
                        for j in range(J):
                            c_sc[j].wait(pool, 16 * (g - 1))
                    hold()
                    pool.tensor_copy(idx_c[i][:, :], idx[:, bass.ds(g * J, J)]).then_inc(c_ix.sem, 1)
                    c_ix.wait(pool, g + 1)
                    c_t.wait(pool, g * KD)
                    c_kp.wait(pool, g)
                    hold()
                    for j in range(J):
                        pool.indirect_dma_start(
                            out=rows[:, j, :], out_offset=None, in_=t["xn"][:, :],
                            in_offset=bass.IndirectOffsetOnAxis(ap=idx_c[i][:, j:j + 1], axis=0),
                        ).then_inc(c_ga[j].sem, 16)

                def inverse_std(g):
                    for j in range(J):
                        n = g * J + j
                        c_mv.wait(pool, n + 1)
                        c_rs.wait(pool, n)
                        hold()
                        pool.tensor_scalar(std[:, j:j + 1], mv[:, j, 1:2], EPS, None, ALU.add).then_inc(c_eps.sem, 1)
                        c_eps.wait(pool, n + 1)
                        pool.tensor_tensor(rstd[:, j:j + 1], std[:, j:j + 1], ends.half[:, :], ALU.pow).then_inc(c_rs.sem, 1)

                def scatter(g, i):
                    for j in range(J):
                        c_sc[j].wait(pool, 16 * g)
                    for j in range(J):
                        c_rw.wait(pool, g * J + j + 1)
                        hold()
                        pool.indirect_dma_start(
                            out=t["out"][:, :], in_=res[j][:, :], in_offset=None, compute_op=ALU.add,
                            out_offset=bass.IndirectOffsetOnAxis(ap=idx_c[i][:, j:j + 1], axis=0),
                        ).then_inc(c_sc[j].sem, 16)

                gather(0, 0, True)
                inverse_std(0)
                with pool.Fori(0, E) as e:
                    for i in range(2):
                        g = 2 * e + i
                        gather(g + 1, 1 - i)
                        inverse_std(g + 1)
                        scatter(g, i)
                for j in range(J):
                    c_sc[j].wait(pool, 16 * G)

            @block.scalar
            def _(act):
                def w_high(n, s):
                    act.copy(w1h[s % 4][:, :], w1r[:, s % FT, :]).then_inc(c_wh.sem, 1)
                    act.copy(w2h[s % 4][:, :], w2r[:, s % FT, :]).then_inc(c_wh.sem, 1)

                def t_high(g, k, i):
                    c_t.wait(act, g * KD + k + 1)
                    act.copy(yt_h[i][:, k, :], pt[k % 2][:, :]).then_inc(c_th.sem, 1)

                for s in range(2):
                    c_w[s].wait(act, 32)
                    w_high(s, s)
                for k in range(KD):
                    t_high(0, k, 0)
                with act.Fori(0, E) as e:
                    for i in range(2):
                        g = 2 * e + i
                        for s in range(FT):
                            n = g * FT + s
                            c_p2.wait(act, g * FT if s < 2 else n - 1)
                            if i == 0 or s + 2 < FT:
                                c_w[(s + 2) % FT].wait(act, e * 32 + 32)
                            else:
                                c_w[(s + 2) % FT].wait(act, e * 32 + 64)
                            w_high(n + 2, s + 2)
                            c_hl.wait(act, g * FT if s < 2 else n - 1)
                            c_b1.wait(act, g + 1)
                            c_p1.wait(act, n + 1)
                            act.activation(hid[s % 2][:, :], ph[s % 2][:, :], ACT.Gelu_apprx_tanh,
                                           bias=b1c[i][:, s:s + 1]).then_inc(c_ge.sem, 1)
                            c_p2.wait(act, g * FT if s < 4 else n - 3)
                            c_ge.wait(act, n + 1)
                            act.copy(hid_h[s % 4][:, :], hid[s % 2][:, :]).then_inc(c_hh.sem, 1)
                            if s - 1 in T_AT:
                                t_high(g + 1, T_AT.index(s - 1), 1 - i)

            @block.vector
            def _(dve):
                def w_low(n, s):
                    for q, (r, h, l) in enumerate(((w1r, w1h, w1l), (w2r, w2h, w2l))):
                        c_wh.wait(dve, 2 * n + q + 1)
                        dve.tensor_tensor(l[s % 4][:, :], r[:, s % FT, :], f(h[s % 4][:, :]),
                                          ALU.subtract).then_inc(c_wl.sem, 1)

                def t_low(g, k, i):
                    c_th.wait(dve, g * KD + k + 1)
                    dve.tensor_tensor(yt_l[i][:, k, :], pt[k % 2][:, :], f(yt_h[i][:, k, :]),
                                      ALU.subtract).then_inc(c_tl.sem, 1)

                def statistics(g, j):
                    n = g * J + j
                    c_ga[j].wait(dve, 16 * (g + 1))
                    c_mv.wait(dve, n)
                    dve.bn_stats(stats[:, j, :], rows[:, j, 0:D]).then_inc(c_bn.sem, 1)
                    c_bn.wait(dve, n + 1)
                    c_nm.wait(dve, g * J)
                    dve.sem_inc(d_tick, 1)
                    dve.bn_aggr(mv[:, j, :], stats[:, j, :]).then_inc(c_mv.sem, 1)

                def normalise(g, j):
                    n = g * J + j
                    c_rs.wait(dve, n + 1)
                    c_mv.wait(dve, n + 1)
                    c_g.wait(dve, n)
                    dve.scalar_tensor_tensor(out=rows[:, j, 0:D], in0=rows[:, j, 0:D], scalar=mv[:, j, 0:1],
                                             in1=gamma[:, :], op0=ALU.subtract, op1=ALU.mult).then_inc(c_g.sem, 1)
                    c_g.wait(dve, n + 1)
                    dve.scalar_tensor_tensor(out=rows[:, j, 0:D], in0=rows[:, j, 0:D], scalar=rstd[:, j:j + 1],
                                             in1=beta[:, :], op0=ALU.mult, op1=ALU.add).then_inc(c_nm.sem, 1)

                def keep(g, e, i, first_turn=False):
                    c_rw.wait(dve, 0 if first_turn else (g - 1) * J)
                    dve.tensor_copy(kept[i][:, :, :], rows[:, :, D:XW]).then_inc(c_kp.sem, 1)
                    c_ge.wait(dve, 0 if first_turn else (g - 1) * FT)
                    dve.sem_inc(d_tick, 1)
                    dve.tensor_copy(b1c[i][:, :], b1[:, bass.ds(e * FT, FT)]).then_inc(c_b1.sem, 1)

                c_small.wait(dve, 16 * 4)
                c_pad.wait(dve, 2)
                for s in range(2):
                    w_low(s, s)
                statistics(0, 0)
                for j in range(1, J):
                    statistics(0, j)
                    normalise(0, j - 1)
                normalise(0, J - 1)
                keep(0, 0, 0, True)
                for k in range(KD):
                    t_low(0, k, 0)
                with dve.Fori(0, E) as e:
                    for i in range(2):
                        g = 2 * e + i
                        for s in range(FT):
                            n = g * FT + s
                            w_low(n + 2, s + 2)
                            if 3 <= s < 3 + J:
                                statistics(g + 1, s - 3)
                            c_hh.wait(dve, n + 1)
                            dve.tensor_tensor(hid_l[s % 4][:, :], hid[s % 2][:, :], f(hid_h[s % 4][:, :]),
                                              ALU.subtract).then_inc(c_hl.sem, 1)
                            if 3 <= s < 3 + J:
                                normalise(g + 1, s - 3)
                            if s == J + 3:
                                keep(g + 1, e + i, 1 - i)
                            if 8 <= s < 8 + J:
                                j = s - 8
                                c_sc[j].wait(dve, 16 * g)
                                c_kp.wait(dve, g + 1)
                                dve.tensor_scalar(res[j][:, :], b2[:, bass.ds(e, 1), :].rearrange("p o d -> p (o d)"),
                                                  kept[i][:, j, bass.ds(e, 1)], None, ALU.mult).then_inc(c_bw.sem, 1)
                            if s - 1 in T_AT:
                                t_low(g + 1, T_AT.index(s - 1), 1 - i)
                        c_p2.wait(dve, (g + 1) * FT)
                        c_bw.wait(dve, (g + 1) * J)
                        for j in range(J):
                            dve.scalar_tensor_tensor(out=res[j][:, :], in0=po[j][:, :],
                                                     scalar=kept[i][:, j, bass.ds(e, 1)], in1=res[j][:, :],
                                                     op0=ALU.mult, op1=ALU.add).then_inc(c_rw.sem, 1)

            @block.tensor
            def _(pe):
                def three(dst, ah, al, bh, bl, start, stop):
                    pe.matmul(dst, ah, bh, start=start, stop=False)
                    pe.matmul(dst, ah, bl, start=False, stop=False)
                    return pe.matmul(dst, al, bh, start=False, stop=stop)

                def trn(g, k):
                    if k == 0:
                        c_nm.wait(pe, J * (g + 1))
                    c_tl.wait(pe, g * KD + (k - 1 if k >= 2 else 0))
                    for j in range(J):
                        last = pe.transpose(pt[k % 2][:, j * P:(j + 1) * P], rows[:, j, k * P:(k + 1) * P],
                                            ident[:, :])
                    last.then_inc(c_t.sem, 1)

                def hidden(g, s, i):
                    n = g * FT + s
                    c_wl.wait(pe, 2 * n + 2)
                    if s == 0:
                        c_tl.wait(pe, (g + 1) * KD)
                    c_ge.wait(pe, g * FT if s < 2 else n - 1)
                    for k in range(KD):
                        w = slice(k * P, (k + 1) * P)
                        last = three(ph[s % 2][:, :], w1h[s % 4][:, w], w1l[s % 4][:, w],
                                     yt_h[i][:, k, :], yt_l[i][:, k, :], k == 0, k == KD - 1)
                    last.then_inc(c_p1.sem, 1)

                def out_share(g, s):
                    c_hl.wait(pe, g * FT + s + 1)
                    if s == 0:
                        c_rw.wait(pe, g * J)
                    for j in range(J):
                        w = slice(j * P, (j + 1) * P)
                        last = three(po[j][:, :], hid_h[s % 4][:, w], hid_l[s % 4][:, w],
                                     w2h[s % 4][:, :], w2l[s % 4][:, :], s == 0, s == FT - 1)
                    last.then_inc(c_p2.sem, 1)

                for k in range(KD):
                    trn(0, k)
                with pe.Fori(0, E) as e:
                    for i in range(2):
                        g = 2 * e + i
                        hidden(g, 0, i)
                        for s in range(1, FT + 1):
                            if s < FT:
                                hidden(g, s, i)
                            out_share(g, s - 1)
                            if s - 1 in T_AT:
                                trn(g + 1, T_AT.index(s - 1))


def build(nc, t):
    t["xn"] = nc.dram_tensor("xn_rows", (N, XW), F32, kind="Internal").ap()
    slots_d = nc.dram_tensor("slots", (E * HI, LO), U32, kind="Internal").ap()
    with ExitStack() as stack:
        m = Mem(nc, stack)
        gates = m.sb("gates", [P, E, NT])
        thr = m.sb("threshold", [P, E])
        ident = m.sb("ident", [P, P])
        ends = RowEnds(m, t)
        m.start()
        with ExitStack() as mixer:
            w = MixerWeights(Mem(nc, mixer))
            stage_gate(nc, t, gates, ident, w, ends)
            ends.banks()
            stage_mixer(nc, t, gates, thr, ident, w, ends)
        ew = ExpertWeights(Mem(nc, stack), t)
        stage_lists(nc, gates, thr, slots_d, ends, ew)
        stage_experts(nc, t, ident, ends, ew)


SHAPES = {
    "x": (N, D), "gate_w": (P, KD, E), "w_in": (P, NW, KD * P), "conv_w": (P, NC_, 4), "conv_b": (P, NC_),
    "d_param": (P, NC_), "ln_g": (1, D), "ln_b": (1, D), "w_out": (P, NC_, D), "w_c": (S, 2, D), "w_b": (P, NC_ * S),
    "fc1": (E, FT, P, D), "fc2": (E, FT, P, D), "b1": (P, E * FT), "b2": (1, E * D), "f_ln_g": (1, D), "f_ln_b": (1, D),
}


def kernel(**i):
    import numpy as np
    import concourse.bacc as bacc
    from concourse.bass_utils import run_bass_kernel_spmd as run

    a = {k.replace("L0_", ""): np.asarray(v) for k, v in i.items()}

    def by_channel(v):
        return v.reshape(NC_, P, -1).transpose(1, 0, 2)

    arrays = {
        "x": a["attn_x"].reshape(N, D),
        "gate_w": a["ffn_gate_w"].reshape(E, KD, P).transpose(2, 1, 0),
        "w_in": a["attn_W_in"].reshape(NW, P, KD, P).transpose(3, 0, 2, 1).reshape(P, NW, KD * P),
        "conv_w": by_channel(a["attn_conv_w"]),
        "conv_b": by_channel(a["attn_conv_b"]).reshape(P, NC_),
        "d_param": by_channel(a["attn_D_param"]).reshape(P, NC_),
        "ln_g": a["attn_ln_gamma"].reshape(1, D),
        "ln_b": a["attn_ln_beta"].reshape(1, D),
        "w_out": by_channel(a["attn_W_out"].T),
        "w_c": a["attn_W_C"].T.reshape(S, 2, D),
        "w_b": by_channel(a["attn_W_B"].T).reshape(P, NC_ * S),
        "fc1": a["ffn_fc1s"].reshape(E, FT, P, KD, P).transpose(0, 1, 4, 3, 2).reshape(E, FT, P, D),
        "fc2": a["ffn_fc2s"].transpose(0, 2, 1).reshape(E, FT, P, D),
        "b1": a["ffn_b1s"].reshape(E, FT, P).transpose(2, 0, 1).reshape(P, E * FT),
        "b2": a["ffn_b2s"].reshape(1, E * D),
        "f_ln_g": a["ffn_ln_gamma"].reshape(1, D),
        "f_ln_b": a["ffn_ln_beta"].reshape(1, D),
    }
    arrays = {f"{k}_in": np.ascontiguousarray(v) for k, v in arrays.items()}
    nc = bacc.Bacc("TRN2", target_bir_lowering=False, num_devices=1)
    t = {k: nc.dram_tensor(f"{k}_in", s, F32, kind="ExternalInput").ap() for k, s in SHAPES.items()}
    t["out"] = nc.dram_tensor("out_dram", (N, D), F32, kind="ExternalOutput").ap()
    build(nc, t)
    r = run(nc, [arrays], core_ids=[0])
    return r.results[0]["out_dram"].reshape(a["attn_x"].shape)
```
